# Optimizing a Trainium2 kernel written in Bass

```python
import numpy as np
import jax
import jax.numpy as jnp

def _softmax(x, axis=-1):
    return jax.nn.softmax(x, axis=axis)

def _gelu(x):
    return jax.nn.gelu(x, approximate=True)

def _silu(x):
    return jax.nn.silu(x)

def _sigmoid(x):
    return jax.nn.sigmoid(x)

def _layernorm(x, axis=-1, eps=1e-05):
    m = jnp.mean(x, axis=axis, keepdims=True)
    v = jnp.var(x, axis=axis, keepdims=True)
    return (x - m) / jnp.sqrt(v + eps)

def _scatter_add(tgt, idx, src, axis=0):
    return tgt.at[idx].add(src)

def _segment_sum(src, seg, n):
    return jax.ops.segment_sum(src, seg, n)
kernel_name = 'mk_hybrid_d2_jaxref_r8_cdaee9'

def setup_inputs(seed: int=0):
    np.random.seed(seed)
    _w = jnp.asarray

    def _L0_attn_a_setup():
        import jax, jax.numpy as jnp
        import numpy as np
        NUM_HEADS = 16
        HIDDEN = 128
        HEAD_DIM = HIDDEN // NUM_HEADS
        B, L = (1, 256)
        key = jax.random.key(seed)
        ks = jax.random.split(key, 5)
        scale = 1.0 / np.sqrt(HIDDEN)
        x = jax.random.normal(ks[0], (B, L, HIDDEN), dtype=jnp.float32)
        Wq = jax.random.normal(ks[1], (HIDDEN, HIDDEN), dtype=jnp.float32) * scale
        Wk = jax.random.normal(ks[2], (HIDDEN, HIDDEN), dtype=jnp.float32) * scale
        Wv = jax.random.normal(ks[3], (HIDDEN, HIDDEN), dtype=jnp.float32) * scale
        Wo = jax.random.normal(ks[4], (HIDDEN, HIDDEN), dtype=jnp.float32) * scale
        return {'x': x, 'Wq': Wq, 'Wk': Wk, 'Wv': Wv, 'Wo': Wo}
    _L0_attn_a_in = _L0_attn_a_setup()

    def _L0_attn_b_setup():
        import jax, jax.numpy as jnp
        import numpy as np
        HEADS = 16
        DIM_HEAD = 64
        key = jax.random.key(seed)
        k1, k2, k3 = jax.random.split(key, 3)
        dim = 128
        x = jax.random.normal(k1, (2, 256, dim), dtype=jnp.float32)
        w_qkv = jax.random.normal(k2, (dim, 3 * HEADS * DIM_HEAD), dtype=jnp.float32) * dim ** (-0.5)
        w_out = jax.random.normal(k3, (HEADS * DIM_HEAD, dim), dtype=jnp.float32) * (HEADS * DIM_HEAD) ** (-0.5)
        return {'x': x, 'w_qkv': w_qkv, 'w_out': w_out}
    _L0_attn_b_in = _L0_attn_b_setup()

    def _L0_ffn_setup():
        import jax, jax.numpy as jnp
        import numpy as np
        E = 8
        TOP_K = 2
        ROUTE_SCALE = 1.0
        ALPHA = 1.702
        LIMIT = 7.0
        D = 128
        F = 128
        B, S = (2, 128)

        def swiglu(h):
            g = jnp.minimum(h[..., ::2], LIMIT)
            l = jnp.clip(h[..., 1::2], -LIMIT, LIMIT)
            return g * jax.nn.sigmoid(ALPHA * g) * (l + 1.0)
        if __name__ == '__main__':
            out = reference(**setup_inputs())
            print(out.shape, out.dtype)
        key = jax.random.key(seed)
        ks = jax.random.split(key, 16)
        sd = 1.0 / np.sqrt(D)
        sf = 1.0 / np.sqrt(F)
        return {'x': jax.random.normal(ks[0], (B, S, D), jnp.float32), 'gate_w': jax.random.normal(ks[1], (E, D), jnp.float32) * sd, 'gate_b': jax.random.normal(ks[2], (E,), jnp.float32) * 0.01, 'w1': jax.random.normal(ks[3], (E, 2 * F, D), jnp.float32) * sd, 'b1': jax.random.normal(ks[4], (E, 2 * F), jnp.float32) * 0.01, 'w3': jax.random.normal(ks[5], (E, 2 * F, D), jnp.float32) * sd, 'b3': jax.random.normal(ks[6], (E, 2 * F), jnp.float32) * 0.01, 'w2': jax.random.normal(ks[7], (E, D, F), jnp.float32) * sf, 'b2': jax.random.normal(ks[8], (E, D), jnp.float32) * 0.01, 'sw1': jax.random.normal(ks[9], (2 * F, D), jnp.float32) * sd, 'sb1': jax.random.normal(ks[10], (2 * F,), jnp.float32) * 0.01, 'sw3': jax.random.normal(ks[11], (2 * F, D), jnp.float32) * sd, 'sb3': jax.random.normal(ks[12], (2 * F,), jnp.float32) * 0.01, 'sw2': jax.random.normal(ks[13], (D, F), jnp.float32) * sf, 'sb2': jax.random.normal(ks[14], (D,), jnp.float32) * 0.01}
    _L0_ffn_in = _L0_ffn_setup()

    def _L1_attn_a_setup():
        import jax, jax.numpy as jnp
        import numpy as np
        NUM_HEADS = 16
        D_MODEL = 128
        D_K = D_MODEL // NUM_HEADS
        MAX_SEQ_LEN = 512
        ROPE_BASE = 10000.0
        BATCH = 2
        SEQ_LEN = 256

        def _rope_tables(seq_len, d_k, base=ROPE_BASE):
            theta = 1.0 / base ** (jnp.arange(0, d_k, 2, dtype=jnp.float32) / d_k)
            m = jnp.arange(seq_len, dtype=jnp.float32)
            m_theta = jnp.outer(m, theta)
            ang = jnp.concatenate([m_theta, m_theta], axis=-1)
            return (jnp.cos(ang), jnp.sin(ang))

        def _apply_rope(x, cos, sin):
            d2 = x.shape[-1] // 2
            x1, x2 = (x[..., :d2], x[..., d2:])
            x_flip = jnp.concatenate([-x2, x1], axis=-1)
            return x * cos + x_flip * sin
        key = jax.random.key(seed)
        kx, kq, kk, kv, ko = jax.random.split(key, 5)
        s = 1.0 / np.sqrt(D_MODEL)
        x = jax.random.normal(kx, (BATCH, SEQ_LEN, D_MODEL), dtype=jnp.float32)
        W_Q = jax.random.uniform(kq, (D_MODEL, D_MODEL), jnp.float32, -s, s)
        W_K = jax.random.uniform(kk, (D_MODEL, D_MODEL), jnp.float32, -s, s)
        W_V = jax.random.uniform(kv, (D_MODEL, D_MODEL), jnp.float32, -s, s)
        W_O = jax.random.uniform(ko, (D_MODEL, D_MODEL), jnp.float32, -s, s)
        return {'x': x, 'W_Q': W_Q, 'W_K': W_K, 'W_V': W_V, 'W_O': W_O}
    _L1_attn_a_in = _L1_attn_a_setup()

    def _L1_attn_b_setup():
        import jax, jax.numpy as jnp
        import numpy as np
        B, L, R = (4, 256, 128)
        HID, EXP, K = (64, 2, 3)
        D = HID * EXP
        N = HID
        key = jax.random.key(seed)
        ks = jax.random.split(key, 16)
        g = lambda k, s: jax.random.normal(k, s, dtype=jnp.float32) * 0.02
        inp = {'up_x': jax.random.normal(ks[0], (B, L, R), dtype=jnp.float32), 'W_up': g(ks[1], (R, 2 * D)), 'b_up': g(ks[2], (2 * D,)), 'conv_w': g(ks[3], (D, K)), 'conv_b': g(ks[4], (D,)), 'W_delta': g(ks[5], (D, D)), 'b_delta': g(ks[6], (D,)), 'W_B': g(ks[7], (D, N)), 'b_B': g(ks[8], (N,)), 'W_C': g(ks[9], (D, N)), 'b_C': g(ks[10], (N,)), 'A_log': jnp.log(jnp.broadcast_to(jnp.arange(1, N + 1, dtype=jnp.float32), (D, N))), 'D_skip': jnp.ones((D,), dtype=jnp.float32), 'W_down': g(ks[11], (D, R)), 'b_down': g(ks[12], (R,))}
        return inp
    _L1_attn_b_in = _L1_attn_b_setup()

    def _L1_ffn_setup():
        import jax, jax.numpy as jnp
        import numpy as np
        E = 32
        K = 4
        H = 128
        I = 64
        B, S = (2, 256)
        T = B * S
        C = 128
        ROUTED_SCALE = 1.0

        def _silu_and_mul(gu):
            g, u = jnp.split(gu, 2, axis=-1)
            return jax.nn.silu(g) * u
        key = jax.random.key(seed)
        ks = jax.random.split(key, 6)
        s = 0.02
        return {'hidden_states': jax.random.normal(ks[0], (B, S, H), jnp.float32), 'gate_w': jax.random.normal(ks[1], (E, H), jnp.float32) * s, 'w_gate_up': jax.random.normal(ks[2], (E, H, 2 * I), jnp.float32) * s, 'w_down': jax.random.normal(ks[3], (E, I, H), jnp.float32) * s, 'shared_w_gate_up': jax.random.normal(ks[4], (H, 2 * I), jnp.float32) * s, 'shared_w_down': jax.random.normal(ks[5], (I, H), jnp.float32) * s}
    _L1_ffn_in = _L1_ffn_setup()
    _d = {'L0_attn_a_x': _L0_attn_a_in['x'], 'L0_attn_a_Wq': _L0_attn_a_in['Wq'], 'L0_attn_a_Wk': _L0_attn_a_in['Wk'], 'L0_attn_a_Wv': _L0_attn_a_in['Wv'], 'L0_attn_a_Wo': _L0_attn_a_in['Wo'], 'L0_attn_b_w_qkv': _L0_attn_b_in['w_qkv'], 'L0_attn_b_w_out': _L0_attn_b_in['w_out'], 'L0_ffn_gate_w': _L0_ffn_in['gate_w'], 'L0_ffn_gate_b': _L0_ffn_in['gate_b'], 'L0_ffn_w1': _L0_ffn_in['w1'], 'L0_ffn_b1': _L0_ffn_in['b1'], 'L0_ffn_w3': _L0_ffn_in['w3'], 'L0_ffn_b3': _L0_ffn_in['b3'], 'L0_ffn_w2': _L0_ffn_in['w2'], 'L0_ffn_b2': _L0_ffn_in['b2'], 'L0_ffn_sw1': _L0_ffn_in['sw1'], 'L0_ffn_sb1': _L0_ffn_in['sb1'], 'L0_ffn_sw3': _L0_ffn_in['sw3'], 'L0_ffn_sb3': _L0_ffn_in['sb3'], 'L0_ffn_sw2': _L0_ffn_in['sw2'], 'L0_ffn_sb2': _L0_ffn_in['sb2'], 'L1_attn_a_W_Q': _L1_attn_a_in['W_Q'], 'L1_attn_a_W_K': _L1_attn_a_in['W_K'], 'L1_attn_a_W_V': _L1_attn_a_in['W_V'], 'L1_attn_a_W_O': _L1_attn_a_in['W_O'], 'L1_attn_b_W_up': _L1_attn_b_in['W_up'], 'L1_attn_b_b_up': _L1_attn_b_in['b_up'], 'L1_attn_b_conv_w': _L1_attn_b_in['conv_w'], 'L1_attn_b_conv_b': _L1_attn_b_in['conv_b'], 'L1_attn_b_W_delta': _L1_attn_b_in['W_delta'], 'L1_attn_b_b_delta': _L1_attn_b_in['b_delta'], 'L1_attn_b_W_B': _L1_attn_b_in['W_B'], 'L1_attn_b_b_B': _L1_attn_b_in['b_B'], 'L1_attn_b_W_C': _L1_attn_b_in['W_C'], 'L1_attn_b_b_C': _L1_attn_b_in['b_C'], 'L1_attn_b_A_log': _L1_attn_b_in['A_log'], 'L1_attn_b_D_skip': _L1_attn_b_in['D_skip'], 'L1_attn_b_W_down': _L1_attn_b_in['W_down'], 'L1_attn_b_b_down': _L1_attn_b_in['b_down'], 'L1_ffn_gate_w': _L1_ffn_in['gate_w'], 'L1_ffn_w_gate_up': _L1_ffn_in['w_gate_up'], 'L1_ffn_w_down': _L1_ffn_in['w_down'], 'L1_ffn_shared_w_gate_up': _L1_ffn_in['shared_w_gate_up'], 'L1_ffn_shared_w_down': _L1_ffn_in['shared_w_down']}
    _x0 = _d['L0_attn_a_x']
    _d['L0_attn_a_x'] = jax.random.normal(jax.random.fold_in(jax.random.key(seed), 1), (8, 256, 128), dtype=_x0.dtype)
    del _x0
    return _d

def reference(L0_attn_a_x, L0_attn_a_Wq, L0_attn_a_Wk, L0_attn_a_Wv, L0_attn_a_Wo, L0_attn_b_w_qkv, L0_attn_b_w_out, L0_ffn_gate_w, L0_ffn_gate_b, L0_ffn_w1, L0_ffn_b1, L0_ffn_w3, L0_ffn_b3, L0_ffn_w2, L0_ffn_b2, L0_ffn_sw1, L0_ffn_sb1, L0_ffn_sw3, L0_ffn_sb3, L0_ffn_sw2, L0_ffn_sb2, L1_attn_a_W_Q, L1_attn_a_W_K, L1_attn_a_W_V, L1_attn_a_W_O, L1_attn_b_W_up, L1_attn_b_b_up, L1_attn_b_conv_w, L1_attn_b_conv_b, L1_attn_b_W_delta, L1_attn_b_b_delta, L1_attn_b_W_B, L1_attn_b_b_B, L1_attn_b_W_C, L1_attn_b_b_C, L1_attn_b_A_log, L1_attn_b_D_skip, L1_attn_b_W_down, L1_attn_b_b_down, L1_ffn_gate_w, L1_ffn_w_gate_up, L1_ffn_w_down, L1_ffn_shared_w_gate_up, L1_ffn_shared_w_down):

    def _L0_attn_a_ref(x, Wq, Wk, Wv, Wo):
        import jax, jax.numpy as jnp
        import numpy as np
        NUM_HEADS = 16
        HIDDEN = 128
        HEAD_DIM = HIDDEN // NUM_HEADS
        B, L = (1, 256)
        Bx, Lx, _ = x.shape
        q = (x @ Wq.T).reshape(Bx, Lx, NUM_HEADS, HEAD_DIM)
        k = (x @ Wk.T).reshape(Bx, Lx, NUM_HEADS, HEAD_DIM)
        v = (x @ Wv.T).reshape(Bx, Lx, NUM_HEADS, HEAD_DIM)
        q = jax.nn.elu(q) + 1.0
        k = jax.nn.elu(k) + 1.0
        kv = jnp.einsum('blhd,blhe->blhde', k, v)
        kv_cumsum = jnp.cumsum(kv, axis=1)
        k_cumsum = jnp.cumsum(k, axis=1)
        out = jnp.einsum('blhd,blhde->blhe', q, kv_cumsum)
        denom = jnp.clip(jnp.einsum('blhd,blhd->blh', q, k_cumsum), 1e-06, None)
        out = out / denom[..., None]
        return out.reshape(Bx, Lx, HIDDEN) @ Wo.T

    def _L0_attn_b_ref(x, w_qkv, w_out):
        import jax, jax.numpy as jnp
        import numpy as np
        HEADS = 16
        DIM_HEAD = 64
        b, n, _ = x.shape
        scale = DIM_HEAD ** (-0.5)
        qkv = x @ w_qkv
        qkv = qkv.reshape(b, n, 3, HEADS, DIM_HEAD)
        qkv = jnp.transpose(qkv, (2, 0, 3, 1, 4))
        q, k, v = (qkv[0], qkv[1], qkv[2])
        q = q * scale
        sim = jnp.einsum('bhid,bhjd->bhij', q, k)
        attn = jax.nn.softmax(sim, axis=-1)
        out = jnp.einsum('bhij,bhjd->bhid', attn, v)
        out = jnp.transpose(out, (0, 2, 1, 3)).reshape(b, n, HEADS * DIM_HEAD)
        return out @ w_out

    def _L0_ffn_ref(x, gate_w, gate_b, w1, b1, w3, b3, w2, b2, sw1, sb1, sw3, sb3, sw2, sb2):
        import jax, jax.numpy as jnp
        import numpy as np
        E = 8
        TOP_K = 2
        ROUTE_SCALE = 1.0
        ALPHA = 1.702
        LIMIT = 7.0
        D = 128
        F = 128
        B, S = (2, 128)

        def swiglu(h):
            g = jnp.minimum(h[..., ::2], LIMIT)
            l = jnp.clip(h[..., 1::2], -LIMIT, LIMIT)
            return g * jax.nn.sigmoid(ALPHA * g) * (l + 1.0)
        if __name__ == '__main__':
            out = reference(**setup_inputs())
            print(out.shape, out.dtype)
        inp_shape = x.shape
        xt = x.reshape(-1, D)
        logits = xt @ gate_w.T
        scores = jax.nn.softmax(logits.astype(jnp.float32), axis=-1)
        biased = scores + gate_b.astype(jnp.float32)
        idx = jax.lax.top_k(biased, TOP_K)[1]
        weights = (jnp.take_along_axis(scores, idx, axis=-1) * ROUTE_SCALE).astype(x.dtype)
        cw = jnp.sum(jax.nn.one_hot(idx, E, dtype=x.dtype) * weights[..., None], axis=1)
        h1 = jnp.einsum('td,efd->etf', xt, w1) + b1[:, None, :]
        h3 = jnp.einsum('td,efd->etf', xt, w3) + b3[:, None, :]
        a = swiglu(h1 * h3)
        y = jnp.einsum('etf,edf->etd', a, w2) + b2[:, None, :]
        routed = jnp.einsum('te,etd->td', cw, y)
        sh = swiglu((xt @ sw1.T + sb1) * (xt @ sw3.T + sb3))
        shared = sh @ sw2.T + sb2
        return (routed + shared).reshape(inp_shape)

    def _L1_attn_a_ref(x, W_Q, W_K, W_V, W_O):
        import jax, jax.numpy as jnp
        import numpy as np
        NUM_HEADS = 16
        D_MODEL = 128
        D_K = D_MODEL // NUM_HEADS
        MAX_SEQ_LEN = 512
        ROPE_BASE = 10000.0
        BATCH = 2
        SEQ_LEN = 256

        def _rope_tables(seq_len, d_k, base=ROPE_BASE):
            theta = 1.0 / base ** (jnp.arange(0, d_k, 2, dtype=jnp.float32) / d_k)
            m = jnp.arange(seq_len, dtype=jnp.float32)
            m_theta = jnp.outer(m, theta)
            ang = jnp.concatenate([m_theta, m_theta], axis=-1)
            return (jnp.cos(ang), jnp.sin(ang))

        def _apply_rope(x, cos, sin):
            d2 = x.shape[-1] // 2
            x1, x2 = (x[..., :d2], x[..., d2:])
            x_flip = jnp.concatenate([-x2, x1], axis=-1)
            return x * cos + x_flip * sin
        B, S, _ = x.shape

        def proj(W):
            y = jnp.einsum('bsd,ed->bse', x, W)
            return y.reshape(B, S, NUM_HEADS, D_K).transpose(0, 2, 1, 3)
        Q, K, V = (proj(W_Q), proj(W_K), proj(W_V))
        cos, sin = _rope_tables(S, D_K)
        Q = _apply_rope(Q, cos, sin)
        K = _apply_rope(K, cos, sin)
        scores = jnp.einsum('bhsd,bhtd->bhst', Q, K) / jnp.sqrt(jnp.float32(D_K))
        causal = jnp.tril(jnp.ones((S, S), dtype=bool))
        scores = jnp.where(causal[None, None], scores, -jnp.inf)
        attn = jax.nn.softmax(scores, axis=-1)
        out = jnp.einsum('bhst,bhtd->bhsd', attn, V)
        out = out.transpose(0, 2, 1, 3).reshape(B, S, D_MODEL)
        return jnp.einsum('bsd,ed->bse', out, W_O)

    def _L1_attn_b_ref(up_x, W_up, b_up, conv_w, conv_b, W_delta, b_delta, W_B, b_B, W_C, b_C, A_log, D_skip, W_down, b_down):
        import jax, jax.numpy as jnp
        import numpy as np
        B, L, R = (4, 256, 128)
        HID, EXP, K = (64, 2, 3)
        D = HID * EXP
        N = HID
        Lq = up_x.shape[1]
        u = up_x @ W_up + b_up
        left, right = jnp.split(u, 2, axis=-1)
        xp = jnp.pad(left, ((0, 0), (K - 1, 0), (0, 0)))
        conv = sum((conv_w[:, k] * xp[:, k:k + Lq, :] for k in range(K))) + conv_b
        x = jax.nn.silu(conv)
        delta = jax.nn.softplus(x @ W_delta + b_delta)
        Bm = x @ W_B + b_B
        Cm = x @ W_C + b_C
        A = -jnp.exp(A_log)
        dA = jnp.exp(delta[..., None] * A)
        dBx = delta[..., None] * Bm[:, :, None, :] * x[..., None]

        def step(h, inputs):
            dA_t, dBx_t, C_t = inputs
            h = dA_t * h + dBx_t
            y_t = jnp.einsum('bdn,bn->bd', h, C_t)
            return (h, y_t)
        h0 = jnp.zeros((up_x.shape[0], D, N), dtype=x.dtype)
        _, ys = jax.lax.scan(step, h0, (jnp.swapaxes(dA, 0, 1), jnp.swapaxes(dBx, 0, 1), jnp.swapaxes(Cm, 0, 1)))
        y = jnp.swapaxes(ys, 0, 1) + D_skip * x
        gated = y * jax.nn.silu(right)
        return gated @ W_down + b_down

    def _L1_ffn_ref(hidden_states, gate_w, w_gate_up, w_down, shared_w_gate_up, shared_w_down):
        import jax, jax.numpy as jnp
        import numpy as np
        E = 32
        K = 4
        H = 128
        I = 64
        B, S = (2, 256)
        T = B * S
        C = 128
        ROUTED_SCALE = 1.0

        def _silu_and_mul(gu):
            g, u = jnp.split(gu, 2, axis=-1)
            return jax.nn.silu(g) * u
        b, s, h = hidden_states.shape
        x = hidden_states.reshape(-1, h)
        t = x.shape[0]
        logits = x @ gate_w.T
        probs = jax.nn.softmax(logits, axis=-1)
        topk_w, topk_idx = jax.lax.top_k(probs, K)
        topk_w = topk_w / jnp.sum(topk_w, axis=-1, keepdims=True)
        topk_w = topk_w * ROUTED_SCALE
        e_flat = topk_idx.reshape(-1)
        w_flat = topk_w.reshape(-1)
        t_flat = jnp.repeat(jnp.arange(t), K)
        order = jnp.argsort(e_flat)
        e_s, w_s, t_s = (e_flat[order], w_flat[order], t_flat[order])
        counts = jax.ops.segment_sum(jnp.ones_like(e_s), e_s, num_segments=E)
        starts = jnp.cumsum(counts) - counts
        pos = jnp.arange(t * K) - starts[e_s]
        slot = jnp.minimum(pos, C)
        buf = jnp.zeros((E, C + 1, h), x.dtype).at[e_s, slot].set(x[t_s])
        gu = jnp.einsum('ech,ehi->eci', buf[:, :C], w_gate_up)
        expert_out = jnp.einsum('eci,eih->ech', _silu_and_mul(gu), w_down)
        expert_out = jnp.pad(expert_out, ((0, 0), (0, 1), (0, 0)))
        gate = jnp.where(pos < C, w_s, 0.0)[:, None]
        routed = jnp.zeros_like(x).at[t_s].add(expert_out[e_s, slot] * gate)
        shared = _silu_and_mul(x @ shared_w_gate_up) @ shared_w_down
        return (routed + shared).reshape(b, s, h)
    x = L0_attn_a_x
    x = x + _L0_attn_a_ref(_layernorm(x, axis=-1), L0_attn_a_Wq, L0_attn_a_Wk, L0_attn_a_Wv, L0_attn_a_Wo)
    x = x + _L0_ffn_ref(_layernorm(x, axis=-1), L0_ffn_gate_w, L0_ffn_gate_b, L0_ffn_w1, L0_ffn_b1, L0_ffn_w3, L0_ffn_b3, L0_ffn_w2, L0_ffn_b2, L0_ffn_sw1, L0_ffn_sb1, L0_ffn_sw3, L0_ffn_sb3, L0_ffn_sw2, L0_ffn_sb2)
    x = x + _L0_attn_b_ref(_layernorm(x, axis=-1), L0_attn_b_w_qkv, L0_attn_b_w_out)
    x = x + _L0_ffn_ref(_layernorm(x, axis=-1), L0_ffn_gate_w, L0_ffn_gate_b, L0_ffn_w1, L0_ffn_b1, L0_ffn_w3, L0_ffn_b3, L0_ffn_w2, L0_ffn_b2, L0_ffn_sw1, L0_ffn_sb1, L0_ffn_sw3, L0_ffn_sb3, L0_ffn_sw2, L0_ffn_sb2)
    x = x + _L1_attn_a_ref(_layernorm(x, axis=-1), L1_attn_a_W_Q, L1_attn_a_W_K, L1_attn_a_W_V, L1_attn_a_W_O)
    x = x + _L1_ffn_ref(_layernorm(x, axis=-1), L1_ffn_gate_w, L1_ffn_w_gate_up, L1_ffn_w_down, L1_ffn_shared_w_gate_up, L1_ffn_shared_w_down)
    x = x + _L1_attn_b_ref(_layernorm(x, axis=-1), L1_attn_b_W_up, L1_attn_b_b_up, L1_attn_b_conv_w, L1_attn_b_conv_b, L1_attn_b_W_delta, L1_attn_b_b_delta, L1_attn_b_W_B, L1_attn_b_b_B, L1_attn_b_W_C, L1_attn_b_b_C, L1_attn_b_A_log, L1_attn_b_D_skip, L1_attn_b_W_down, L1_attn_b_b_down)
    x = x + _L1_ffn_ref(_layernorm(x, axis=-1), L1_ffn_gate_w, L1_ffn_w_gate_up, L1_ffn_w_down, L1_ffn_shared_w_gate_up, L1_ffn_shared_w_down)
    return x

_drawn_inputs = setup_inputs


def setup_inputs(seed=0):
    import zlib

    import numpy as np

    out = dict(_drawn_inputs(seed))
    spreads = {'L1_attn_b_D_skip': (1.0, 0.6)}
    factors = {'L0_ffn_b1': 7.194,
     'L0_ffn_b3': 7.165,
     'L0_ffn_b2': 8.0,
     'L0_ffn_sb1': 3.482,
     'L0_ffn_sb3': 4.225,
     'L0_ffn_sb2': 3.272,
     'L1_attn_a_W_Q': 6.992,
     'L1_attn_a_W_K': 6.959,
     'L1_attn_b_W_up': 8.0,
     'L1_attn_b_b_up': 8.0,
     'L1_attn_b_conv_w': 8.0,
     'L1_attn_b_conv_b': 8.0,
     'L1_attn_b_W_delta': 8.0,
     'L1_attn_b_b_delta': 8.0,
     'L1_attn_b_W_B': 8.0,
     'L1_attn_b_b_B': 8.0,
     'L1_attn_b_W_C': 8.0,
     'L1_attn_b_b_C': 8.0,
     'L1_attn_b_A_log': 8.0,
     'L1_attn_b_W_down': 8.0,
     'L1_attn_b_b_down': 6.076,
     'L1_ffn_gate_w': 8.0,
     'L1_ffn_w_gate_up': 8.0,
     'L1_ffn_w_down': 8.0,
     'L1_ffn_shared_w_gate_up': 8.0,
     'L1_ffn_shared_w_down': 8.0}
    for name, (base, spread) in spreads.items():
        noise = np.random.default_rng([zlib.crc32(name.encode()), seed]).standard_normal(out[name].shape)
        drawn = base * np.exp(spread * noise) if base else spread * noise
        out[name] = jnp.asarray(drawn.astype(out[name].dtype))
    for name, factor in factors.items():
        out[name] = (out[name] * factor).astype(out[name].dtype)
    return out
```

```python
from contextlib import ExitStack

import concourse.bass as bass
from concourse import mybir

LAYERS = 8

ALU = mybir.AluOpType
ACT = mybir.ActivationFunctionType
AX_X = mybir.AxisListType.X
F32 = mybir.dt.float32
BF16 = mybir.dt.bfloat16

P = 128
T = 512
NT = T // P
L = 256
NB = T // L
H = 16
DA = 8
DB = 64
E0, K0 = 8, 2
E1, K1 = 32, 4
CAP = 128
ALPHA, LIMIT = 1.702, 7.0
BIG = 1e30


def layout(parts):
    at, where = 0, {}
    for name, width in parts:
        where[name] = (at, width)
        at += width
    return where, at


def tables():
    const = layout([("mean", P), ("ident", P), ("tri", 3 * P), ("trib", 3 * P), ("cosq", L), ("sinq", L),
                    ("cosk", L), ("sink", L), ("ones", L), ("heads", H), ("hot", 2 * P), ("rows", 4), ("eps", 1),
                    ("seg0", NT * E0), ("seg1", NT * E1)])
    half = layout([("sel0", (E0 + 1) * P), ("sel1", (E1 // 2) * P), ("pick", 16 * P), ("lower", P), ("ones", P),
                   ("identb", P)])
    groups = [
        layout([("wq", P), ("wk", P), ("wv", P), ("wo", P)]),
        layout([("gate", E0), ("gate_b", E0), ("b1g", 9), ("b1l", 9), ("b3g", 9), ("b3l", 9), ("b2", P)]
               + [(f"{w}{e}", P) for e in range(E0 + 1) for w in ("w1g", "w3g", "w1l", "w3l", "w2")]),
        layout([("wqkv", 3 * H * DB), ("wout", H * DB)]),
        layout([("wq", P), ("wqf", P), ("wk", P), ("wkf", P), ("wv", P), ("wo", P)]),
        layout([("gate", E1), ("sg", 64), ("su", 64), ("sd", P)]
               + [(f"{w}{p}", P) for p in range(E1 // 2) for w in ("g", "u", "d")]),
        layout([("left", P), ("right", P), ("delta", P), ("wb", P), ("wc", P), ("down", P), ("b_left", 1),
                ("b_right", 1), ("conv_w", 3), ("conv_b", 1), ("b_delta", 1), ("b_b", 1), ("b_c", 1),
                ("skip", 1), ("b_down", 1), ("a_log", 64)]),
    ]
    return const, half, groups


class Core:

    def __init__(self, nc, ctx):
        self.nc, self.ctx = nc, ctx
        self.const_at, self.half_at, self.group_at = tables()
        sb = self.sb
        self.const = sb("const", [P, self.const_at[1]])
        self.half = sb("half", [P, self.half_at[1]], BF16)
        self.weights = [sb(f"weights{g}", [P, width]) for g, (_, width) in enumerate(self.group_at)]
        self.x = sb("x_resid", [P, T])
        self.xn = sb("x_norm", [P, T])
        self.cent = sb("x_centred", [P, T])
        self.sq = sb("x_square", [P, T])
        self.a_neg = sb("a_neg", [P, 64])
        self.base = sb("base", [P, 2, E1])
        self.banks = ctx.enter_context(nc.psum_tensor("banks", [P, 8, 512], F32))
        self.vm = sb("v_by_head", [P, NT, H * (P + DA)])
        self.bank = [self.banks[:, i, :] for i in range(8)]
        self.loaded = ctx.enter_context(nc.semaphore("loaded"))
        self.w_loaded = [ctx.enter_context(nc.semaphore(f"w_loaded{g}")) for g in range(6)]
        self.once = ctx.enter_context(nc.semaphore("once"))
        self.sets = {}
        self.stale = None

    def sb(self, name, shape, dt=F32):
        return self.ctx.enter_context(self.nc.sbuf_tensor(name, shape, dt))

    def c(self, name):
        at, width = self.const_at[0][name]
        return self.const[:, at:at + width]

    def h(self, name):
        at, width = self.half_at[0][name]
        return self.half[:, at:at + width]

    def w(self, g, name):
        at, width = self.group_at[g][0][name]
        return self.weights[g][:, at:at + width]

    def semaphores(self, layer, names):
        if layer not in self.sets:
            self.sets[layer] = {n: self.ctx.enter_context(self.nc.semaphore(f"{layer}_{n}")) for n in names}
        return self.sets[layer]

    def zero_stale(self, engine, mine):
        if self.stale is not None and self.stale is not mine:
            nums = [s.num for s in self.stale.values()]
            engine.sem_clear(range(min(nums), max(nums) + 1))
        self.stale = mine


def chained(engine, sem):
    count = [0]

    def link(ins):
        count[0] += 1
        ins.then_inc(sem, 1)
        engine.wait_ge(sem, count[0])
    return link


def spread(ap, shape, axis):
    return ap.unsqueeze(axis).broadcast_to(shape)


OUT_SEMAPHORES = ["turned", "copied", "stored"]
NORM = ["n_mean", "n_cent", "n_sq", "n_var", "n_ln", "n_rstd", "n_out"]


def norm_tensor(k, pe, s):
    pe.matmul(k.bank[6][:], k.c("mean"), k.x[:], start=True, stop=True).then_inc(s["n_mean"], 1)
    pe.wait_ge(s["n_sq"], 1)
    pe.matmul(k.bank[7][:], k.c("mean"), k.sq[:], start=True, stop=True).then_inc(s["n_var"], 1)
    pe.wait_ge(s["n_out"], 1)


def norm_scalar(k, act, s):
    act.wait_ge(s["n_cent"], 1)
    act.activation(k.sq[:], k.cent[:], ACT.Square).then_inc(s["n_sq"], 1)
    act.wait_ge(s["n_var"], 1)
    act.activation(k.sq[:], k.bank[7][:], ACT.Ln, bias=k.c("eps")).then_inc(s["n_ln"], 1)
    act.wait_ge(s["n_ln"], 1)
    act.activation(k.sq[:], k.sq[:], ACT.Exp, scale=-0.5).then_inc(s["n_rstd"], 1)


def norm_vector(k, dve, s):
    dve.wait_ge(s["n_mean"], 1)
    dve.tensor_tensor(k.cent[:], k.x[:], k.bank[6][:], ALU.subtract).then_inc(s["n_cent"], 1)
    dve.wait_ge(s["n_rstd"], 1)
    dve.tensor_tensor(k.xn[:], k.cent[:], k.sq[:], ALU.mult).then_inc(s["n_out"], 1)
    dve.wait_ge(s["n_out"], 1)


def load_tokens(k, it, x_in, tag):
    nc = k.nc
    s = k.semaphores("io", ["tokens", "turned", "copied", "stored"])
    with nc.sbuf_tensor(f"tok_in{tag}", [P, NT, P], F32) as tok, nc.Block(no_gpsimd_drain=True) as block:
        @block.sync
        def _(sp):
            k.zero_stale(sp, s)
            sp.dma_start(tok[:], x_in[bass.ds(it, 1)].rearrange("o (j p) d -> p (o j) d", p=P)).then_inc(s["tokens"], 16)

        @block.tensor
        def _(pe):
            pe.wait_ge(s["tokens"], 16)
            pe.wait_ge(k.loaded, 32)
            for j in range(NT):
                ins = pe.transpose(k.bank[0][:, j * P:(j + 1) * P], tok[:, j, :], k.c("ident"))
            ins.then_inc(s["turned"], 1)

        @block.vector
        def _(dve):
            dve.wait_ge(s["turned"], 1)
            dve.tensor_copy(k.x[:], k.bank[0][:]).then_inc(s["copied"], 1)


def store_tokens(k, it, x_out, tag):
    nc = k.nc
    s = k.semaphores("out", OUT_SEMAPHORES)
    with nc.sbuf_tensor(f"tok_out{tag}", [P, NT, P], F32) as tok, nc.Block(no_gpsimd_drain=True) as block:
        @block.tensor
        def _(pe):
            pe.wait_ge(k.loaded, 32)
            for j in range(NT):
                ins = pe.transpose(k.bank[0][:, j * P:(j + 1) * P], k.x[:, j * P:(j + 1) * P], k.c("ident"))
            ins.then_inc(s["turned"], 1)

        @block.vector
        def _(dve):
            dve.wait_ge(s["turned"], 1)
            dve.tensor_copy(tok[:].rearrange("p j d -> p (j d)"), k.bank[0][:]).then_inc(s["copied"], 1)

        @block.sync
        def _(sp):
            k.zero_stale(sp, s)
            sp.wait_ge(s["copied"], 1)
            sp.dma_start(x_out[bass.ds(it, 1)].rearrange("o (j p) d -> p (o j) d", p=P), tok[:]).then_inc(s["stored"], 16)
            sp.wait_ge(s["stored"], 16)


def narrow_attention(k, tag, linear):
    nc = k.nc
    G = 0 if linear else 3
    layer = "lin" if linear else "rot"
    s = k.semaphores("narrow", NORM + ["proj", "low", "high", "qk", "vcopy", "dve", "scores", "probs_in", "probs",
                                       "turned", "pt", "pv", "sums", "prod", "wide", "wide_t", "ot", "y", "done"])
    w = lambda name: k.w(G, name)
    stages = [(b, c, jj) for b in range(NB) for c in range(4) for jj in range(2)]
    NS = len(stages)
    by_head = k.vm[:, :, 0:H * (P + DA)].rearrange("p t (h x) -> p t h x", x=P + DA)[:, :, :, 0:DA]
    with ExitStack() as ctx:
        def sb(name, shape, dt=F32):
            return ctx.enter_context(nc.sbuf_tensor(f"{layer}_{name}{tag}", shape, dt))
        q, kk = sb("q", [P, T]), sb("k", [P, T])
        km = sb("km", [P, 4, T])
        t1, t2 = sb("t1", [P, T]), sb("t2", [P, T])
        pin = sb("pin", [P, 2, 2, 3 * P])
        pt = sb("pt", [P, 2, 2, 3 * P])
        low = sb("low", [P, 2, 4])
        den = sb("den", [P, NT, H])
        wide = sb("wide", [P, NT, H, DA])
        ot = sb("ot", [P, T])
        block = ctx.enter_context(nc.Block(no_gpsimd_drain=True))

        @block.sync
        def _(sp):
            k.zero_stale(sp, s)

        @block.tensor
        def _(pe):
            pe.wait_ge(k.loaded, 32)
            pe.wait_ge(k.w_loaded[G], 16)
            norm_tensor(k, pe, s)
            names = ["wq", "wk"] if linear else ["wq", "wqf", "wk", "wkf"]
            for n, name in enumerate(names):
                pe.matmul(k.bank[n][:], w(name), k.xn[:], start=True, stop=True).then_inc(s["proj"], 1)
            for j in range(NT):
                ins = pe.matmul(k.bank[4][:, j * P:(j + 1) * P], k.xn[:, j * P:(j + 1) * P], w("wv"),
                                start=True, stop=True)
            ins.then_inc(s["proj"], 1)

            def scores(i):
                b, c, jj = stages[i]
                if i >= 2:
                    pe.wait_ge(s["probs" if linear else "probs_in"], i - 1)
                for m in range(2):
                    j = 2 * jj + m
                    r = slice(32 * j, 32 * j + 32)
                    t0, o = b * L, k.bank[2 * (i % 2) + m]
                    if linear:
                        pe.matmul(o[:, 0:L], km[r, c, t0:t0 + P], q[r, t0:t0 + L], start=True, stop=True)
                        ins = pe.matmul(o[:, L:L + P], km[r, c, t0 + P:t0 + L], q[r, t0 + P:t0 + L],
                                        start=True, stop=True)
                    else:
                        pe.matmul(o[:, 0:P], q[r, t0:t0 + P], km[r, c, t0:t0 + P], start=True, stop=True)
                        ins = pe.matmul(o[:, P:P + L], q[r, t0 + P:t0 + L], km[r, c, t0:t0 + L],
                                        start=True, stop=True)
                ins.then_inc(s["scores"], 1)

            def turn(i):
                pe.wait_ge(s["probs"], i + 1)
                if i >= 1:
                    pe.wait_ge(s["pt"], i)
                for m in range(2):
                    for n in range(3):
                        ins = pe.transpose(k.bank[4 + m][:, n * P:(n + 1) * P],
                                           pin[:, i % 2, m, n * P:(n + 1) * P], k.c("ident"))
                ins.then_inc(s["turned"], 1)

            def weigh(i):
                b, c, jj = stages[i]
                pe.wait_ge(s["probs" if linear else "pt"], i + 1)
                for m in range(2):
                    head = 4 * (2 * jj + m) + c
                    p, first, last = pt[:, i % 2, m, :], c == jj == m == 0, head == 4 * 3 + 3
                    v = lambda tile: k.vm[:, tile, head * P:(head + 1) * P]
                    pe.matmul(k.bank[6][:, b * L:(b + 1) * L], v(2 * b), p[:, 0:L], start=first, stop=False,
                              skip_group_check=True)
                    ins = pe.matmul(k.bank[6][:, b * L + P:(b + 1) * L], v(2 * b + 1), p[:, L:L + P],
                                    start=False, stop=last, skip_group_check=True)
                ins.then_inc(s["pv"], 1)

            pe.wait_ge(s["qk"], 1)
            pe.wait_ge(s["vcopy"], 1)
            scores(0)
            scores(1)
            if linear:
                for i in range(NS):
                    weigh(i)
                    if i + 2 < NS:
                        scores(i + 2)
                    if i == 1:
                        pe.wait_ge(s["prod"], 1)
                        for j in range(NT):
                            ins = pe.matmul(k.bank[5][:, j * H:(j + 1) * H], t1[:, j * P:(j + 1) * P],
                                            k.c("heads"), start=True, stop=True)
                        ins.then_inc(s["sums"], 1)
            else:
                turn(0)
                for i in range(NS):
                    if i + 2 < NS:
                        scores(i + 2)
                    if i + 1 < NS:
                        turn(i + 1)
                    weigh(i)
            pe.wait_ge(s["wide"], 1)
            for j in range(NT):
                ins = pe.transpose(k.bank[7][:, j * P:(j + 1) * P],
                                   wide[:, j].rearrange("p h e -> p (h e)"), k.c("ident"))
            ins.then_inc(s["wide_t"], 1)
            pe.wait_ge(s["ot"], 1)
            pe.matmul(k.bank[0][:], w("wo"), ot[:], start=True, stop=True).then_inc(s["y"], 1)

        @block.scalar
        def _(act):
            act.wait_ge(k.loaded, 32)
            norm_scalar(k, act, s)
            if linear:
                for n, t in enumerate((t1, t2)):
                    act.wait_ge(s["low"], n + 1)
                    act.activation(t[:], t[:], ACT.Exp).then_inc(s["high"], 1)
            act.wait_ge(k.once, 1)
            act.wait_ge(s["proj"], 3 if linear else 5)
            act.activation(by_head, k.bank[4][:].rearrange("p (t h e) -> p t h e", t=NT, h=H),
                           ACT.Copy).then_inc(s["vcopy"], 1)
            if not linear:
                for i in range(NS):
                    b, c, jj = stages[i]
                    act.wait_ge(s["probs_in"], i + 1)
                    for m in range(2):
                        for t, cols in enumerate((slice(0, P), slice(P, 3 * P))):
                            head = 4 * (2 * jj + m) + c
                            ins = act.activation(pin[:, i % 2, m, cols], pin[:, i % 2, m, cols], ACT.Exp,
                                                 bias=low[:, i % 2, 2 * m + t:2 * m + t + 1], scale=-1.0,
                                                 accum_out=den[:, 2 * b + t, head:head + 1])
                    ins.then_inc(s["probs"], 1)
            act.wait_ge(s["wide_t"], 1)
            act.activation(t2[:], k.bank[7][:], ACT.Copy).then_inc(s["wide_t"], 1)

        @block.vector
        def _(dve):
            link = chained(dve, s["dve"])
            dve.wait_ge(k.loaded, 32)
            norm_vector(k, dve, s)
            if linear:
                for n, t in enumerate((t1, t2)):
                    dve.wait_ge(s["proj"], n + 1)
                    dve.tensor_scalar(t[:], k.bank[n][:], 0.0, None, ALU.min).then_inc(s["low"], 1)
                for n, (t, o) in enumerate(((t1, q), (t2, kk))):
                    dve.wait_ge(s["high"], n + 1)
                    link(dve.scalar_tensor_tensor(o[:], k.bank[n][:], 0.0, t[:], ALU.max, ALU.add))
            else:
                rope = [(q, 0, 1, "cosq", "sinq"), (kk, 2, 3, "cosk", "sink")]
                for o, a, f, cos, sin in rope:
                    dve.wait_ge(s["proj"], f + 1)
                    table = lambda name: spread(k.c(name), [P, NB, L], 1)
                    two = lambda ap: ap.rearrange("p (b t) -> p b t", b=NB)
                    link(dve.tensor_tensor(two(t1[:]), two(k.bank[a][:]), table(cos), ALU.mult))
                    link(dve.tensor_tensor(two(t2[:]), two(k.bank[f][:]), table(sin), ALU.mult))
                    link(dve.tensor_tensor(o[:], t1[:], t2[:], ALU.add))
            for c in range(4):
                ins = dve.tensor_scalar(km[:, c, :], kk[:], k.c("rows")[:, c:c + 1], None, ALU.mult)
            ins.then_inc(s["qk"], 1)
            for i in range(NS + 1):
                if i < NS:
                    dve.wait_ge(s["scores"], i + 1)
                    if linear:
                        if i >= 2:
                            dve.wait_ge(s["pv"], i - 1)
                        for m in range(2):
                            ins = dve.tensor_tensor(pt[:, i % 2, m, :], k.bank[2 * (i % 2) + m][:, 0:3 * P],
                                                    k.c("tri"), ALU.mult)
                        ins.then_inc(s["probs"], 1)
                    else:
                        if i >= 2:
                            dve.wait_ge(s["turned"], i - 1)
                        for m in range(2):
                            for t, cols in enumerate((slice(0, P), slice(P, 3 * P))):
                                ins = dve.tensor_tensor_reduce(
                                    pin[:, i % 2, m, cols], k.bank[2 * (i % 2) + m][:, cols],
                                    k.c("trib")[:, cols], 1.0, 3e38, ALU.add, ALU.min,
                                    low[:, i % 2, 2 * m + t:2 * m + t + 1])
                        ins.then_inc(s["probs_in"], 1)
                if linear and i == 0:
                    for b in range(NB):
                        cols = slice(b * L, (b + 1) * L)
                        link(dve.tensor_tensor_scan(t2[:, cols], k.c("ones"), kk[:, cols], 0.0, ALU.mult, ALU.add))
                    dve.tensor_tensor(t1[:], t2[:], q[:], ALU.mult).then_inc(s["prod"], 1)
                if i >= 1 and not linear:
                    dve.wait_ge(s["turned"], i)
                    if i >= 3:
                        dve.wait_ge(s["pv"], i - 2)
                    for m in range(2):
                        ins = dve.tensor_copy(pt[:, (i - 1) % 2, m, :], k.bank[4 + m][:, 0:3 * P])
                    ins.then_inc(s["pt"], 1)
            flat = lambda ap: ap[:].rearrange("p t h -> p (t h)")
            if linear:
                dve.wait_ge(s["sums"], 1)
                link(dve.tensor_scalar(flat(den), k.bank[5][:, 0:NT * H], 1e-6, None, ALU.max))
            else:
                dve.wait_ge(s["probs"], NS)
            link(dve.reciprocal(den[:], den[:]))
            dve.tensor_copy(wide[:], spread(den[:], [P, NT, H, DA], 3)).then_inc(s["wide"], 1)
            dve.wait_ge(s["pv"], NS)
            dve.wait_ge(s["wide_t"], 2)
            dve.tensor_tensor(ot[:], k.bank[6][:], t2[:], ALU.mult).then_inc(s["ot"], 1)
            dve.wait_ge(s["y"], 1)
            dve.tensor_tensor(k.x[:], k.x[:], k.bank[0][:], ALU.add).then_inc(s["done"], 1)


ROUTE = ["logits", "r_diff", "r_exp", "r_split", "r_turned", "r_rows", "r_count", "r_dve"]


def route_tensor(k, pe, s, g, experts, ranks, split, mask, cw):
    gate = k.w(g, "gate")
    for j in range(NT):
        ins = pe.matmul(k.bank[6][:, j * experts:(j + 1) * experts], k.xn[:, j * P:(j + 1) * P], gate,
                        start=True, stop=True)
    ins.then_inc(s["logits"], 1)
    if mask is not None:
        pe.wait_ge(s["r_count"], 1)
        pe.wait_ge(s["r_diff"], 1)
        for j in range(NT + 1):
            out = k.bank[6][:, j * experts:(j + 1) * experts]
            for i in range(min(j, NT)):
                ins = pe.matmul(out, k.h("ones"), mask[:, i, :], start=(i == 0), stop=(i == j - 1 and j == NT))
            if j < NT:
                ins = pe.matmul(out, k.h("lower"), mask[:, j, :], start=(j == 0), stop=True)
        ins.then_inc(s["r_count"], 1)
    pe.wait_ge(s["r_split"], 1)
    rows = split.shape[2]
    turned = k.bank[7][:].bitcast(BF16)
    for j in range(NT):
        ins = pe.transpose(turned[0:rows, j * P:(j + 1) * P], split[:, j, :], k.h("identb"))
    ins.then_inc(s["r_turned"], 1)


def route_vector(k, dve, s, link, buf, experts, choices, bias, seg, cap):
    E = experts
    logits = k.bank[6][:, 0:NT * E].rearrange("p (j e) -> p j e", e=E)
    full = [P, NT, E]
    dve.wait_ge(s["logits"], 1)
    link(dve.tensor_reduce(buf["top"][:], logits, AX_X, ALU.max))
    dve.tensor_tensor(buf["diff"][:], logits, spread(buf["top"][:], full, 2), ALU.subtract).then_inc(s["r_diff"], 1)
    dve.wait_ge(s["r_exp"], 1)
    link(dve.tensor_reduce(buf["sum"][:], buf["exp"][:], AX_X, ALU.add))
    link(dve.reciprocal(buf["sum"][:], buf["sum"][:]))
    link(dve.tensor_tensor(buf["score"][:], buf["exp"][:], spread(buf["sum"][:], full, 2), ALU.mult))
    ranked = buf["score"]
    if bias is not None:
        ranked = buf["diff"]
        link(dve.tensor_tensor(ranked[:], buf["score"][:], spread(bias, full, 1), ALU.add))
    for j in range(NT):
        ins = dve.max(buf["best"][:, j, :], ranked[:, j, :])
    link(ins)
    last = spread(buf["best"][:, :, choices - 1], full, 2)
    link(dve.tensor_tensor(buf["over"][:], ranked[:], last, ALU.is_gt))
    link(dve.tensor_reduce(buf["top"][:], buf["over"][:], AX_X, ALU.add))
    link(dve.tensor_scalar(buf["top"][:], buf["top"][:], -1.0, float(choices), ALU.mult, ALU.add))
    link(dve.tensor_tensor(buf["equal"][:], ranked[:], last, ALU.is_equal))
    flat = lambda b: b[:].rearrange("p j e -> p (j e)")
    link(dve.tensor_tensor_scan(flat(buf["rank"]), k.c(seg), flat(buf["equal"]), 0.0, ALU.mult, ALU.add))
    link(dve.tensor_tensor(buf["rank"][:], buf["rank"][:], spread(buf["top"][:], full, 2), ALU.is_le))
    link(dve.tensor_tensor(buf["equal"][:], buf["equal"][:], buf["rank"][:], ALU.mult))
    link(dve.tensor_tensor(buf["over"][:], buf["over"][:], buf["equal"][:], ALU.add))
    cw = buf["cw"][:, :, 0:E]
    link(dve.tensor_tensor(cw, buf["score"][:], buf["over"][:], ALU.mult))
    if cap:
        dve.tensor_copy(buf["mask"][:], buf["over"][:]).then_inc(s["r_count"], 1)
        link(dve.tensor_reduce(buf["sum"][:], cw, AX_X, ALU.add))
        link(dve.reciprocal(buf["sum"][:], buf["sum"][:]))
        link(dve.tensor_tensor(cw, cw, spread(buf["sum"][:], full, 2), ALU.mult))
        dve.wait_ge(s["r_count"], 2)
        link(dve.tensor_tensor(buf["rank"][:], logits, spread(buf["base"], full, 1), ALU.add))
        link(dve.tensor_scalar(buf["rank"][:], buf["rank"][:], float(CAP), None, ALU.is_le))
        dve.tensor_tensor(buf["base"], buf["base"], k.bank[6][:, NT * E:(NT + 1) * E], ALU.add)
        link(dve.tensor_tensor(cw, cw, buf["rank"][:], ALU.mult))
    W = buf["cw"].shape[2]
    part = lambda n: buf["split"][:, :, n * W:(n + 1) * W]
    link(dve.tensor_copy(part(0), buf["cw"][:]))
    link(dve.tensor_tensor(buf["rest"][:], buf["cw"][:], part(0), ALU.subtract))
    link(dve.tensor_copy(part(1), buf["rest"][:]))
    link(dve.tensor_tensor(buf["rest"][:], buf["rest"][:], part(1), ALU.subtract))
    dve.tensor_copy(part(2), buf["rest"][:]).then_inc(s["r_split"], 1)
    dve.wait_ge(s["r_turned"], 1)
    rows = 3 * W
    dve.tensor_copy(buf["rows"][0:rows, :], k.bank[7][:].bitcast(BF16)[0:rows, 0:T]).then_inc(s["r_rows"], 1)


def route_buffers(sb, experts, width, base):
    full = [P, NT, experts]
    buf = {n: sb("r_" + n, full) for n in ("diff", "exp", "score", "over", "equal", "rank")}
    buf["best"] = sb("r_best", [P, NT, 8])
    buf["top"], buf["sum"] = sb("r_top", [P, NT]), sb("r_sum", [P, NT])
    buf["cw"], buf["rest"] = sb("r_cw", [P, NT, width]), sb("r_rest", [P, NT, width])
    buf["split"] = sb("r_split", [P, NT, 3 * width], BF16)
    buf["rows"] = sb("r_rows", [P, T], BF16)
    buf["mask"] = sb("r_mask", full, BF16)
    buf["base"] = base
    return buf


def biased_ffn(k, tag):
    nc = k.nc
    G, N, W = 1, E0 + 1, E0 + 1
    s = k.semaphores("ffn0", NORM + ROUTE + ["dve", "h", "cw", "h1", "h3", "gate", "tanh", "act", "down", "b2", "done"])
    w = lambda name: k.w(G, name)
    with ExitStack() as ctx:
        def sb(name, shape, dt=F32):
            return ctx.enter_context(nc.sbuf_tensor(f"ffn0_{name}{tag}", shape, dt))
        buf = route_buffers(sb, E0, W, None)
        s1 = [sb(f"s1{c}", [P, 2, T]) for c in "gl"]
        hg, hl = sb("hg", [P, 2, T]), sb("hl", [P, 2, T])
        th = sb("th", [P, 2, T])
        p1 = sb("p1", [P, T])
        a = sb("a", [P, 2, T])
        cwr = sb("cwr", [P, T])
        block = ctx.enter_context(nc.Block(no_gpsimd_drain=True))

        @block.sync
        def _(sp):
            k.zero_stale(sp, s)

        @block.tensor
        def _(pe):
            pe.wait_ge(k.loaded, 32)
            pe.wait_ge(k.w_loaded[G], 16)
            norm_tensor(k, pe, s)

            def up(e):
                for n, (name, freed) in enumerate((("w1g", "h1"), ("w3g", "h3"), ("w1l", "h1"), ("w3l", "h3"))):
                    if e >= 1:
                        pe.wait_ge(s[freed], 2 * (e - 1) + n // 2 + 1)
                    pe.matmul(k.bank[n][:], w(f"{name}{e}"), k.xn[:], start=True, stop=True).then_inc(s["h"], 1)

            def spread_weights(e):
                if e >= 1:
                    pe.wait_ge(s["act"], e)
                pe.matmul(k.bank[4][:], k.h("sel0")[0:3 * W, e * P:(e + 1) * P], buf["rows"][0:3 * W, :],
                          start=True, stop=True).then_inc(s["cw"], 1)

            def down(e):
                pe.wait_ge(s["act"], e + 1)
                pe.matmul(k.bank[5][:], w(f"w2{e}"), a[:, e % 2, :], start=(e == 0), stop=False) \
                    .then_inc(s["down"], 1)

            up(0)
            route_tensor(k, pe, s, G, E0, None, buf["split"], None, None)
            pe.wait_ge(s["r_rows"], 1)
            spread_weights(0)
            for e in range(1, N):
                up(e)
                down(e - 1)
                spread_weights(e)
            for j in range(NT):
                ins = pe.transpose(k.bank[6][0:W, j * P:(j + 1) * P], buf["cw"][:, j, :], k.c("ident"))
            ins.then_inc(s["b2"], 1)
            down(N - 1)
            pe.wait_ge(s["b2"], 2)
            pe.matmul(k.bank[5][:], w("b2")[0:W, :], cwr[0:W, :], start=False, stop=True).then_inc(s["down"], 1)

        @block.scalar
        def _(act):
            act.wait_ge(k.loaded, 32)
            act.wait_ge(k.w_loaded[G], 16)
            norm_scalar(k, act, s)

            def first(e, c):
                act.wait_ge(s["h"], 4 * e + 2 * c + 1)
                if e >= 2:
                    act.wait_ge(s["h3"], 2 * (e - 2) + c + 1)
                act.activation(s1[c][:, e % 2, :], k.bank[2 * c][:], ACT.Identity,
                               bias=w("b1" + "gl"[c])[:, e:e + 1]).then_inc(s["h1"], 1)

            for e in range(N):
                first(e, 0)
                if e == 0:
                    act.wait_ge(s["r_diff"], 1)
                    act.activation(buf["exp"][:], buf["diff"][:], ACT.Exp).then_inc(s["r_exp"], 1)
                first(e, 1)
                act.wait_ge(s["gate"], e + 1)
                if e >= 2:
                    act.wait_ge(s["act"], e - 1)
                act.activation(th[:, e % 2, :], hg[:, e % 2, :], ACT.Tanh, scale=ALPHA / 2).then_inc(s["tanh"], 1)
            act.wait_ge(s["b2"], 1)
            act.activation(cwr[0:W, :], k.bank[6][0:W, :], ACT.Copy).then_inc(s["b2"], 1)

        @block.vector
        def _(dve):
            link = chained(dve, s["dve"])
            dve.wait_ge(k.loaded, 32)
            dve.wait_ge(k.w_loaded[G], 16)
            norm_vector(k, dve, s)
            link(dve.memset(buf["cw"][:, :, E0:W], 1.0))

            def hidden(e, c, h):
                dve.wait_ge(s["h1"], 2 * e + c + 1)
                dve.wait_ge(s["h"], 4 * e + 2 * c + 2)
                dve.scalar_tensor_tensor(h[:, e % 2, :], k.bank[2 * c + 1][:], w("b3" + "gl"[c])[:, e:e + 1],
                                         s1[c][:, e % 2, :], ALU.add, ALU.mult).then_inc(s["h3"], 1)
                dve.wait_ge(s["h3"], 2 * e + c + 1)

            def halves(e):
                hidden(e, 0, hg)
                dve.tensor_scalar(hg[:, e % 2, :], hg[:, e % 2, :], LIMIT, None, ALU.min).then_inc(s["gate"], 1)
                hidden(e, 1, hl)
                link(dve.tensor_scalar(hl[:, e % 2, :], hl[:, e % 2, :], LIMIT, -LIMIT, ALU.min, ALU.max))

            route_vector(k, dve, s, link, buf, E0, K0, w("gate_b"), "seg0", False)
            for e in range(N):
                halves(e)
                dve.wait_ge(s["tanh"], e + 1)
                link(dve.scalar_tensor_tensor(p1[:], th[:, e % 2, :], 1.0, hg[:, e % 2, :], ALU.add, ALU.mult))
                link(dve.scalar_tensor_tensor(p1[:], hl[:, e % 2, :], 1.0, p1[:], ALU.add, ALU.mult))
                dve.wait_ge(s["cw"], e + 1)
                if e >= 2:
                    dve.wait_ge(s["down"], e - 1)
                dve.tensor_tensor(a[:, e % 2, :], p1[:], k.bank[4][:], ALU.mult).then_inc(s["act"], 1)
                dve.wait_ge(s["act"], e + 1)
            dve.wait_ge(s["down"], N + 1)
            dve.tensor_tensor(k.x[:], k.x[:], k.bank[5][:], ALU.add).then_inc(s["done"], 1)


def wide_attention(k, tag):
    nc = k.nc
    G, HP = 2, H // 2
    s = k.semaphores("wide", NORM + ["v", "v_act", "v_dve", "q", "qc", "k", "kc", "scores", "max", "probs", "turned",
                                     "pt_act", "pt_dve", "pv", "outn", "ot", "ot_act", "ot_dve", "y", "dve", "done"])
    at, _ = k.group_at[G][0]["wqkv"]
    wcol = lambda n: k.weights[G][:, at + n * P:at + (n + 1) * P]
    stages = [(g, b) for g in range(HP) for b in range(NB)]
    NS = len(stages)
    with ExitStack() as ctx:
        def sb(name, shape, dt=F32):
            return ctx.enter_context(nc.sbuf_tensor(f"wide_{name}{tag}", shape, dt))
        q, kk = sb("q", [P, 2, T]), sb("k", [P, 2, T])
        va = sb("va", [P, NT, H, DB + 1])
        pin = sb("pin", [P, 2, 2, T])
        pt = sb("pt", [P, 2, 2, T])
        low = sb("low", [P, 2, 4])
        rden = sb("rden", [P, 2, 2])
        on = sb("on", [P, NT, H, DB])
        ot = sb("ot", [P, 2, T])
        block = ctx.enter_context(nc.Block(no_gpsimd_drain=True))
        out = k.bank[6][:, 0:4 * (DB + 1)].rearrange("p (t m e) -> p t m e", t=2, m=2)

        @block.sync
        def _(sp):
            k.zero_stale(sp, s)

        @block.tensor
        def _(pe):
            pe.wait_ge(k.loaded, 32)
            pe.wait_ge(k.w_loaded[G], 16)
            norm_tensor(k, pe, s)
            for n in range(2 * NT):
                j, half = n // 2, n % 2
                if n >= 6:
                    pe.wait_ge(s["v_act" if n % 2 == 0 else "v_dve"], (n - 6) // 2 + 1)
                first = at + (2 * H * DB) + half * 512
                pe.matmul(k.bank[n % 6][:], k.xn[:, j * P:(j + 1) * P], k.weights[G][:, first:first + 512],
                          start=True, stop=True).then_inc(s["v"], 1)

            def project(g, which):
                if which == 0:
                    if g >= 1:
                        pe.wait_ge(s["kc"], g)
                    pe.matmul(k.bank[7][:], wcol(g), k.xn[:], start=True, stop=True).then_inc(s["q"], 1)
                else:
                    pe.wait_ge(s["qc"], g + 1)
                    pe.matmul(k.bank[7][:], wcol(HP + g), k.xn[:], start=True, stop=True).then_inc(s["k"], 1)

            def scores(i):
                g, b = stages[i]
                pe.wait_ge(s["kc"], g + 1)
                if i >= 2:
                    pe.wait_ge(s["probs"], i - 1)
                else:
                    pe.wait_ge(s["v_act"], NT)
                    pe.wait_ge(s["v_dve"], NT)
                for m in range(2):
                    r = slice(64 * m, 64 * m + 64)
                    for t in range(2):
                        ins = pe.matmul(k.bank[2 * (i % 2) + m][:, t * L:(t + 1) * L],
                                        q[r, g % 2, b * L + t * P:b * L + (t + 1) * P],
                                        kk[r, g % 2, b * L:(b + 1) * L], start=True, stop=True)
                ins.then_inc(s["scores"], 1)

            def turn(i):
                pe.wait_ge(s["probs"], i + 1)
                if i >= 1:
                    pe.wait_ge(s["pt_act"], i)
                    pe.wait_ge(s["pt_dve"], i)
                for m in range(2):
                    for key in range(2):
                        for t in range(2):
                            ins = pe.transpose(k.bank[4 + m][:, key * L + t * P:key * L + (t + 1) * P],
                                               pin[:, i % 2, m, t * L + key * P:t * L + (key + 1) * P], k.c("ident"))
                ins.then_inc(s["turned"], 1)

            def weigh(i):
                g, b = stages[i]
                pe.wait_ge(s["pt_act"], i + 1)
                pe.wait_ge(s["pt_dve"], i + 1)
                if i >= 1:
                    pe.wait_ge(s["outn"], i)
                for m in range(2):
                    for t in range(2):
                        for key in range(2):
                            ins = pe.matmul(out[:, t, m, :], pt[:, i % 2, m, key * L + t * P:key * L + (t + 1) * P],
                                            va[:, 2 * b + key, 2 * g + m, :], start=(key == 0), stop=(key == 1))
                ins.then_inc(s["pv"], 1)

            project(0, 0)
            project(0, 1)
            for i in range(NS + 2):
                if i < NS:
                    scores(i)
                    if i + 2 < NS:
                        project(i // 2 + 1, i % 2)
                if 1 <= i <= NS:
                    turn(i - 1)
                if i >= 2:
                    weigh(i - 2)
            pe.wait_ge(s["outn"], NS)
            for g in range(HP):
                if g >= 2:
                    pe.wait_ge(s["ot_act" if g % 2 == 0 else "ot_dve"], g // 2)
                for j in range(NT):
                    ins = pe.transpose(k.bank[g % 2][:, j * P:(j + 1) * P],
                                       on[:, j, 2 * g:2 * g + 2, :].rearrange("p h e -> p (h e)"), k.c("ident"))
                ins.then_inc(s["ot"], 1)
                if g >= 1:
                    last = g - 1
                    pe.wait_ge(s["ot_act" if last % 2 == 0 else "ot_dve"], last // 2 + 1)
                    pe.matmul(k.bank[7][:], k.w(G, "wout")[:, last * P:(last + 1) * P], ot[:, last % 2, :],
                              start=(last == 0), stop=False).then_inc(s["y"], 1)
            pe.wait_ge(s["ot_dve"], HP // 2)
            pe.matmul(k.bank[7][:], k.w(G, "wout")[:, (HP - 1) * P:], ot[:, 1, :],
                      start=False, stop=True).then_inc(s["y"], 1)

        @block.scalar
        def _(act):
            act.wait_ge(k.loaded, 32)
            norm_scalar(k, act, s)
            for n in range(0, 2 * NT, 2):
                act.wait_ge(s["v"], n + 1)
                act.activation(va[:, n // 2, 0:8, 0:DB], k.bank[n % 6].rearrange("p (h e) -> p h e", e=DB),
                               ACT.Copy).then_inc(s["v_act"], 1)

            def copy_q(g):
                act.wait_ge(s["q"], g + 1)
                if g >= 2:
                    act.wait_ge(s["scores"], 2 * g - 2)
                act.activation(q[:, g % 2, :], k.bank[7][:], ACT.Copy, scale=float(DB) ** -0.5).then_inc(s["qc"], 1)

            def copy_k(g):
                act.wait_ge(s["k"], g + 1)
                if g >= 2:
                    act.wait_ge(s["scores"], 2 * g - 2)
                act.activation(kk[:, g % 2, :], k.bank[7][:], ACT.Copy).then_inc(s["kc"], 1)

            copy_q(0)
            copy_k(0)
            for i in range(NS + 1):
                if i < NS:
                    act.wait_ge(s["max"], i + 1)
                    if i >= 2:
                        act.wait_ge(s["turned"], i - 1)
                    for m in range(2):
                        for t in range(2):
                            cols = slice(t * L, (t + 1) * L)
                            ins = act.activation(pin[:, i % 2, m, cols], k.bank[2 * (i % 2) + m][:, cols], ACT.Exp,
                                                 bias=low[:, i % 2, 2 * m + t:2 * m + t + 1])
                    ins.then_inc(s["probs"], 1)
                    if i + 2 < NS:
                        (copy_q if i % 2 == 0 else copy_k)(i // 2 + 1)
                if i >= 1:
                    act.wait_ge(s["turned"], i)
                    if i >= 3:
                        act.wait_ge(s["pv"], i - 2)
                    act.activation(pt[:, (i - 1) % 2, 0, :], k.bank[4][:], ACT.Copy).then_inc(s["pt_act"], 1)
            for g in range(0, HP, 2):
                act.wait_ge(s["ot"], g + 1)
                if g >= 2:
                    act.wait_ge(s["y"], g - 1)
                act.activation(ot[:, 0, :], k.bank[0][:], ACT.Copy).then_inc(s["ot_act"], 1)

        @block.vector
        def _(dve):
            link = chained(dve, s["dve"])
            dve.wait_ge(k.loaded, 32)
            norm_vector(k, dve, s)
            link(dve.memset(va[:, :, :, DB:DB + 1], 1.0))
            for n in range(1, 2 * NT, 2):
                dve.wait_ge(s["v"], n + 1)
                dve.tensor_copy(va[:, n // 2, 8:16, 0:DB], k.bank[n % 6].rearrange("p (h e) -> p h e", e=DB)) \
                    .then_inc(s["v_dve"], 1)
            for i in range(NS + 2):
                if i < NS:
                    dve.wait_ge(s["scores"], i + 1)
                    if i >= 2:
                        dve.wait_ge(s["probs"], i - 1)
                    dve.tensor_reduce(low[:, i % 2, :],
                                      k.banks[:, 2 * (i % 2):2 * (i % 2) + 2, :].rearrange("p m (t c) -> p (m t) c", c=L),
                                      AX_X, ALU.max, negate=True).then_inc(s["max"], 1)
                if 1 <= i <= NS:
                    dve.wait_ge(s["turned"], i)
                    if i >= 3:
                        dve.wait_ge(s["pv"], i - 2)
                    dve.tensor_copy(pt[:, (i - 1) % 2, 1, :], k.bank[5][:]).then_inc(s["pt_dve"], 1)
                if i >= 2:
                    g, b = stages[i - 2]
                    dve.wait_ge(s["pv"], i - 1)
                    link(dve.reciprocal(rden[:], out[:, :, :, DB]))
                    dve.tensor_tensor(on[:, 2 * b:2 * b + 2, 2 * g:2 * g + 2, :], out[:, :, :, 0:DB],
                                      spread(rden[:], [P, 2, 2, DB], 3), ALU.mult).then_inc(s["outn"], 1)
                    dve.wait_ge(s["outn"], i - 1)
            for g in range(1, HP, 2):
                dve.wait_ge(s["ot"], g + 1)
                if g >= 2:
                    dve.wait_ge(s["y"], g - 1)
                dve.tensor_copy(ot[:, 1, :], k.bank[1][:]).then_inc(s["ot_dve"], 1)
            dve.wait_ge(s["y"], HP)
            dve.tensor_tensor(k.x[:], k.x[:], k.bank[7][:], ALU.add).then_inc(s["done"], 1)


def capped_ffn(k, tag):
    nc = k.nc
    G, N = 4, E1 // 2 + 1
    which = int(tag) // 7
    s = k.semaphores("ffn1", NORM + ROUTE + ["dve", "g", "u", "cw", "tanh", "g_read", "u_read", "act", "down", "done"])
    w = lambda name: k.w(G, name)
    with ExitStack() as ctx:
        def sb(name, shape, dt=F32):
            return ctx.enter_context(nc.sbuf_tensor(f"ffn1_{name}{tag}", shape, dt))
        buf = route_buffers(sb, E1, E1, k.base[:, which, :])
        th, p1, a = sb("th", [P, 2, T]), sb("p1", [P, 2, T]), sb("a", [P, 2, T])
        block = ctx.enter_context(nc.Block(no_gpsimd_drain=True))

        @block.sync
        def _(sp):
            k.zero_stale(sp, s)

        @block.tensor
        def _(pe):
            pe.wait_ge(k.loaded, 32)
            pe.wait_ge(k.w_loaded[G], 16)
            norm_tensor(k, pe, s)

            def up(n):
                rows = 64 if n == 0 else P
                names = ("sg", "su") if n == 0 else (f"g{n - 1}", f"u{n - 1}")
                for m, (name, sem) in enumerate(zip(names, ("g", "u"))):
                    if n >= 2:
                        pe.wait_ge(s[sem + "_read"], n - 1)
                    pe.matmul(k.bank[2 * m + n % 2][0:rows, :], w(name), k.xn[:], start=True, stop=True) \
                        .then_inc(s[sem], 1)

            def spread_weights(n):
                if n >= 2:
                    pe.wait_ge(s["act"], n)
                pe.matmul(k.bank[4][:], k.h("sel1")[0:3 * E1, (n - 1) * P:n * P], buf["rows"][0:3 * E1, :],
                          start=True, stop=True).then_inc(s["cw"], 1)

            def down(n):
                pe.wait_ge(s["act"], n + 1)
                rows = 64 if n == 0 else P
                pe.matmul(k.bank[5][:], w("sd" if n == 0 else f"d{n - 1}")[0:rows, :], a[0:rows, n % 2, :],
                          start=(n == 0), stop=(n == N - 1)).then_inc(s["down"], 1)

            up(0)
            up(1)
            route_tensor(k, pe, s, G, E1, None, buf["split"], buf["mask"], None)
            down(0)
            pe.wait_ge(s["r_rows"], 1)
            spread_weights(1)
            for n in range(2, N):
                up(n)
                down(n - 1)
                spread_weights(n)
            down(N - 1)

        @block.scalar
        def _(act):
            act.wait_ge(k.loaded, 32)
            norm_scalar(k, act, s)
            for n in range(N):
                rows = 64 if n == 0 else P
                act.wait_ge(s["g"], n + 1)
                if n >= 2:
                    act.wait_ge(s["g_read"], n - 1)
                act.activation(th[0:rows, n % 2, :], k.bank[n % 2][0:rows, :], ACT.Tanh, scale=0.5) \
                    .then_inc(s["tanh"], 1)
                if n == 0:
                    act.wait_ge(s["r_diff"], 1)
                    act.activation(buf["exp"][:], buf["diff"][:], ACT.Exp).then_inc(s["r_exp"], 1)

        @block.vector
        def _(dve):
            link = chained(dve, s["dve"])
            dve.wait_ge(k.loaded, 32)
            norm_vector(k, dve, s)
            route_vector(k, dve, s, link, buf, E1, K1, None, "seg1", True)
            for n in range(N):
                rows = slice(0, 64 if n == 0 else P)
                i = n % 2
                dve.wait_ge(s["tanh"], n + 1)
                dve.scalar_tensor_tensor(p1[rows, i, :], th[rows, i, :], 1.0, k.bank[i][rows, :], ALU.add, ALU.mult) \
                    .then_inc(s["g_read"], 1)
                dve.wait_ge(s["g_read"], n + 1)
                dve.wait_ge(s["u"], n + 1)
                dve.tensor_tensor(p1[rows, i, :], p1[rows, i, :], k.bank[2 + i][rows, :], ALU.mult) \
                    .then_inc(s["u_read"], 1)
                dve.wait_ge(s["u_read"], n + 1)
                if n >= 2:
                    dve.wait_ge(s["down"], n - 1)
                if n == 0:
                    dve.tensor_scalar(a[rows, i, :], p1[rows, i, :], 0.5, None, ALU.mult).then_inc(s["act"], 1)
                else:
                    dve.wait_ge(s["cw"], n)
                    dve.tensor_tensor(a[:, i, :], p1[:, i, :], k.bank[4][:], ALU.mult).then_inc(s["act"], 1)
            dve.wait_ge(s["down"], N)
            dve.tensor_tensor(k.x[:], k.x[:], k.bank[5][:], ALU.add).then_inc(s["done"], 1)


def state_space(k, tag):
    nc = k.nc
    G, NP, HG = 5, 64, 3
    s = k.semaphores("ssm", NORM + ["up", "left", "right", "tanh_r", "conv", "tanh_c", "x", "proj", "z", "e", "ln",
                                    "split", "packed", "bc", "cc", "a", "da", "dbx", "h", "hc", "red", "gated", "down",
                                    "dve", "acts", "done"])
    w = lambda name: k.w(G, name)
    with ExitStack() as ctx:
        def sb(name, shape, dt=F32):
            return ctx.enter_context(nc.sbuf_tensor(f"ssm_{name}{tag}", shape, dt))
        left = sb("left", [P, NB, L + 2])
        right, gate = sb("right", [P, T]), sb("gate", [P, T])
        conv, tc, xs = sb("conv", [P, T]), sb("tc", [P, T]), sb("xs", [P, T])
        z, e, ln = sb("z", [P, T]), sb("e", [P, T]), sb("ln", [P, T])
        u, fix, delta, dx = sb("u", [P, T]), sb("fix", [P, T]), sb("delta", [P, T]), sb("dx", [P, T])
        parts = sb("parts", [P, 2, 3, T], BF16)
        packed = sb("packed", [P, 2, 4, T], BF16)
        bm, cm = sb("bm", [P, T]), sb("cm", [P, T])
        da, dbx = sb("da", [P, 2, T]), sb("dbx", [P, T])
        h, hc = sb("h", [P, 3, T]), sb("hc", [P, 3, T])
        block = ctx.enter_context(nc.Block(no_gpsimd_drain=True))
        two = lambda ap: ap.rearrange("p (b t) -> p b t", b=NB)

        def spot(p):
            return p // 16, p % 16

        @block.sync
        def _(sp):
            k.zero_stale(sp, s)
            for which in range(2):
                for part in range(3):
                    sp.wait_ge(s["split"], 3 * which + part + 1)
                    for g in range(4):
                        sp.dma_start(packed[32 * part:32 * part + 32, which, g, :],
                                     parts[32 * g:32 * g + 32, which, part, :]).then_inc(s["packed"], 16)

        @block.tensor
        def _(pe):
            pe.wait_ge(k.loaded, 32)
            pe.wait_ge(k.w_loaded[G], 16)
            norm_tensor(k, pe, s)
            pe.matmul(k.bank[0][:], w("left"), k.xn[:], start=True, stop=True).then_inc(s["up"], 1)
            pe.matmul(k.bank[1][:], w("right"), k.xn[:], start=True, stop=True).then_inc(s["up"], 1)
            pe.wait_ge(s["x"], 1)
            for n, name in enumerate(("delta", "wb", "wc")):
                pe.matmul(k.bank[2 + n][:], w(name), xs[:], start=True, stop=True).then_inc(s["proj"], 1)
            pe.wait_ge(s["cc"], 2)
            pe.wait_ge(s["packed"], 16 * 24)

            def spread_rows(p):
                g, c = spot(p)
                if p >= 2:
                    pe.wait_ge(s["da"], p - 1)
                    pe.wait_ge(s["dbx"], p - 1)
                pick = k.h("pick")[0:96, c * P:(c + 1) * P]
                pe.matmul(k.bank[p % 2][:], pick, packed[0:96, 0, g, :], start=True, stop=True).then_inc(s["bc"], 1)
                pe.matmul(k.bank[2 + p % 2][:], pick, packed[0:96, 1, g, :], start=True, stop=True) \
                    .then_inc(s["bc"], 1)

            def reduce(p):
                g, c = spot(p)
                pe.wait_ge(s["hc"], p + 1)
                row = 32 * g + c
                pe.matmul(k.bank[5][:], k.c("hot")[:, P - row:2 * P - row], hc[:, p % 3, :],
                          start=(p == 0), stop=(p == NP - 1)).then_inc(s["red"], 1)

            for p in range(NP + 3):
                if p < NP:
                    spread_rows(p)
                if p >= 3:
                    reduce(p - 3)
            pe.wait_ge(s["gated"], 1)
            pe.matmul(k.bank[6][:], w("down"), conv[:], start=True, stop=True).then_inc(s["down"], 1)

        @block.scalar
        def _(act):
            link = chained(act, s["acts"])
            act.wait_ge(k.loaded, 32)
            act.wait_ge(k.w_loaded[G], 16)
            act.activation(k.a_neg[:], w("a_log"), ACT.Exp).then_inc(s["a"], 1)
            norm_scalar(k, act, s)
            act.wait_ge(s["up"], 1)
            act.activation(left[:, :, 2:L + 2], two(k.bank[0]), ACT.Identity, bias=w("b_left")).then_inc(s["left"], 1)
            act.wait_ge(s["up"], 2)
            act.activation(right[:], k.bank[1][:], ACT.Identity, bias=w("b_right")).then_inc(s["right"], 1)
            act.wait_ge(s["right"], 1)
            act.activation(gate[:], right[:], ACT.Tanh, scale=0.5).then_inc(s["tanh_r"], 1)
            act.wait_ge(s["conv"], 1)
            act.activation(tc[:], conv[:], ACT.Tanh, scale=0.5).then_inc(s["tanh_c"], 1)
            act.wait_ge(s["proj"], 1)
            act.activation(z[:], k.bank[2][:], ACT.Identity, bias=w("b_delta")).then_inc(s["z"], 1)
            act.wait_ge(s["z"], 1)
            link(act.activation(e[:], z[:], ACT.Abs))
            act.activation(e[:], e[:], ACT.Exp, scale=-1.0).then_inc(s["e"], 1)
            act.wait_ge(s["proj"], 2)
            act.activation(bm[:], k.bank[3][:], ACT.Identity, bias=w("b_b")).then_inc(s["cc"], 1)
            act.wait_ge(s["proj"], 3)
            act.activation(cm[:], k.bank[4][:], ACT.Identity, bias=w("b_c")).then_inc(s["cc"], 1)
            act.wait_ge(s["e"], 2)
            act.activation(ln[:], u[:], ACT.Ln).then_inc(s["ln"], 1)
            act.wait_ge(s["a"], 2)
            for p in range(NP):
                act.wait_ge(s["bc"], 2 * p + 1)
                if p >= 2:
                    act.wait_ge(s["h"], p - 1)
                act.activation(da[:, p % 2, :], k.bank[p % 2][:], ACT.Exp, scale=k.a_neg[:, p:p + 1]) \
                    .then_inc(s["da"], 1)

        @block.gpsimd
        def _(pool):
            pool.wait_ge(s["cc"], 2)
            for p in range(NP):
                pool.wait_ge(s["h"], p + 1)
                if p >= 3:
                    pool.wait_ge(s["red"], p - 2)
                pool.tensor_tensor(hc[:, p % 3, :], h[:, p % 3, :], cm[:], ALU.mult).then_inc(s["hc"], 1)

        @block.vector
        def _(dve):
            link = chained(dve, s["dve"])
            dve.wait_ge(k.loaded, 32)
            dve.wait_ge(k.w_loaded[G], 16)
            norm_vector(k, dve, s)
            dve.wait_ge(s["a"], 1)
            dve.tensor_scalar(k.a_neg[:], k.a_neg[:], -1.0, None, ALU.mult).then_inc(s["a"], 1)
            link(dve.memset(left[:, :, 0:2], 0.0))
            dve.wait_ge(s["left"], 1)
            taps = w("conv_w")
            link(dve.tensor_scalar(two(conv[:]), left[:, :, 0:L], taps[:, 0:1], w("conv_b"), ALU.mult, ALU.add))
            link(dve.scalar_tensor_tensor(two(conv[:]), left[:, :, 1:L + 1], taps[:, 1:2], two(conv[:]),
                                          ALU.mult, ALU.add))
            dve.scalar_tensor_tensor(two(conv[:]), left[:, :, 2:L + 2], taps[:, 2:3], two(conv[:]),
                                     ALU.mult, ALU.add).then_inc(s["conv"], 1)
            dve.wait_ge(s["tanh_c"], 1)
            link(dve.scalar_tensor_tensor(xs[:], tc[:], 1.0, conv[:], ALU.add, ALU.mult))
            dve.tensor_scalar(xs[:], xs[:], 0.5, None, ALU.mult).then_inc(s["x"], 1)
            dve.wait_ge(s["x"], 1)
            dve.wait_ge(s["tanh_r"], 1)
            link(dve.scalar_tensor_tensor(gate[:], gate[:], 1.0, right[:], ALU.add, ALU.mult))
            dve.wait_ge(s["e"], 1)
            dve.tensor_scalar(u[:], e[:], 1.0, None, ALU.add).then_inc(s["e"], 1)
            dve.wait_ge(s["e"], 2)
            link(dve.scalar_tensor_tensor(fix[:], u[:], 1.0, e[:], ALU.subtract, ALU.subtract))
            dve.wait_ge(s["ln"], 1)
            link(dve.tensor_tensor(ln[:], ln[:], fix[:], ALU.subtract))
            link(dve.scalar_tensor_tensor(delta[:], z[:], 0.0, ln[:], ALU.max, ALU.add))
            link(dve.tensor_tensor(dx[:], delta[:], xs[:], ALU.mult))
            for which, v in enumerate((delta, dx)):
                dve.tensor_copy(parts[:, which, 0, :], v[:]).then_inc(s["split"], 1)
                dve.wait_ge(s["split"], 3 * which + 1)
                link(dve.tensor_tensor(fix[:], v[:], parts[:, which, 0, :], ALU.subtract))
                dve.tensor_copy(parts[:, which, 1, :], fix[:]).then_inc(s["split"], 1)
                dve.wait_ge(s["split"], 3 * which + 2)
                link(dve.tensor_tensor(fix[:], fix[:], parts[:, which, 1, :], ALU.subtract))
                dve.tensor_copy(parts[:, which, 2, :], fix[:]).then_inc(s["split"], 1)
                dve.wait_ge(s["split"], 3 * which + 3)
            dve.wait_ge(s["cc"], 1)
            for p in range(NP):
                dve.wait_ge(s["bc"], 2 * p + 2)
                if p >= 1:
                    dve.wait_ge(s["h"], p)
                dve.tensor_tensor(dbx[:], k.bank[2 + p % 2][:], bm[:], ALU.mult).then_inc(s["dbx"], 1)
                dve.wait_ge(s["dbx"], p + 1)
                dve.wait_ge(s["da"], p + 1)
                if p >= 3:
                    dve.wait_ge(s["hc"], p - 2)
                for b in range(NB):
                    cols = slice(b * L, (b + 1) * L)
                    ins = dve.tensor_tensor_scan(h[:, p % 3, cols], da[:, p % 2, cols], dbx[:, cols], 0.0,
                                                 ALU.mult, ALU.add)
                ins.then_inc(s["h"], 1)
            dve.wait_ge(s["red"], NP)
            link(dve.scalar_tensor_tensor(fix[:], xs[:], w("skip"), k.bank[5][:], ALU.mult, ALU.add))
            dve.scalar_tensor_tensor(conv[:], fix[:], 0.5, gate[:], ALU.mult, ALU.mult).then_inc(s["gated"], 1)
            dve.wait_ge(s["down"], 1)
            dve.scalar_tensor_tensor(k.x[:], k.bank[6][:], w("b_down"), k.x[:], ALU.add, ALU.add) \
                .then_inc(s["done"], 1)
def hybrid_kernel(nc, x_in, const_in, half_in, weights_in, x_out):
    with ExitStack() as ctx:
        k = Core(nc, ctx)
        a_log_at = k.group_at[5][0]["a_log"][0]
        with nc.Block(no_gpsimd_drain=True) as block:
            @block.sync
            def _(sp):
                sp.dma_start(k.const[:], const_in).then_inc(k.loaded, 16)
                sp.dma_start(k.half[:], half_in).then_inc(k.loaded, 16)
                for g in range(6):
                    if g <= LAST_GROUP:
                        sp.dma_start(k.weights[g][:], weights_in[g]).then_inc(k.w_loaded[g], 16)

            @block.vector
            def _(dve):
                dve.memset(k.base[:], 0.0)
                dve.memset(k.vm[:], 0.0).then_inc(k.once, 1)
        k.stale = k.semaphores("out", OUT_SEMAPHORES)
        with nc.Fori(0, x_in.shape[0]) as it:
            load_tokens(k, it, x_in, "")
            for n, layer in enumerate(PLAN[:LAYERS]):
                layer(k, n)
            store_tokens(k, it, x_out, "")


PLAN = [lambda k, n: narrow_attention(k, n, True), lambda k, n: biased_ffn(k, n),
        lambda k, n: wide_attention(k, n), lambda k, n: biased_ffn(k, n),
        lambda k, n: narrow_attention(k, n, False), lambda k, n: capped_ffn(k, n),
        lambda k, n: state_space(k, n), lambda k, n: capped_ffn(k, n)]
LAST_GROUP = 5


def kernel(**inputs):
    import numpy as np
    import concourse.bacc as bacc
    from concourse.bass_utils import run_bass_kernel_spmd

    const_at, half_at, group_at = tables()
    v = {name: np.ascontiguousarray(a) for name, a in inputs.items()}
    f32 = np.dtype("float32")

    const = np.zeros((P, const_at[1]), f32)
    half = np.zeros((P, half_at[1]), f32)

    def put(packed, where, name, a, rows=slice(0, P)):
        at, width = where[name]
        packed[rows, at:at + width] = a

    idx = np.arange(P)
    tri = (idx[:, None] <= idx[None, :])
    ones = np.ones((P, P), f32)
    put(const, const_at[0], "mean", ones / P)
    put(const, const_at[0], "ident", np.eye(P))
    put(const, const_at[0], "tri", np.concatenate([tri, ones, tri], 1))
    hide = np.where(tri.T, 0.0, BIG)
    put(const, const_at[0], "trib", np.concatenate([hide, hide * 0, hide], 1))
    pair = (idx % DA) % (DA // 2)
    theta = (1.0 / np.float32(10000.0) ** (np.arange(0, DA, 2, dtype=f32) / np.float32(DA))).astype(f32)
    angle = (np.arange(L, dtype=f32)[None, :] * theta[pair][:, None]).astype(f32)
    sign = np.where(idx % DA < DA // 2, -1.0, 1.0)[:, None]
    scale = -1.0 / np.sqrt(np.float64(DA))
    cos, sin = np.cos(angle.astype(np.float64)), np.sin(angle.astype(np.float64)) * sign
    put(const, const_at[0], "cosq", cos * scale)
    put(const, const_at[0], "sinq", sin * scale)
    put(const, const_at[0], "cosk", cos)
    put(const, const_at[0], "sink", sin)
    hot = np.zeros((P, 2 * P), f32)
    hot[:64, P] = 1.0
    hot[64:, P + 16] = 1.0
    put(const, const_at[0], "hot", hot)
    put(const, const_at[0], "rows", (idx[:, None] // DA % 4 == np.arange(4)[None, :]))
    put(const, const_at[0], "eps", 1e-5)
    put(const, const_at[0], "ones", 1.0)
    put(const, const_at[0], "heads", (idx[:, None] // DA == np.arange(H)[None, :]))
    put(const, const_at[0], "seg0", np.tile(np.arange(E0) != 0, NT)[None, :])
    put(const, const_at[0], "seg1", np.tile(np.arange(E1) != 0, NT)[None, :])
    for e in range(E0 + 1):
        sel = np.zeros((P, P), f32)
        sel[[e, E0 + 1 + e, 2 * (E0 + 1) + e], :] = 0.5
        at = half_at[0]["sel0"][0] + e * P
        half[:, at:at + P] = sel
    for p in range(E1 // 2):
        sel = np.zeros((P, P), f32)
        for part in range(3):
            sel[part * E1 + 2 * p, :64] = 0.5
            sel[part * E1 + 2 * p + 1, 64:] = 0.5
        at = half_at[0]["sel1"][0] + p * P
        half[:, at:at + P] = sel
    for c in range(16):
        sel = np.zeros((P, P), f32)
        for part in range(3):
            sel[part * 32 + c, :64] = 1.0
            sel[part * 32 + 16 + c, 64:] = 1.0
        at = half_at[0]["pick"][0] + c * P
        half[:, at:at + P] = sel
    put(half, half_at[0], "lower", tri)
    put(half, half_at[0], "ones", 1.0)
    put(half, half_at[0], "identb", np.eye(P))
    half = half.astype(np.dtype("bfloat16"))

    packs = [np.zeros((P, width), f32) for _, width in group_at]

    def lay(g, name, a):
        at, width = group_at[g][0][name]
        packs[g][:a.shape[0], at:at + width] = a

    for name, key in (("wq", "Wq"), ("wk", "Wk"), ("wv", "Wv"), ("wo", "Wo")):
        lay(0, name, v[f"L0_attn_a_{key}"].T)
    lay(1, "gate", v["L0_ffn_gate_w"].T)
    lay(1, "gate_b", np.broadcast_to(v["L0_ffn_gate_b"], (P, E0)))
    lay(1, "b2", np.concatenate([v["L0_ffn_b2"], v["L0_ffn_sb2"][None]], 0))
    w1 = np.concatenate([v["L0_ffn_w1"], v["L0_ffn_sw1"][None]], 0)
    w3 = np.concatenate([v["L0_ffn_w3"], v["L0_ffn_sw3"][None]], 0)
    w2 = np.concatenate([v["L0_ffn_w2"], v["L0_ffn_sw2"][None]], 0)
    b1 = np.concatenate([v["L0_ffn_b1"], v["L0_ffn_sb1"][None]], 0)
    b3 = np.concatenate([v["L0_ffn_b3"], v["L0_ffn_sb3"][None]], 0)
    for name, b in (("b1", b1), ("b3", b3)):
        lay(1, name + "g", b[:, 0::2].T)
        lay(1, name + "l", b[:, 1::2].T)
    for e in range(E0 + 1):
        for name, a in (("w1", w1), ("w3", w3)):
            lay(1, f"{name}g{e}", a[e, 0::2].T)
            lay(1, f"{name}l{e}", a[e, 1::2].T)
        lay(1, f"w2{e}", w2[e].T)
    lay(2, "wqkv", v["L0_attn_b_w_qkv"])
    lay(2, "wout", v["L0_attn_b_w_out"].reshape(8, P, P).transpose(1, 0, 2).reshape(P, 8 * P))
    flip = (idx // DA) * DA + (idx % DA + DA // 2) % DA
    for name, key in (("wq", "W_Q"), ("wk", "W_K"), ("wv", "W_V"), ("wo", "W_O")):
        lay(3, name, v[f"L1_attn_a_{key}"].T)
    lay(3, "wqf", v["L1_attn_a_W_Q"][flip].T)
    lay(3, "wkf", v["L1_attn_a_W_K"][flip].T)
    gu, dn = v["L1_ffn_w_gate_up"], v["L1_ffn_w_down"]
    lay(4, "gate", v["L1_ffn_gate_w"].T)
    lay(4, "sg", v["L1_ffn_shared_w_gate_up"][:, :64])
    lay(4, "su", v["L1_ffn_shared_w_gate_up"][:, 64:])
    lay(4, "sd", v["L1_ffn_shared_w_down"])
    for p in range(E1 // 2):
        lay(4, f"g{p}", np.concatenate([gu[2 * p][:, :64], gu[2 * p + 1][:, :64]], 1))
        lay(4, f"u{p}", np.concatenate([gu[2 * p][:, 64:], gu[2 * p + 1][:, 64:]], 1))
        lay(4, f"d{p}", np.concatenate([dn[2 * p], dn[2 * p + 1]], 0))
    m = {key[len("L1_attn_b_"):]: a for key, a in v.items() if key.startswith("L1_attn_b_")}
    lay(5, "left", m["W_up"][:, :P])
    lay(5, "right", m["W_up"][:, P:])
    lay(5, "delta", m["W_delta"])
    lay(5, "wb", np.concatenate([m["W_B"], m["W_B"]], 1))
    lay(5, "wc", np.concatenate([m["W_C"], m["W_C"]], 1))
    lay(5, "down", m["W_down"])
    lay(5, "b_left", m["b_up"][:P, None])
    lay(5, "b_right", m["b_up"][P:, None])
    lay(5, "conv_w", m["conv_w"])
    lay(5, "conv_b", m["conv_b"][:, None])
    lay(5, "b_delta", m["b_delta"][:, None])
    lay(5, "b_b", np.concatenate([m["b_B"], m["b_B"]], 0)[:, None])
    lay(5, "b_c", np.concatenate([m["b_C"], m["b_C"]], 0)[:, None])
    lay(5, "skip", m["D_skip"][:, None])
    lay(5, "b_down", m["b_down"][:, None])
    lay(5, "a_log", m["A_log"].reshape(4, 2, 16, 64).transpose(1, 3, 0, 2).reshape(P, 64))

    x = v["L0_attn_a_x"]
    passes = x.shape[0] // NB
    arrays = {"x": x.reshape(passes, T, P), "const": const, "half": half}
    arrays.update({f"weights_{g}": a for g, a in enumerate(packs)})
    nc = bacc.Bacc("TRN2", target_bir_lowering=False, num_devices=1)
    ap = {name: nc.dram_tensor(f"in_{name}", a.shape, mybir.dt.from_np(a.dtype), kind="ExternalInput").ap()
          for name, a in arrays.items()}
    out = nc.dram_tensor("out", (passes, T, P), F32, kind="ExternalOutput").ap()
    hybrid_kernel(nc, ap["x"], ap["const"], ap["half"], [ap[f"weights_{g}"] for g in range(6)], out)
    got = run_bass_kernel_spmd(nc, [{f"in_{name}": a for name, a in arrays.items()}], core_ids=[0])
    return got.results[0]["out"].reshape(x.shape)
```

```python
from contextlib import ExitStack

import concourse.bass as bass
from concourse import mybir

LAYERS = 8

ALU = mybir.AluOpType
ACT = mybir.ActivationFunctionType
AX_X = mybir.AxisListType.X
F32 = mybir.dt.float32
BF16 = mybir.dt.bfloat16

P = 128
T = 512
NT = T // P
L = 256
NB = T // L
H = 16
DA = 8
DB = 64
E0, K0 = 8, 2
E1, K1 = 32, 4
CAP = 128
ALPHA, LIMIT = 1.702, 7.0
BIG = 1e30


def layout(parts):
    at, where = 0, {}
    for name, width in parts:
        where[name] = (at, width)
        at += width
    return where, at


def tables():
    const = layout([("mean", P), ("ident", P), ("tri", 3 * P), ("trib", 3 * P), ("cosq", L), ("sinq", L),
                    ("cosk", L), ("sink", L), ("ones", L), ("heads", H), ("hot", 2 * P), ("rows", 4), ("eps", 1),
                    ("seg0", NT * E0), ("seg1", NT * E1)])
    half = layout([("sel0", (E0 + 1) * P), ("sel1", (E1 // 2) * P), ("pick", 16 * P), ("lower", P), ("ones", P),
                   ("identb", P)])
    groups = [
        layout([("wq", P), ("wk", P), ("wv", P), ("wo", P)]),
        layout([("gate", E0), ("gate_b", E0), ("b1g", 9), ("b1l", 9), ("b3g", 9), ("b3l", 9), ("b2", P)]
               + [(f"{w}{e}", P) for e in range(E0 + 1) for w in ("w1g", "w3g", "w1l", "w3l", "w2")]),
        layout([("wqkv", 3 * H * DB), ("wout", H * DB)]),
        layout([("wq", P), ("wqf", P), ("wk", P), ("wkf", P), ("wv", P), ("wo", P)]),
        layout([("gate", E1), ("sg", 64), ("su", 64), ("sd", P)]
               + [(f"{w}{p}", P) for p in range(E1 // 2) for w in ("g", "u", "d")]),
        layout([("left", P), ("right", P), ("delta", P), ("wb", P), ("wc", P), ("down", P), ("b_left", 1),
                ("b_right", 1), ("conv_w", 3), ("conv_b", 1), ("b_delta", 1), ("b_b", 1), ("b_c", 1),
                ("skip", 1), ("b_down", 1), ("a_log", 64)]),
    ]
    return const, half, groups


class Core:

    def __init__(self, nc, ctx):
        self.nc, self.ctx = nc, ctx
        self.const_at, self.half_at, self.group_at = tables()
        sb = self.sb
        self.const = sb("const", [P, self.const_at[1]])
        self.half = sb("half", [P, self.half_at[1]], BF16)
        self.weights = [sb(f"weights{g}", [P, width]) for g, (_, width) in enumerate(self.group_at)]
        self.x = sb("x_resid", [P, T])
        self.xn = sb("x_norm", [P, T])
        self.cent = sb("x_centred", [P, T])
        self.sq = sb("x_square", [P, T])
        self.a_neg = sb("a_neg", [P, 64])
        self.base = sb("base", [P, 2, E1])
        self.banks = ctx.enter_context(nc.psum_tensor("banks", [P, 8, 512], F32))
        self.vm = sb("v_by_head", [P, NT, H * (P + DA)])
        self.bank = [self.banks[:, i, :] for i in range(8)]
        self.tok_in, self.tok_out = sb("tok_in", [P, NT, P]), sb("tok_out", [P, NT, P])
        self.tokens = ctx.enter_context(nc.semaphore("tokens"))
        self.half_loaded = ctx.enter_context(nc.semaphore("half_loaded"))
        self.loaded = ctx.enter_context(nc.semaphore("loaded"))
        self.w_loaded = [ctx.enter_context(nc.semaphore(f"w_loaded{g}")) for g in range(6)]
        self.once = ctx.enter_context(nc.semaphore("once"))
        self.sets = {}
        self.stale = None

    def sb(self, name, shape, dt=F32):
        return self.ctx.enter_context(self.nc.sbuf_tensor(name, shape, dt))

    def c(self, name):
        at, width = self.const_at[0][name]
        return self.const[:, at:at + width]

    def h(self, name):
        at, width = self.half_at[0][name]
        return self.half[:, at:at + width]

    def w(self, g, name):
        at, width = self.group_at[g][0][name]
        return self.weights[g][:, at:at + width]

    def semaphores(self, layer, names):
        if layer not in self.sets:
            self.sets[layer] = {n: self.ctx.enter_context(self.nc.semaphore(f"{layer}_{n}")) for n in names}
        return self.sets[layer]

    def zero_stale(self, engine, mine):
        if self.stale is not None and self.stale is not mine:
            nums = [s.num for s in self.stale.values()]
            engine.sem_clear(range(min(nums), max(nums) + 1))
        self.stale = mine


def chained(engine, sem):
    count = [0]

    def link(ins):
        count[0] += 1
        ins.then_inc(sem, 1)
        engine.wait_ge(sem, count[0])
    return link


def spread(ap, shape, axis):
    return ap.unsqueeze(axis).broadcast_to(shape)


TURN = ["turned", "turned_in", "copied", "copied_in", "stored"]
NORM = ["n_mean", "n_cent", "n_sq", "n_var", "n_ln", "n_rstd", "n_out"]


def halves():
    return [slice(b * L, (b + 1) * L) for b in range(NB)]


def norm_tensor(k, pe, s):
    for n, cols in enumerate(halves()):
        pe.matmul(k.bank[6 + n][:, 0:L], k.c("mean"), k.x[:, cols], start=True, stop=True).then_inc(s["n_mean"], 1)
    for n, cols in enumerate(halves()):
        pe.wait_ge(s["n_sq"], n + 1)
        pe.matmul(k.bank[6 + n][:, L:2 * L], k.c("mean"), k.sq[:, cols], start=True, stop=True).then_inc(s["n_var"], 1)
    pe.wait_ge(s["n_out"], NB)


def norm_scalar(k, act, s, then):
    act.preload_act_table_set("natural_log_exp_and_others")
    for n, cols in enumerate(halves()):
        act.wait_ge(s["n_cent"], n + 1)
        act.activation(k.sq[:, cols], k.cent[:, cols], ACT.Square).then_inc(s["n_sq"], 1)
    for n, cols in enumerate(halves()):
        act.wait_ge(s["n_var"], n + 1)
        act.activation(k.sq[:, cols], k.bank[6 + n][:, L:2 * L], ACT.Ln, bias=k.c("eps")).then_inc(s["n_ln"], 1)
        act.wait_ge(s["n_ln"], n + 1)
        act.activation(k.sq[:, cols], k.sq[:, cols], ACT.Exp, scale=-0.5).then_inc(s["n_rstd"], 1)
    if then is not None:
        act.preload_act_table_set(then)


def norm_vector(k, dve, s):
    for n, cols in enumerate(halves()):
        dve.wait_ge(s["n_mean"], n + 1)
        dve.tensor_tensor(k.cent[:, cols], k.x[:, cols], k.bank[6 + n][:, 0:L], ALU.subtract).then_inc(s["n_cent"], 1)
    for n, cols in enumerate(halves()):
        dve.wait_ge(s["n_rstd"], n + 1)
        dve.tensor_tensor(k.xn[:, cols], k.cent[:, cols], k.sq[:, cols], ALU.mult).then_inc(s["n_out"], 1)
    dve.wait_ge(s["n_out"], NB)


def turn_tokens(k, x_out, it, tag):
    nc = k.nc
    s = k.semaphores("turn", TURN)
    with nc.Block(no_gpsimd_drain=True) as block:
        @block.sync
        def _(sp):
            k.zero_stale(sp, s)
            if it is not None:
                sp.wait_ge(s["copied"], 1)
                sp.dma_start(x_out[bass.ds(it, 1)].rearrange("o (j p) d -> p (o j) d", p=P), k.tok_out[:]) \
                    .then_inc(s["stored"], 16)
            else:
                sp.sem_inc(s["stored"], 16)

        @block.tensor
        def _(pe):
            pe.wait_ge(k.loaded, 16)
            if it is not None:
                for j in range(NT):
                    ins = pe.transpose(k.bank[0][:, j * P:(j + 1) * P], k.x[:, j * P:(j + 1) * P], k.c("ident"))
                ins.then_inc(s["turned"], 1)
            pe.wait_ge(k.tokens, 16)
            for j in range(NT):
                ins = pe.transpose(k.bank[1][:, j * P:(j + 1) * P], k.tok_in[:, j, :], k.c("ident"))
            ins.then_inc(s["turned_in"], 1)

        @block.vector
        def _(dve):
            if it is not None:
                dve.wait_ge(s["turned"], 1)
                dve.tensor_copy(k.tok_out[:].rearrange("p j d -> p (j d)"), k.bank[0][:]).then_inc(s["copied"], 1)
            dve.wait_ge(s["turned_in"], 1)
            dve.tensor_copy(k.x[:], k.bank[1][:]).then_inc(s["copied_in"], 1)


def narrow_attention(k, tag, linear, x_in=None, it=None):
    nc = k.nc
    G = 0 if linear else 3
    layer = "lin" if linear else "rot"
    passes = x_in.shape[0] if linear else None
    s = k.semaphores("narrow", NORM + ["proj", "low", "high", "qk", "vcopy", "dve", "scores", "probs_in", "probs",
                                       "turned", "pt", "pv", "sums", "prod", "wide", "wide_t", "ot", "y", "done"])
    w = lambda name: k.w(G, name)
    stages = [(b, c, jj) for b in range(NB) for c in range(4) for jj in range(2)]
    NS = len(stages)
    by_head = k.vm[:, :, 0:H * (P + DA)].rearrange("p t (h x) -> p t h x", x=P + DA)[:, :, :, 0:DA]
    with ExitStack() as ctx:
        def sb(name, shape, dt=F32):
            return ctx.enter_context(nc.sbuf_tensor(f"{layer}_{name}{tag}", shape, dt))
        q, kk = sb("q", [P, T]), sb("k", [P, T])
        km = sb("km", [P, 4, T])
        t1, t2 = sb("t1", [P, T]), sb("t2", [P, T])
        pin = sb("pin", [P, 2, 2, 3 * P])
        pt = sb("pt", [P, 2, 2, 3 * P])
        low = sb("low", [P, 2, 4])
        den = sb("den", [P, NT, H])
        wide = sb("wide", [P, NT, H, DA])
        ot = sb("ot", [P, T])
        block = ctx.enter_context(nc.Block(no_gpsimd_drain=True))

        @block.sync
        def _(sp):
            if linear:
                if it is not None:
                    sp.wait_ge(k.stale["stored"], 16)
                k.zero_stale(sp, s)
                sp.sem_clear(k.tokens)
                sp.dma_start(k.tok_in[:], x_in[bass.ds((it + 1) % passes, 1)].rearrange("o (j p) d -> p (o j) d", p=P)) \
                    .then_inc(k.tokens, 16)
            else:
                k.zero_stale(sp, s)

        @block.tensor
        def _(pe):
            pe.wait_ge(k.loaded, 16)
            pe.wait_ge(k.w_loaded[G], 16)
            norm_tensor(k, pe, s)
            names = ["wq", "wk"] if linear else ["wq", "wqf", "wk", "wkf"]
            for n, name in enumerate(names):
                pe.matmul(k.bank[n][:], w(name), k.xn[:], start=True, stop=True).then_inc(s["proj"], 1)
            for j in range(NT):
                ins = pe.matmul(k.bank[4][:, j * P:(j + 1) * P], k.xn[:, j * P:(j + 1) * P], w("wv"),
                                start=True, stop=True)
            ins.then_inc(s["proj"], 1)

            def scores(i):
                b, c, jj = stages[i]
                if i >= 2:
                    pe.wait_ge(s["probs" if linear else "probs_in"], i - 1)
                for m in range(2):
                    j = 2 * jj + m
                    r = slice(32 * j, 32 * j + 32)
                    t0, o = b * L, k.bank[2 * (i % 2) + m]
                    if linear:
                        pe.matmul(o[:, 0:L], km[r, c, t0:t0 + P], q[r, t0:t0 + L], start=True, stop=True)
                        ins = pe.matmul(o[:, L:L + P], km[r, c, t0 + P:t0 + L], q[r, t0 + P:t0 + L],
                                        start=True, stop=True)
                    else:
                        pe.matmul(o[:, 0:P], q[r, t0:t0 + P], km[r, c, t0:t0 + P], start=True, stop=True)
                        ins = pe.matmul(o[:, P:P + L], q[r, t0 + P:t0 + L], km[r, c, t0:t0 + L],
                                        start=True, stop=True)
                ins.then_inc(s["scores"], 1)

            def turn(i):
                pe.wait_ge(s["probs"], i + 1)
                if i >= 1:
                    pe.wait_ge(s["pt"], i)
                for m in range(2):
                    for n in range(3):
                        ins = pe.transpose(k.bank[4 + m][:, n * P:(n + 1) * P],
                                           pin[:, i % 2, m, n * P:(n + 1) * P], k.c("ident"))
                ins.then_inc(s["turned"], 1)

            def weigh(i):
                b, c, jj = stages[i]
                pe.wait_ge(s["probs" if linear else "pt"], i + 1)
                for m in range(2):
                    head = 4 * (2 * jj + m) + c
                    p, first, last = pt[:, i % 2, m, :], c == jj == m == 0, head == 4 * 3 + 3
                    v = lambda tile: k.vm[:, tile, head * P:(head + 1) * P]
                    pe.matmul(k.bank[6][:, b * L:(b + 1) * L], v(2 * b), p[:, 0:L], start=first, stop=False,
                              skip_group_check=True)
                    ins = pe.matmul(k.bank[6][:, b * L + P:(b + 1) * L], v(2 * b + 1), p[:, L:L + P],
                                    start=False, stop=last, skip_group_check=True)
                ins.then_inc(s["pv"], 1)

            pe.wait_ge(s["qk"], 1)
            pe.wait_ge(s["vcopy"], 1)
            scores(0)
            scores(1)
            if linear:
                for i in range(NS):
                    weigh(i)
                    if i + 2 < NS:
                        scores(i + 2)
                    if i == 1:
                        pe.wait_ge(s["prod"], 1)
                        for j in range(NT):
                            ins = pe.matmul(k.bank[5][:, j * H:(j + 1) * H], t1[:, j * P:(j + 1) * P],
                                            k.c("heads"), start=True, stop=True)
                        ins.then_inc(s["sums"], 1)
            else:
                turn(0)
                for i in range(NS):
                    if i + 2 < NS:
                        scores(i + 2)
                    if i + 1 < NS:
                        turn(i + 1)
                    weigh(i)
            pe.wait_ge(s["wide"], 1)
            for j in range(NT):
                ins = pe.transpose(k.bank[7][:, j * P:(j + 1) * P],
                                   wide[:, j].rearrange("p h e -> p (h e)"), k.c("ident"))
            ins.then_inc(s["wide_t"], 1)
            pe.wait_ge(s["ot"], 1)
            pe.matmul(k.bank[0][:], w("wo"), ot[:], start=True, stop=True).then_inc(s["y"], 1)

        @block.scalar
        def _(act):
            act.wait_ge(k.loaded, 16)
            norm_scalar(k, act, s, None)
            if linear:
                for n, t in enumerate((t1, t2)):
                    act.wait_ge(s["low"], n + 1)
                    act.activation(t[:], t[:], ACT.Exp).then_inc(s["high"], 1)
            act.wait_ge(k.once, 1)
            act.wait_ge(s["proj"], 3 if linear else 5)
            act.activation(by_head, k.bank[4][:].rearrange("p (t h e) -> p t h e", t=NT, h=H),
                           ACT.Copy).then_inc(s["vcopy"], 1)
            if not linear:
                for i in range(NS):
                    b, c, jj = stages[i]
                    act.wait_ge(s["probs_in"], i + 1)
                    for m in range(2):
                        for t, cols in enumerate((slice(0, P), slice(P, 3 * P))):
                            head = 4 * (2 * jj + m) + c
                            ins = act.activation(pin[:, i % 2, m, cols], pin[:, i % 2, m, cols], ACT.Exp,
                                                 bias=low[:, i % 2, 2 * m + t:2 * m + t + 1], scale=-1.0,
                                                 accum_out=den[:, 2 * b + t, head:head + 1])
                    ins.then_inc(s["probs"], 1)
            act.wait_ge(s["wide_t"], 1)
            act.activation(t2[:], k.bank[7][:], ACT.Copy).then_inc(s["wide_t"], 1)

        @block.vector
        def _(dve):
            link = chained(dve, s["dve"])
            dve.wait_ge(k.loaded, 16)
            norm_vector(k, dve, s)
            if linear:
                for n, t in enumerate((t1, t2)):
                    dve.wait_ge(s["proj"], n + 1)
                    dve.tensor_scalar(t[:], k.bank[n][:], 0.0, None, ALU.min).then_inc(s["low"], 1)
                for n, (t, o) in enumerate(((t1, q), (t2, kk))):
                    dve.wait_ge(s["high"], n + 1)
                    link(dve.scalar_tensor_tensor(o[:], k.bank[n][:], 0.0, t[:], ALU.max, ALU.add))
            else:
                rope = [(q, 0, 1, "cosq", "sinq"), (kk, 2, 3, "cosk", "sink")]
                for o, a, f, cos, sin in rope:
                    dve.wait_ge(s["proj"], f + 1)
                    table = lambda name: spread(k.c(name), [P, NB, L], 1)
                    two = lambda ap: ap.rearrange("p (b t) -> p b t", b=NB)
                    link(dve.tensor_tensor(two(t1[:]), two(k.bank[a][:]), table(cos), ALU.mult))
                    link(dve.tensor_tensor(two(t2[:]), two(k.bank[f][:]), table(sin), ALU.mult))
                    link(dve.tensor_tensor(o[:], t1[:], t2[:], ALU.add))
            for c in range(4):
                ins = dve.tensor_scalar(km[:, c, :], kk[:], k.c("rows")[:, c:c + 1], None, ALU.mult)
            ins.then_inc(s["qk"], 1)
            for i in range(NS + 1):
                if i < NS:
                    dve.wait_ge(s["scores"], i + 1)
                    if linear:
                        if i >= 2:
                            dve.wait_ge(s["pv"], i - 1)
                        for m in range(2):
                            ins = dve.tensor_tensor(pt[:, i % 2, m, :], k.bank[2 * (i % 2) + m][:, 0:3 * P],
                                                    k.c("tri"), ALU.mult)
                        ins.then_inc(s["probs"], 1)
                    else:
                        if i >= 2:
                            dve.wait_ge(s["turned"], i - 1)
                        for m in range(2):
                            for t, cols in enumerate((slice(0, P), slice(P, 3 * P))):
                                ins = dve.tensor_tensor_reduce(
                                    pin[:, i % 2, m, cols], k.bank[2 * (i % 2) + m][:, cols],
                                    k.c("trib")[:, cols], 1.0, 3e38, ALU.add, ALU.min,
                                    low[:, i % 2, 2 * m + t:2 * m + t + 1])
                        ins.then_inc(s["probs_in"], 1)
                if linear and i == 0:
                    for b in range(NB):
                        cols = slice(b * L, (b + 1) * L)
                        link(dve.tensor_tensor_scan(t2[:, cols], k.c("ones"), kk[:, cols], 0.0, ALU.mult, ALU.add))
                    dve.tensor_tensor(t1[:], t2[:], q[:], ALU.mult).then_inc(s["prod"], 1)
                if i >= 1 and not linear:
                    dve.wait_ge(s["turned"], i)
                    if i >= 3:
                        dve.wait_ge(s["pv"], i - 2)
                    for m in range(2):
                        ins = dve.tensor_copy(pt[:, (i - 1) % 2, m, :], k.bank[4 + m][:, 0:3 * P])
                    ins.then_inc(s["pt"], 1)
            flat = lambda ap: ap[:].rearrange("p t h -> p (t h)")
            if linear:
                dve.wait_ge(s["sums"], 1)
                link(dve.tensor_scalar(flat(den), k.bank[5][:, 0:NT * H], 1e-6, None, ALU.max))
            else:
                dve.wait_ge(s["probs"], NS)
            link(dve.reciprocal(den[:], den[:]))
            dve.tensor_copy(wide[:], spread(den[:], [P, NT, H, DA], 3)).then_inc(s["wide"], 1)
            dve.wait_ge(s["pv"], NS)
            dve.wait_ge(s["wide_t"], 2)
            dve.tensor_tensor(ot[:], k.bank[6][:], t2[:], ALU.mult).then_inc(s["ot"], 1)
            dve.wait_ge(s["y"], 1)
            dve.tensor_tensor(k.x[:], k.x[:], k.bank[0][:], ALU.add).then_inc(s["done"], 1)


ROUTE = ["logits", "r_diff", "r_exp", "r_split", "r_turned", "r_rows", "r_count", "r_dve"]


def route_logits(k, pe, s, g, experts):
    for j in range(NT):
        ins = pe.matmul(k.bank[6][:, j * experts:(j + 1) * experts], k.xn[:, j * P:(j + 1) * P], k.w(g, "gate"),
                        start=True, stop=True)
    ins.then_inc(s["logits"], 1)


def route_counts(k, pe, s, experts, mask):
    pe.wait_ge(s["r_count"], 1)
    pe.wait_ge(s["r_diff"], 1)
    for j in range(NT + 1):
        out = k.bank[6][:, j * experts:(j + 1) * experts]
        for i in range(min(j, NT)):
            ins = pe.matmul(out, k.h("ones"), mask[:, i, :], start=(i == 0), stop=(i == j - 1 and j == NT))
        if j < NT:
            ins = pe.matmul(out, k.h("lower"), mask[:, j, :], start=(j == 0), stop=True)
    ins.then_inc(s["r_count"], 1)


def route_turn(k, pe, s, split):
    pe.wait_ge(s["r_split"], 1)
    rows = split.shape[2]
    turned = k.bank[7][:].bitcast(BF16)
    for j in range(NT):
        ins = pe.transpose(turned[0:rows, j * P:(j + 1) * P], split[:, j, :], k.h("identb"))
    ins.then_inc(s["r_turned"], 1)


def route_vector(k, dve, s, link, buf, experts, choices, bias, seg, cap, meanwhile):
    E = experts
    logits = k.bank[6][:, 0:NT * E].rearrange("p (j e) -> p j e", e=E)
    full = [P, NT, E]
    dve.wait_ge(s["logits"], 1)
    link(dve.tensor_reduce(buf["top"][:], logits, AX_X, ALU.max))
    dve.tensor_tensor(buf["diff"][:], logits, spread(buf["top"][:], full, 2), ALU.subtract).then_inc(s["r_diff"], 1)
    meanwhile(0)
    dve.wait_ge(s["r_exp"], 1)
    link(dve.tensor_reduce(buf["sum"][:], buf["exp"][:], AX_X, ALU.add))
    link(dve.reciprocal(buf["sum"][:], buf["sum"][:]))
    link(dve.tensor_tensor(buf["score"][:], buf["exp"][:], spread(buf["sum"][:], full, 2), ALU.mult))
    ranked = buf["score"]
    if bias is not None:
        ranked = buf["diff"]
        link(dve.tensor_tensor(ranked[:], buf["score"][:], spread(bias, full, 1), ALU.add))
    for j in range(NT):
        ins = dve.max(buf["best"][:, j, :], ranked[:, j, :])
    link(ins)
    last = spread(buf["best"][:, :, choices - 1], full, 2)
    link(dve.tensor_tensor(buf["over"][:], ranked[:], last, ALU.is_gt))
    link(dve.tensor_reduce(buf["top"][:], buf["over"][:], AX_X, ALU.add))
    link(dve.tensor_scalar(buf["top"][:], buf["top"][:], -1.0, float(choices), ALU.mult, ALU.add))
    link(dve.tensor_tensor(buf["equal"][:], ranked[:], last, ALU.is_equal))
    flat = lambda b: b[:].rearrange("p j e -> p (j e)")
    link(dve.tensor_tensor_scan(flat(buf["rank"]), k.c(seg), flat(buf["equal"]), 0.0, ALU.mult, ALU.add))
    link(dve.tensor_tensor(buf["rank"][:], buf["rank"][:], spread(buf["top"][:], full, 2), ALU.is_le))
    link(dve.tensor_tensor(buf["equal"][:], buf["equal"][:], buf["rank"][:], ALU.mult))
    link(dve.tensor_tensor(buf["over"][:], buf["over"][:], buf["equal"][:], ALU.add))
    cw = buf["cw"][:, :, 0:E]
    link(dve.tensor_tensor(cw, buf["score"][:], buf["over"][:], ALU.mult))
    if cap:
        dve.tensor_copy(buf["mask"][:], buf["over"][:]).then_inc(s["r_count"], 1)
        link(dve.tensor_reduce(buf["sum"][:], cw, AX_X, ALU.add))
        link(dve.reciprocal(buf["sum"][:], buf["sum"][:]))
        link(dve.tensor_tensor(cw, cw, spread(buf["sum"][:], full, 2), ALU.mult))
        meanwhile(1)
        dve.wait_ge(s["r_count"], 2)
        link(dve.tensor_tensor(buf["rank"][:], logits, spread(buf["base"], full, 1), ALU.add))
        link(dve.tensor_scalar(buf["rank"][:], buf["rank"][:], float(CAP), None, ALU.is_le))
        dve.tensor_tensor(buf["base"], buf["base"], k.bank[6][:, NT * E:(NT + 1) * E], ALU.add)
        link(dve.tensor_tensor(cw, cw, buf["rank"][:], ALU.mult))
    else:
        meanwhile(1)
    W = buf["cw"].shape[2]
    part = lambda n: buf["split"][:, :, n * W:(n + 1) * W]
    link(dve.tensor_copy(part(0), buf["cw"][:]))
    link(dve.tensor_tensor(buf["rest"][:], buf["cw"][:], part(0), ALU.subtract))
    link(dve.tensor_copy(part(1), buf["rest"][:]))
    link(dve.tensor_tensor(buf["rest"][:], buf["rest"][:], part(1), ALU.subtract))
    dve.tensor_copy(part(2), buf["rest"][:]).then_inc(s["r_split"], 1)
    meanwhile(2)
    dve.wait_ge(s["r_turned"], 1)
    rows = 3 * W
    dve.tensor_copy(buf["rows"][0:rows, :], k.bank[7][:].bitcast(BF16)[0:rows, 0:T]).then_inc(s["r_rows"], 1)


def route_buffers(sb, experts, width, base):
    full = [P, NT, experts]
    buf = {n: sb("r_" + n, full) for n in ("diff", "exp", "score", "over", "equal", "rank")}
    buf["best"] = sb("r_best", [P, NT, 8])
    buf["top"], buf["sum"] = sb("r_top", [P, NT]), sb("r_sum", [P, NT])
    buf["cw"], buf["rest"] = sb("r_cw", [P, NT, width]), sb("r_rest", [P, NT, width])
    buf["split"] = sb("r_split", [P, NT, 3 * width], BF16)
    buf["rows"] = sb("r_rows", [P, T], BF16)
    buf["mask"] = sb("r_mask", full, BF16)
    buf["base"] = base
    return buf


def biased_ffn(k, tag):
    nc = k.nc
    G, N, W = 1, E0 + 1, E0 + 1
    s = k.semaphores("ffn0", NORM + ROUTE + ["dve", "h", "cw", "h1", "h3", "gate", "linear", "tanh", "act", "down",
                                            "b2", "done"])
    w = lambda name: k.w(G, name)
    with ExitStack() as ctx:
        def sb(name, shape, dt=F32):
            return ctx.enter_context(nc.sbuf_tensor(f"ffn0_{name}{tag}", shape, dt))
        buf = route_buffers(sb, E0, W, None)
        s1 = [sb(f"s1{c}", [P, 2, T]) for c in "gl"]
        hg, hl = sb("hg", [P, 2, T]), sb("hl", [P, 2, T])
        th = sb("th", [P, 2, T])
        p1 = sb("p1", [P, T])
        a = sb("a", [P, 2, T])
        cwr = sb("cwr", [P, T])
        block = ctx.enter_context(nc.Block(no_gpsimd_drain=True))

        @block.sync
        def _(sp):
            k.zero_stale(sp, s)

        @block.tensor
        def _(pe):
            pe.wait_ge(k.loaded, 16)
            pe.wait_ge(k.half_loaded, 16)
            pe.wait_ge(k.w_loaded[G], 16)
            norm_tensor(k, pe, s)

            def up(e):
                for n, (name, freed) in enumerate((("w1g", "h1"), ("w3g", "h3"), ("w1l", "h1"), ("w3l", "h3"))):
                    if e >= 1:
                        pe.wait_ge(s[freed], 2 * (e - 1) + n // 2 + 1)
                    pe.matmul(k.bank[n][:], w(f"{name}{e}"), k.xn[:], start=True, stop=True).then_inc(s["h"], 1)

            def spread_weights(e):
                if e >= 1:
                    pe.wait_ge(s["act"], e)
                pe.matmul(k.bank[4][:], k.h("sel0")[0:3 * W, e * P:(e + 1) * P], buf["rows"][0:3 * W, :],
                          start=True, stop=True).then_inc(s["cw"], 1)

            def down(e):
                pe.wait_ge(s["act"], e + 1)
                pe.matmul(k.bank[5][:], w(f"w2{e}"), a[:, e % 2, :], start=(e == 0), stop=False) \
                    .then_inc(s["down"], 1)

            route_logits(k, pe, s, G, E0)
            for e in range(3):
                up(e)
            route_turn(k, pe, s, buf["split"])
            pe.wait_ge(s["r_rows"], 1)
            spread_weights(0)
            for e in range(1, N):
                if e + 2 < N:
                    up(e + 2)
                down(e - 1)
                spread_weights(e)
            for j in range(NT):
                ins = pe.transpose(k.bank[6][0:W, j * P:(j + 1) * P], buf["cw"][:, j, :], k.c("ident"))
            ins.then_inc(s["b2"], 1)
            down(N - 1)
            pe.wait_ge(s["b2"], 2)
            pe.matmul(k.bank[5][:], w("b2")[0:W, :], cwr[0:W, :], start=False, stop=True).then_inc(s["down"], 1)

        @block.scalar
        def _(act):
            act.wait_ge(k.loaded, 16)
            act.wait_ge(k.w_loaded[G], 16)
            norm_scalar(k, act, s, "exp_and_others")

            def first(e, c):
                act.wait_ge(s["h"], 4 * e + 2 * c + 1)
                if e >= 2:
                    act.wait_ge(s["h3"], 2 * (e - 2) + c + 1)
                act.activation(s1[c][:, e % 2, :], k.bank[2 * c][:], ACT.Identity,
                               bias=w("b1" + "gl"[c])[:, e:e + 1]).then_inc(s["h1"], 1)

            first(0, 0)
            act.wait_ge(s["r_diff"], 1)
            act.activation(buf["exp"][:], buf["diff"][:], ACT.Exp).then_inc(s["r_exp"], 1)
            first(0, 1)
            for e in range(N):
                if e + 1 < N:
                    first(e + 1, 0)
                    first(e + 1, 1)
                act.wait_ge(s["gate"], e + 1)
                if e >= 2:
                    act.wait_ge(s["act"], e - 1)
                act.activation(th[:, e % 2, :], hg[:, e % 2, :], ACT.Tanh, scale=ALPHA / 2).then_inc(s["tanh"], 1)
            act.wait_ge(s["b2"], 1)
            act.activation(cwr[0:W, :], k.bank[6][0:W, :], ACT.Copy).then_inc(s["b2"], 1)

        @block.gpsimd
        def _(pool):
            for e in range(N):
                pool.wait_ge(s["h3"], 2 * e + 1)
                pool.tensor_scalar(hg[:, e % 2, :], hg[:, e % 2, :], LIMIT, None, ALU.min).then_inc(s["gate"], 1)
                pool.wait_ge(s["h3"], 2 * e + 2)
                pool.tensor_scalar(hl[:, e % 2, :], hl[:, e % 2, :], 1.0, LIMIT + 1.0, ALU.add, ALU.min) \
                    .then_inc(s["linear"], 1)

        @block.vector
        def _(dve):
            link = chained(dve, s["dve"])
            dve.wait_ge(k.loaded, 16)
            dve.wait_ge(k.w_loaded[G], 16)
            norm_vector(k, dve, s)
            link(dve.memset(buf["cw"][:, :, E0:W], 1.0))

            def hidden(e):
                for c, h in enumerate((hg, hl)):
                    dve.wait_ge(s["h1"], 2 * e + c + 1)
                    dve.wait_ge(s["h"], 4 * e + 2 * c + 2)
                    dve.scalar_tensor_tensor(h[:, e % 2, :], k.bank[2 * c + 1][:], w("b3" + "gl"[c])[:, e:e + 1],
                                             s1[c][:, e % 2, :], ALU.add, ALU.mult).then_inc(s["h3"], 1)

            def meanwhile(n):
                if n < 2:
                    hidden(n)

            route_vector(k, dve, s, link, buf, E0, K0, w("gate_b"), "seg0", False, meanwhile)
            for e in range(N):
                dve.wait_ge(s["tanh"], e + 1)
                link(dve.scalar_tensor_tensor(p1[:], th[:, e % 2, :], 1.0, hg[:, e % 2, :], ALU.add, ALU.mult))
                dve.wait_ge(s["linear"], e + 1)
                link(dve.scalar_tensor_tensor(p1[:], hl[:, e % 2, :], 1.0 - LIMIT, p1[:], ALU.max, ALU.mult))
                if e + 2 < N:
                    hidden(e + 2)
                dve.wait_ge(s["cw"], e + 1)
                if e >= 2:
                    dve.wait_ge(s["down"], e - 1)
                dve.tensor_tensor(a[:, e % 2, :], p1[:], k.bank[4][:], ALU.mult).then_inc(s["act"], 1)
                dve.wait_ge(s["act"], e + 1)
            dve.wait_ge(s["down"], N + 1)
            dve.tensor_tensor(k.x[:], k.x[:], k.bank[5][:], ALU.add).then_inc(s["done"], 1)


def wide_attention(k, tag):
    nc = k.nc
    G, HP = 2, H // 2
    s = k.semaphores("wide", NORM + ["v", "v_act", "v_dve", "q", "qc", "k", "kc", "scores", "max", "probs", "turned",
                                     "pt_act", "pt_dve", "pv", "outn", "ot", "ot_act", "ot_dve", "y", "dve", "done"])
    at, _ = k.group_at[G][0]["wqkv"]
    wcol = lambda n: k.weights[G][:, at + n * P:at + (n + 1) * P]
    stages = [(g, b) for g in range(HP) for b in range(NB)]
    NS = len(stages)
    with ExitStack() as ctx:
        def sb(name, shape, dt=F32):
            return ctx.enter_context(nc.sbuf_tensor(f"wide_{name}{tag}", shape, dt))
        q, kk = sb("q", [P, 2, T]), sb("k", [P, 2, T])
        va = sb("va", [P, NT, H, DB + 1])
        pin = sb("pin", [P, 2, 2, T])
        pt = sb("pt", [P, 2, 2, T])
        low = sb("low", [P, 2, 4])
        rden = sb("rden", [P, 2, 2])
        on = sb("on", [P, NT, H, DB])
        ot = sb("ot", [P, 2, T])
        block = ctx.enter_context(nc.Block(no_gpsimd_drain=True))
        out = k.bank[6][:, 0:4 * (DB + 1)].rearrange("p (t m e) -> p t m e", t=2, m=2)

        @block.sync
        def _(sp):
            k.zero_stale(sp, s)

        @block.tensor
        def _(pe):
            pe.wait_ge(k.loaded, 16)
            pe.wait_ge(k.w_loaded[G], 16)
            norm_tensor(k, pe, s)
            for n in range(2 * NT):
                j, half = n // 2, n % 2
                if n >= 6:
                    pe.wait_ge(s["v_act" if n % 2 == 0 else "v_dve"], (n - 6) // 2 + 1)
                first = at + (2 * H * DB) + half * 512
                pe.matmul(k.bank[n % 6][:], k.xn[:, j * P:(j + 1) * P], k.weights[G][:, first:first + 512],
                          start=True, stop=True).then_inc(s["v"], 1)

            def project(g, which):
                if which == 0:
                    if g >= 1:
                        pe.wait_ge(s["kc"], g)
                    pe.matmul(k.bank[7][:], wcol(g), k.xn[:], start=True, stop=True).then_inc(s["q"], 1)
                else:
                    pe.wait_ge(s["qc"], g + 1)
                    pe.matmul(k.bank[7][:], wcol(HP + g), k.xn[:], start=True, stop=True).then_inc(s["k"], 1)

            def scores(i):
                g, b = stages[i]
                pe.wait_ge(s["kc"], g + 1)
                if i >= 2:
                    pe.wait_ge(s["probs"], i - 1)
                else:
                    pe.wait_ge(s["v_act"], NT)
                    pe.wait_ge(s["v_dve"], NT)
                for m in range(2):
                    r = slice(64 * m, 64 * m + 64)
                    for t in range(2):
                        ins = pe.matmul(k.bank[2 * (i % 2) + m][:, t * L:(t + 1) * L],
                                        q[r, g % 2, b * L + t * P:b * L + (t + 1) * P],
                                        kk[r, g % 2, b * L:(b + 1) * L], start=True, stop=True)
                ins.then_inc(s["scores"], 1)

            def turn(i):
                pe.wait_ge(s["probs"], i + 1)
                if i >= 1:
                    pe.wait_ge(s["pt_act"], i)
                    pe.wait_ge(s["pt_dve"], i)
                for m in range(2):
                    for key in range(2):
                        for t in range(2):
                            ins = pe.transpose(k.bank[4 + m][:, key * L + t * P:key * L + (t + 1) * P],
                                               pin[:, i % 2, m, t * L + key * P:t * L + (key + 1) * P], k.c("ident"))
                ins.then_inc(s["turned"], 1)

            def weigh(i):
                g, b = stages[i]
                pe.wait_ge(s["pt_act"], i + 1)
                pe.wait_ge(s["pt_dve"], i + 1)
                if i >= 1:
                    pe.wait_ge(s["outn"], i)
                for m in range(2):
                    for t in range(2):
                        for key in range(2):
                            ins = pe.matmul(out[:, t, m, :], pt[:, i % 2, m, key * L + t * P:key * L + (t + 1) * P],
                                            va[:, 2 * b + key, 2 * g + m, :], start=(key == 0), stop=(key == 1))
                ins.then_inc(s["pv"], 1)

            project(0, 0)
            project(0, 1)
            for i in range(NS + 2):
                if i < NS:
                    scores(i)
                    if i + 2 < NS:
                        project(i // 2 + 1, i % 2)
                if 1 <= i <= NS:
                    turn(i - 1)
                if i >= 2:
                    weigh(i - 2)
            pe.wait_ge(s["outn"], NS)
            for g in range(HP):
                if g >= 2:
                    pe.wait_ge(s["ot_act" if g % 2 == 0 else "ot_dve"], g // 2)
                for j in range(NT):
                    ins = pe.transpose(k.bank[g % 2][:, j * P:(j + 1) * P],
                                       on[:, j, 2 * g:2 * g + 2, :].rearrange("p h e -> p (h e)"), k.c("ident"))
                ins.then_inc(s["ot"], 1)
                if g >= 1:
                    last = g - 1
                    pe.wait_ge(s["ot_act" if last % 2 == 0 else "ot_dve"], last // 2 + 1)
                    pe.matmul(k.bank[7][:], k.w(G, "wout")[:, last * P:(last + 1) * P], ot[:, last % 2, :],
                              start=(last == 0), stop=False).then_inc(s["y"], 1)
            pe.wait_ge(s["ot_dve"], HP // 2)
            pe.matmul(k.bank[7][:], k.w(G, "wout")[:, (HP - 1) * P:], ot[:, 1, :],
                      start=False, stop=True).then_inc(s["y"], 1)

        @block.scalar
        def _(act):
            act.wait_ge(k.loaded, 16)
            norm_scalar(k, act, s, None)
            for n in range(0, 2 * NT, 2):
                act.wait_ge(s["v"], n + 1)
                act.activation(va[:, n // 2, 0:8, 0:DB], k.bank[n % 6].rearrange("p (h e) -> p h e", e=DB),
                               ACT.Copy).then_inc(s["v_act"], 1)

            def copy_q(g):
                act.wait_ge(s["q"], g + 1)
                if g >= 2:
                    act.wait_ge(s["scores"], 2 * g - 2)
                act.activation(q[:, g % 2, :], k.bank[7][:], ACT.Copy, scale=float(DB) ** -0.5).then_inc(s["qc"], 1)

            def copy_k(g):
                act.wait_ge(s["k"], g + 1)
                if g >= 2:
                    act.wait_ge(s["scores"], 2 * g - 2)
                act.activation(kk[:, g % 2, :], k.bank[7][:], ACT.Copy).then_inc(s["kc"], 1)

            copy_q(0)
            copy_k(0)
            for i in range(NS + 1):
                if i < NS:
                    act.wait_ge(s["max"], i + 1)
                    if i >= 2:
                        act.wait_ge(s["turned"], i - 1)
                    for m in range(2):
                        for t in range(2):
                            cols = slice(t * L, (t + 1) * L)
                            ins = act.activation(pin[:, i % 2, m, cols], k.bank[2 * (i % 2) + m][:, cols], ACT.Exp,
                                                 bias=low[:, i % 2, 2 * m + t:2 * m + t + 1])
                    ins.then_inc(s["probs"], 1)
                    if i + 2 < NS:
                        (copy_q if i % 2 == 0 else copy_k)(i // 2 + 1)
                if i >= 1:
                    act.wait_ge(s["turned"], i)
                    if i >= 3:
                        act.wait_ge(s["pv"], i - 2)
                    act.activation(pt[:, (i - 1) % 2, 0, :], k.bank[4][:], ACT.Copy).then_inc(s["pt_act"], 1)
            for g in range(0, HP, 2):
                act.wait_ge(s["ot"], g + 1)
                if g >= 2:
                    act.wait_ge(s["y"], g - 1)
                act.activation(ot[:, 0, :], k.bank[0][:], ACT.Copy).then_inc(s["ot_act"], 1)

        @block.vector
        def _(dve):
            link = chained(dve, s["dve"])
            dve.wait_ge(k.loaded, 16)
            norm_vector(k, dve, s)
            link(dve.memset(va[:, :, :, DB:DB + 1], 1.0))
            for n in range(1, 2 * NT, 2):
                dve.wait_ge(s["v"], n + 1)
                dve.tensor_copy(va[:, n // 2, 8:16, 0:DB], k.bank[n % 6].rearrange("p (h e) -> p h e", e=DB)) \
                    .then_inc(s["v_dve"], 1)
            for i in range(NS + 2):
                if i < NS:
                    dve.wait_ge(s["scores"], i + 1)
                    if i >= 2:
                        dve.wait_ge(s["probs"], i - 1)
                    dve.tensor_reduce(low[:, i % 2, :],
                                      k.banks[:, 2 * (i % 2):2 * (i % 2) + 2, :].rearrange("p m (t c) -> p (m t) c", c=L),
                                      AX_X, ALU.max, negate=True).then_inc(s["max"], 1)
                if 1 <= i <= NS:
                    dve.wait_ge(s["turned"], i)
                    if i >= 3:
                        dve.wait_ge(s["pv"], i - 2)
                    dve.tensor_copy(pt[:, (i - 1) % 2, 1, :], k.bank[5][:]).then_inc(s["pt_dve"], 1)
                if i >= 2:
                    g, b = stages[i - 2]
                    dve.wait_ge(s["pv"], i - 1)
                    link(dve.reciprocal(rden[:], out[:, :, :, DB]))
                    dve.tensor_tensor(on[:, 2 * b:2 * b + 2, 2 * g:2 * g + 2, :], out[:, :, :, 0:DB],
                                      spread(rden[:], [P, 2, 2, DB], 3), ALU.mult).then_inc(s["outn"], 1)
                    dve.wait_ge(s["outn"], i - 1)
            for g in range(1, HP, 2):
                dve.wait_ge(s["ot"], g + 1)
                if g >= 2:
                    dve.wait_ge(s["y"], g - 1)
                dve.tensor_copy(ot[:, 1, :], k.bank[1][:]).then_inc(s["ot_dve"], 1)
            dve.wait_ge(s["y"], HP)
            dve.tensor_tensor(k.x[:], k.x[:], k.bank[7][:], ALU.add).then_inc(s["done"], 1)


def capped_ffn(k, tag):
    nc = k.nc
    G, N = 4, E1 // 2 + 1
    AHEAD = 4
    which = int(tag) // 7
    s = k.semaphores("ffn1", NORM + ROUTE + ["dve", "g", "u", "cw", "tanh", "g_read", "u_read", "act", "down", "done"])
    w = lambda name: k.w(G, name)
    with ExitStack() as ctx:
        def sb(name, shape, dt=F32):
            return ctx.enter_context(nc.sbuf_tensor(f"ffn1_{name}{tag}", shape, dt))
        buf = route_buffers(sb, E1, E1, k.base[:, which, :])
        th, p1, a = sb("th", [P, 2, T]), sb("p1", [P, AHEAD + 1, T]), sb("a", [P, 2, T])
        block = ctx.enter_context(nc.Block(no_gpsimd_drain=True))

        @block.sync
        def _(sp):
            k.zero_stale(sp, s)

        @block.tensor
        def _(pe):
            pe.wait_ge(k.loaded, 16)
            pe.wait_ge(k.half_loaded, 16)
            pe.wait_ge(k.w_loaded[G], 16)
            norm_tensor(k, pe, s)

            def up(n):
                rows = 64 if n == 0 else P
                names = ("sg", "su") if n == 0 else (f"g{n - 1}", f"u{n - 1}")
                for m, (name, sem) in enumerate(zip(names, ("g", "u"))):
                    if n >= 2:
                        pe.wait_ge(s[sem + "_read"], n - 1)
                    pe.matmul(k.bank[2 * m + n % 2][0:rows, :], w(name), k.xn[:], start=True, stop=True) \
                        .then_inc(s[sem], 1)

            def spread_weights(n):
                if n >= 2:
                    pe.wait_ge(s["act"], n)
                pe.matmul(k.bank[4][:], k.h("sel1")[0:3 * E1, (n - 1) * P:n * P], buf["rows"][0:3 * E1, :],
                          start=True, stop=True).then_inc(s["cw"], 1)

            def down(n):
                pe.wait_ge(s["act"], n + 1)
                rows = 64 if n == 0 else P
                pe.matmul(k.bank[5][:], w("sd" if n == 0 else f"d{n - 1}")[0:rows, :], a[0:rows, n % 2, :],
                          start=(n == 0), stop=(n == N - 1)).then_inc(s["down"], 1)

            route_logits(k, pe, s, G, E1)
            for n in range(3):
                up(n)
            route_counts(k, pe, s, E1, buf["mask"])
            up(3)
            down(0)
            route_turn(k, pe, s, buf["split"])
            up(4)
            pe.wait_ge(s["r_rows"], 1)
            spread_weights(1)
            for n in range(2, N):
                if n + 3 < N:
                    up(n + 3)
                down(n - 1)
                spread_weights(n)
            down(N - 1)

        @block.scalar
        def _(act):
            act.wait_ge(k.loaded, 16)
            norm_scalar(k, act, s, "exp_and_others")
            for n in range(N):
                rows = 64 if n == 0 else P
                act.wait_ge(s["g"], n + 1)
                if n >= 2:
                    act.wait_ge(s["g_read"], n - 1)
                act.activation(th[0:rows, n % 2, :], k.bank[n % 2][0:rows, :], ACT.Tanh, scale=0.5) \
                    .then_inc(s["tanh"], 1)
                if n == 0:
                    act.wait_ge(s["r_diff"], 1)
                    act.activation(buf["exp"][:], buf["diff"][:], ACT.Exp).then_inc(s["r_exp"], 1)

        @block.vector
        def _(dve):
            link = chained(dve, s["dve"])
            dve.wait_ge(k.loaded, 16)
            norm_vector(k, dve, s)

            def hidden(n):
                rows = slice(0, 64 if n == 0 else P)
                i, o = n % 2, p1[:, n % (AHEAD + 1), :]
                dve.wait_ge(s["tanh"], n + 1)
                dve.scalar_tensor_tensor(o[rows], th[rows, i, :], 1.0, k.bank[i][rows, :], ALU.add, ALU.mult) \
                    .then_inc(s["g_read"], 1)
                dve.wait_ge(s["g_read"], n + 1)
                dve.wait_ge(s["u"], n + 1)
                dve.tensor_tensor(o[rows], o[rows], k.bank[2 + i][rows, :], ALU.mult).then_inc(s["u_read"], 1)

            def weigh(n):
                o = p1[:, n % (AHEAD + 1), :]
                dve.wait_ge(s["u_read"], n + 1)
                if n >= 2:
                    dve.wait_ge(s["down"], n - 1)
                if n == 0:
                    dve.tensor_scalar(a[0:64, 0, :], o[0:64], 0.5, None, ALU.mult).then_inc(s["act"], 1)
                else:
                    dve.wait_ge(s["cw"], n)
                    dve.tensor_tensor(a[:, n % 2, :], o, k.bank[4][:], ALU.mult).then_inc(s["act"], 1)

            def meanwhile(n):
                hidden(n)
                if n == 1:
                    weigh(0)
                if n == 2:
                    hidden(3)

            route_vector(k, dve, s, link, buf, E1, K1, None, "seg1", True, meanwhile)
            for n in range(1, N):
                if n + 3 < N:
                    hidden(n + 3)
                weigh(n)
            dve.wait_ge(s["down"], N)
            dve.tensor_tensor(k.x[:], k.x[:], k.bank[5][:], ALU.add).then_inc(s["done"], 1)


def state_space(k, tag):
    nc = k.nc
    G, NP = 5, 64
    AHEAD, HOLD = 3, 4
    DELTA, DELTA_X = (0, 1, 4), (2, 3, 6)
    s = k.semaphores("ssm", NORM + ["up", "left", "right", "tanh_r", "conv", "tanh_c", "x", "proj", "z", "e", "ln",
                                    "split", "packed0", "packed1", "packed2", "packed3", "bc", "cc", "a", "da",
                                    "dbx", "h", "hc", "red", "gated", "down", "dve", "acts", "done"])
    w = lambda name: k.w(G, name)
    with ExitStack() as ctx:
        def sb(name, shape, dt=F32):
            return ctx.enter_context(nc.sbuf_tensor(f"ssm_{name}{tag}", shape, dt))
        left = sb("left", [P, NB, L + 2])
        right, gate = sb("right", [P, T]), sb("gate", [P, T])
        conv, tc, xs = sb("conv", [P, T]), sb("tc", [P, T]), sb("xs", [P, T])
        z, u, fix, delta = sb("z", [P, T]), sb("u", [P, T]), sb("fix", [P, T]), sb("delta", [P, T])
        e, ln, dx = tc, right, z
        parts = sb("parts", [P, 2, 3, T], BF16)
        packed = sb("packed", [P, 2, 4, T], BF16)
        bm, cm = sb("bm", [P, T]), sb("cm", [P, T])
        da, dbx = sb("da", [P, AHEAD, T]), sb("dbx", [P, AHEAD, T])
        h, hc = sb("h", [P, HOLD, T]), sb("hc", [P, HOLD, T])
        block = ctx.enter_context(nc.Block(no_gpsimd_drain=True))
        two = lambda ap: ap.rearrange("p (b t) -> p b t", b=NB)

        def spot(p):
            return p // 16, p % 16

        @block.sync
        def _(sp):
            k.zero_stale(sp, s)
            sp.wait_ge(s["split"], 6)
            for g in range(4):
                for part in range(3):
                    sp.dma_start(packed[32 * part:32 * part + 32, :, g, :], parts[32 * g:32 * g + 32, :, part, :]) \
                        .then_inc(s[f"packed{g}"], 16)

        @block.tensor
        def _(pe):
            pe.wait_ge(k.loaded, 16)
            pe.wait_ge(k.half_loaded, 16)
            pe.wait_ge(k.w_loaded[G], 16)
            norm_tensor(k, pe, s)
            pe.matmul(k.bank[0][:], w("left"), k.xn[:], start=True, stop=True).then_inc(s["up"], 1)
            pe.matmul(k.bank[1][:], w("right"), k.xn[:], start=True, stop=True).then_inc(s["up"], 1)
            pe.wait_ge(s["x"], 1)
            for n, name in enumerate(("delta", "wb", "wc")):
                pe.matmul(k.bank[2 + n][:], w(name), xs[:], start=True, stop=True).then_inc(s["proj"], 1)
            pe.wait_ge(s["cc"], 2)

            def spread_rows(p):
                g, c = spot(p)
                if c == 0:
                    pe.wait_ge(s[f"packed{g}"], 16 * 3)
                if p >= AHEAD:
                    pe.wait_ge(s["da"], p - AHEAD + 1)
                    pe.wait_ge(s["dbx"], p - AHEAD + 1)
                pick = k.h("pick")[0:96, c * P:(c + 1) * P]
                pe.matmul(k.bank[DELTA[p % AHEAD]][:], pick, packed[0:96, 0, g, :], start=True, stop=True).then_inc(s["bc"], 1)
                pe.matmul(k.bank[DELTA_X[p % AHEAD]][:], pick, packed[0:96, 1, g, :], start=True, stop=True) \
                    .then_inc(s["bc"], 1)

            def reduce(p):
                g, c = spot(p)
                pe.wait_ge(s["hc"], p + 1)
                row = 32 * g + c
                pe.matmul(k.bank[5][:], k.c("hot")[:, P - row:2 * P - row], hc[:, p % HOLD, :],
                          start=(p == 0), stop=(p == NP - 1)).then_inc(s["red"], 1)

            for p in range(NP + HOLD):
                if p < NP:
                    spread_rows(p)
                if p >= HOLD:
                    reduce(p - HOLD)
            pe.wait_ge(s["gated"], 1)
            pe.matmul(k.bank[6][:], w("down"), conv[:], start=True, stop=True).then_inc(s["down"], 1)

        @block.scalar
        def _(act):
            link = chained(act, s["acts"])
            act.wait_ge(k.loaded, 16)
            act.wait_ge(k.w_loaded[G], 16)
            act.activation(k.a_neg[:], w("a_log"), ACT.Exp).then_inc(s["a"], 1)
            norm_scalar(k, act, s, "exp_and_others")
            act.wait_ge(s["up"], 1)
            act.activation(left[:, :, 2:L + 2], two(k.bank[0]), ACT.Identity, bias=w("b_left")).then_inc(s["left"], 1)
            act.wait_ge(s["up"], 2)
            act.activation(right[:], k.bank[1][:], ACT.Identity, bias=w("b_right")).then_inc(s["right"], 1)
            act.wait_ge(s["right"], 1)
            act.activation(gate[:], right[:], ACT.Tanh, scale=0.5).then_inc(s["tanh_r"], 1)
            act.wait_ge(s["conv"], 1)
            act.activation(tc[:], conv[:], ACT.Tanh, scale=0.5).then_inc(s["tanh_c"], 1)
            act.wait_ge(s["proj"], 1)
            act.activation(z[:], k.bank[2][:], ACT.Identity, bias=w("b_delta")).then_inc(s["z"], 1)
            act.preload_act_table_set("natural_log_exp_and_others")
            act.wait_ge(s["z"], 1)
            link(act.activation(e[:], z[:], ACT.Abs))
            act.activation(e[:], e[:], ACT.Exp, scale=-1.0).then_inc(s["e"], 1)
            act.wait_ge(s["proj"], 2)
            act.activation(bm[:], k.bank[3][:], ACT.Identity, bias=w("b_b")).then_inc(s["cc"], 1)
            act.wait_ge(s["proj"], 3)
            act.activation(cm[:], k.bank[4][:], ACT.Identity, bias=w("b_c")).then_inc(s["cc"], 1)
            act.wait_ge(s["e"], 2)
            act.activation(ln[:], u[:], ACT.Ln).then_inc(s["ln"], 1)
            act.wait_ge(s["a"], 2)
            for p in range(NP):
                act.wait_ge(s["bc"], 2 * p + 1)
                if p >= AHEAD:
                    act.wait_ge(s["h"], p - AHEAD + 1)
                act.activation(da[:, p % AHEAD, :], k.bank[DELTA[p % AHEAD]][:], ACT.Exp, scale=k.a_neg[:, p:p + 1]) \
                    .then_inc(s["da"], 1)

        @block.gpsimd
        def _(pool):
            pool.wait_ge(s["cc"], 2)
            for p in range(NP):
                pool.wait_ge(s["h"], p + 1)
                if p >= HOLD:
                    pool.wait_ge(s["red"], p - HOLD + 1)
                pool.tensor_tensor(hc[:, p % HOLD, :], h[:, p % HOLD, :], cm[:], ALU.mult).then_inc(s["hc"], 1)

        @block.vector
        def _(dve):
            link = chained(dve, s["dve"])
            dve.wait_ge(k.loaded, 16)
            dve.wait_ge(k.w_loaded[G], 16)
            norm_vector(k, dve, s)
            dve.wait_ge(s["a"], 1)
            dve.tensor_scalar(k.a_neg[:], k.a_neg[:], -1.0, None, ALU.mult).then_inc(s["a"], 1)
            link(dve.memset(left[:, :, 0:2], 0.0))
            dve.wait_ge(s["left"], 1)
            taps = w("conv_w")
            link(dve.tensor_scalar(two(conv[:]), left[:, :, 0:L], taps[:, 0:1], w("conv_b"), ALU.mult, ALU.add))
            link(dve.scalar_tensor_tensor(two(conv[:]), left[:, :, 1:L + 1], taps[:, 1:2], two(conv[:]),
                                          ALU.mult, ALU.add))
            dve.scalar_tensor_tensor(two(conv[:]), left[:, :, 2:L + 2], taps[:, 2:3], two(conv[:]),
                                     ALU.mult, ALU.add).then_inc(s["conv"], 1)
            dve.wait_ge(s["tanh_c"], 1)
            link(dve.scalar_tensor_tensor(xs[:], tc[:], 1.0, conv[:], ALU.add, ALU.mult))
            dve.tensor_scalar(xs[:], xs[:], 0.5, None, ALU.mult).then_inc(s["x"], 1)
            dve.wait_ge(s["x"], 1)
            dve.wait_ge(s["tanh_r"], 1)
            link(dve.scalar_tensor_tensor(gate[:], gate[:], 1.0, right[:], ALU.add, ALU.mult))
            dve.wait_ge(s["e"], 1)
            dve.tensor_scalar(u[:], e[:], 1.0, None, ALU.add).then_inc(s["e"], 1)
            dve.wait_ge(s["e"], 2)
            link(dve.scalar_tensor_tensor(fix[:], u[:], 1.0, e[:], ALU.subtract, ALU.subtract))
            dve.wait_ge(s["ln"], 1)
            link(dve.tensor_tensor(ln[:], ln[:], fix[:], ALU.subtract))
            link(dve.scalar_tensor_tensor(delta[:], z[:], 0.0, ln[:], ALU.max, ALU.add))
            link(dve.tensor_tensor(dx[:], delta[:], xs[:], ALU.mult))
            for which, v in enumerate((delta, dx)):
                dve.tensor_copy(parts[:, which, 0, :], v[:]).then_inc(s["split"], 1)
                dve.wait_ge(s["split"], 3 * which + 1)
                link(dve.tensor_tensor(fix[:], v[:], parts[:, which, 0, :], ALU.subtract))
                dve.tensor_copy(parts[:, which, 1, :], fix[:]).then_inc(s["split"], 1)
                dve.wait_ge(s["split"], 3 * which + 2)
                link(dve.tensor_tensor(fix[:], fix[:], parts[:, which, 1, :], ALU.subtract))
                dve.tensor_copy(parts[:, which, 2, :], fix[:]).then_inc(s["split"], 1)
                dve.wait_ge(s["split"], 3 * which + 3)
            dve.wait_ge(s["cc"], 1)
            for p in range(NP + 1):
                if p < NP:
                    dve.wait_ge(s["bc"], 2 * p + 2)
                    if p >= AHEAD:
                        dve.wait_ge(s["h"], p - AHEAD + 1)
                    dve.tensor_tensor(dbx[:, p % AHEAD, :], k.bank[DELTA_X[p % AHEAD]][:], bm[:], ALU.mult).then_inc(s["dbx"], 1)
                if p >= 1:
                    n = p - 1
                    dve.wait_ge(s["dbx"], n + 1)
                    dve.wait_ge(s["da"], n + 1)
                    if n >= HOLD:
                        dve.wait_ge(s["hc"], n - HOLD + 1)
                    for b in range(NB):
                        cols = slice(b * L, (b + 1) * L)
                        ins = dve.tensor_tensor_scan(h[:, n % HOLD, cols], da[:, n % AHEAD, cols], dbx[:, n % AHEAD, cols], 0.0,
                                                     ALU.mult, ALU.add)
                    ins.then_inc(s["h"], 1)
            dve.wait_ge(s["red"], NP)
            link(dve.scalar_tensor_tensor(fix[:], xs[:], w("skip"), k.bank[5][:], ALU.mult, ALU.add))
            dve.scalar_tensor_tensor(conv[:], fix[:], 0.5, gate[:], ALU.mult, ALU.mult).then_inc(s["gated"], 1)
            dve.wait_ge(s["down"], 1)
            dve.scalar_tensor_tensor(k.x[:], k.bank[6][:], w("b_down"), k.x[:], ALU.add, ALU.add) \
                .then_inc(s["done"], 1)
def hybrid_kernel(nc, x_in, const_in, half_in, weights_in, x_out):
    with ExitStack() as ctx:
        k = Core(nc, ctx)
        a_log_at = k.group_at[5][0]["a_log"][0]
        with nc.Block(no_gpsimd_drain=True) as block:
            @block.sync
            def _(sp):
                sp.dma_start(k.tok_in[:], x_in[0].rearrange("(j p) d -> p j d", p=P)).then_inc(k.tokens, 16)
                sp.dma_start(k.const[:], const_in).then_inc(k.loaded, 16)
                sp.dma_start(k.weights[0][:], weights_in[0]).then_inc(k.w_loaded[0], 16)
                sp.dma_start(k.weights[1][:], weights_in[1]).then_inc(k.w_loaded[1], 16)
                sp.dma_start(k.half[:], half_in).then_inc(k.half_loaded, 16)
                for g in range(2, 6):
                    sp.dma_start(k.weights[g][:], weights_in[g]).then_inc(k.w_loaded[g], 16)

            @block.vector
            def _(dve):
                dve.memset(k.base[:], 0.0)
                dve.memset(k.vm[:], 0.0).then_inc(k.once, 1)
        turn_tokens(k, x_out, None, "first")
        with nc.Fori(0, x_in.shape[0]) as it:
            for n, layer in enumerate(PLAN[:LAYERS]):
                layer(k, n, x_in, it)
            turn_tokens(k, x_out, it, "")
        with nc.Block(no_gpsimd_drain=True) as block:
            @block.sync
            def _(sp):
                sp.wait_ge(k.semaphores("turn", TURN)["stored"], 16)
                sp.wait_ge(k.tokens, 16)


PLAN = [lambda k, n, x_in, it: narrow_attention(k, n, True, x_in, it), lambda k, n, *_: biased_ffn(k, n),
        lambda k, n, *_: wide_attention(k, n), lambda k, n, *_: biased_ffn(k, n),
        lambda k, n, *_: narrow_attention(k, n, False), lambda k, n, *_: capped_ffn(k, n),
        lambda k, n, *_: state_space(k, n), lambda k, n, *_: capped_ffn(k, n)]


def kernel(**inputs):
    import numpy as np
    import concourse.bacc as bacc
    from concourse.bass_utils import run_bass_kernel_spmd

    const_at, half_at, group_at = tables()
    v = {name: np.ascontiguousarray(a) for name, a in inputs.items()}
    f32 = np.dtype("float32")

    const = np.zeros((P, const_at[1]), f32)
    half = np.zeros((P, half_at[1]), f32)

    def put(packed, where, name, a, rows=slice(0, P)):
        at, width = where[name]
        packed[rows, at:at + width] = a

    idx = np.arange(P)
    tri = (idx[:, None] <= idx[None, :])
    ones = np.ones((P, P), f32)
    put(const, const_at[0], "mean", ones / P)
    put(const, const_at[0], "ident", np.eye(P))
    put(const, const_at[0], "tri", np.concatenate([tri, ones, tri], 1))
    hide = np.where(tri.T, 0.0, BIG)
    put(const, const_at[0], "trib", np.concatenate([hide, hide * 0, hide], 1))
    pair = (idx % DA) % (DA // 2)
    theta = (1.0 / np.float32(10000.0) ** (np.arange(0, DA, 2, dtype=f32) / np.float32(DA))).astype(f32)
    angle = (np.arange(L, dtype=f32)[None, :] * theta[pair][:, None]).astype(f32)
    sign = np.where(idx % DA < DA // 2, -1.0, 1.0)[:, None]
    scale = -1.0 / np.sqrt(np.float64(DA))
    cos, sin = np.cos(angle.astype(np.float64)), np.sin(angle.astype(np.float64)) * sign
    put(const, const_at[0], "cosq", cos * scale)
    put(const, const_at[0], "sinq", sin * scale)
    put(const, const_at[0], "cosk", cos)
    put(const, const_at[0], "sink", sin)
    hot = np.zeros((P, 2 * P), f32)
    hot[:64, P] = 1.0
    hot[64:, P + 16] = 1.0
    put(const, const_at[0], "hot", hot)
    put(const, const_at[0], "rows", (idx[:, None] // DA % 4 == np.arange(4)[None, :]))
    put(const, const_at[0], "eps", 1e-5)
    put(const, const_at[0], "ones", 1.0)
    put(const, const_at[0], "heads", (idx[:, None] // DA == np.arange(H)[None, :]))
    put(const, const_at[0], "seg0", np.tile(np.arange(E0) != 0, NT)[None, :])
    put(const, const_at[0], "seg1", np.tile(np.arange(E1) != 0, NT)[None, :])
    for e in range(E0 + 1):
        sel = np.zeros((P, P), f32)
        sel[[e, E0 + 1 + e, 2 * (E0 + 1) + e], :] = 0.5
        at = half_at[0]["sel0"][0] + e * P
        half[:, at:at + P] = sel
    for p in range(E1 // 2):
        sel = np.zeros((P, P), f32)
        for part in range(3):
            sel[part * E1 + 2 * p, :64] = 0.5
            sel[part * E1 + 2 * p + 1, 64:] = 0.5
        at = half_at[0]["sel1"][0] + p * P
        half[:, at:at + P] = sel
    for c in range(16):
        sel = np.zeros((P, P), f32)
        for part in range(3):
            sel[part * 32 + c, :64] = 1.0
            sel[part * 32 + 16 + c, 64:] = 1.0
        at = half_at[0]["pick"][0] + c * P
        half[:, at:at + P] = sel
    put(half, half_at[0], "lower", tri)
    put(half, half_at[0], "ones", 1.0)
    put(half, half_at[0], "identb", np.eye(P))
    half = half.astype(np.dtype("bfloat16"))

    packs = [np.zeros((P, width), f32) for _, width in group_at]

    def lay(g, name, a):
        at, width = group_at[g][0][name]
        packs[g][:a.shape[0], at:at + width] = a

    for name, key in (("wq", "Wq"), ("wk", "Wk"), ("wv", "Wv"), ("wo", "Wo")):
        lay(0, name, v[f"L0_attn_a_{key}"].T)
    lay(1, "gate", v["L0_ffn_gate_w"].T)
    lay(1, "gate_b", np.broadcast_to(v["L0_ffn_gate_b"], (P, E0)))
    lay(1, "b2", np.concatenate([v["L0_ffn_b2"], v["L0_ffn_sb2"][None]], 0))
    w1 = np.concatenate([v["L0_ffn_w1"], v["L0_ffn_sw1"][None]], 0)
    w3 = np.concatenate([v["L0_ffn_w3"], v["L0_ffn_sw3"][None]], 0)
    w2 = np.concatenate([v["L0_ffn_w2"], v["L0_ffn_sw2"][None]], 0)
    b1 = np.concatenate([v["L0_ffn_b1"], v["L0_ffn_sb1"][None]], 0)
    b3 = np.concatenate([v["L0_ffn_b3"], v["L0_ffn_sb3"][None]], 0)
    for name, b in (("b1", b1), ("b3", b3)):
        lay(1, name + "g", b[:, 0::2].T)
        lay(1, name + "l", b[:, 1::2].T)
    for e in range(E0 + 1):
        for name, a in (("w1", w1), ("w3", w3)):
            lay(1, f"{name}g{e}", a[e, 0::2].T)
            lay(1, f"{name}l{e}", a[e, 1::2].T)
        lay(1, f"w2{e}", w2[e].T)
    lay(2, "wqkv", v["L0_attn_b_w_qkv"])
    lay(2, "wout", v["L0_attn_b_w_out"].reshape(8, P, P).transpose(1, 0, 2).reshape(P, 8 * P))
    flip = (idx // DA) * DA + (idx % DA + DA // 2) % DA
    for name, key in (("wq", "W_Q"), ("wk", "W_K"), ("wv", "W_V"), ("wo", "W_O")):
        lay(3, name, v[f"L1_attn_a_{key}"].T)
    lay(3, "wqf", v["L1_attn_a_W_Q"][flip].T)
    lay(3, "wkf", v["L1_attn_a_W_K"][flip].T)
    gu, dn = v["L1_ffn_w_gate_up"], v["L1_ffn_w_down"]
    lay(4, "gate", v["L1_ffn_gate_w"].T)
    lay(4, "sg", v["L1_ffn_shared_w_gate_up"][:, :64])
    lay(4, "su", v["L1_ffn_shared_w_gate_up"][:, 64:])
    lay(4, "sd", v["L1_ffn_shared_w_down"])
    for p in range(E1 // 2):
        lay(4, f"g{p}", np.concatenate([gu[2 * p][:, :64], gu[2 * p + 1][:, :64]], 1))
        lay(4, f"u{p}", np.concatenate([gu[2 * p][:, 64:], gu[2 * p + 1][:, 64:]], 1))
        lay(4, f"d{p}", np.concatenate([dn[2 * p], dn[2 * p + 1]], 0))
    m = {key[len("L1_attn_b_"):]: a for key, a in v.items() if key.startswith("L1_attn_b_")}
    lay(5, "left", m["W_up"][:, :P])
    lay(5, "right", m["W_up"][:, P:])
    lay(5, "delta", m["W_delta"])
    lay(5, "wb", np.concatenate([m["W_B"], m["W_B"]], 1))
    lay(5, "wc", np.concatenate([m["W_C"], m["W_C"]], 1))
    lay(5, "down", m["W_down"])
    lay(5, "b_left", m["b_up"][:P, None])
    lay(5, "b_right", m["b_up"][P:, None])
    lay(5, "conv_w", m["conv_w"])
    lay(5, "conv_b", m["conv_b"][:, None])
    lay(5, "b_delta", m["b_delta"][:, None])
    lay(5, "b_b", np.concatenate([m["b_B"], m["b_B"]], 0)[:, None])
    lay(5, "b_c", np.concatenate([m["b_C"], m["b_C"]], 0)[:, None])
    lay(5, "skip", m["D_skip"][:, None])
    lay(5, "b_down", m["b_down"][:, None])
    lay(5, "a_log", m["A_log"].reshape(4, 2, 16, 64).transpose(1, 3, 0, 2).reshape(P, 64))

    x = v["L0_attn_a_x"]
    passes = x.shape[0] // NB
    arrays = {"x": x.reshape(passes, T, P), "const": const, "half": half}
    arrays.update({f"weights_{g}": a for g, a in enumerate(packs)})
    nc = bacc.Bacc("TRN2", target_bir_lowering=False, num_devices=1)
    ap = {name: nc.dram_tensor(f"in_{name}", a.shape, mybir.dt.from_np(a.dtype), kind="ExternalInput").ap()
          for name, a in arrays.items()}
    out = nc.dram_tensor("out", (passes, T, P), F32, kind="ExternalOutput").ap()
    hybrid_kernel(nc, ap["x"], ap["const"], ap["half"], [ap[f"weights_{g}"] for g in range(6)], out)
    got = run_bass_kernel_spmd(nc, [{f"in_{name}": a for name, a in arrays.items()}], core_ids=[0])
    return got.results[0]["out"].reshape(x.shape)
```

```python
from contextlib import ExitStack

import concourse.bass as bass
from concourse import mybir

LAYERS = 8

ALU = mybir.AluOpType
ACT = mybir.ActivationFunctionType
AX_X = mybir.AxisListType.X
F32 = mybir.dt.float32
BF16 = mybir.dt.bfloat16
F32R = mybir.dt.float32r

P = 128
T = 512
NT = T // P
L = 256
NB = T // L
H = 16
DA = 8
DB = 64
E0, K0 = 8, 2
E1, K1 = 32, 4
CAP = 128
ALPHA, LIMIT = 1.702, 7.0
WARM = {"squares": 1, "norm": 6, "features": 10, "rotary": 12, "conv": 8, "parts": 24, "residual": 3}
BIG = 1e30


def layout(parts):
    at, where = 0, {}
    for name, width in parts:
        where[name] = (at, width)
        at += width
    return where, at


def tables():
    const = layout([("mean", P), ("centre", P), ("ident", P), ("tri", 3 * P), ("trib", 3 * P), ("cosq", L), ("sinq", L),
                    ("cosk", L), ("sink", L), ("ones", L), ("heads", H), ("hot", 2 * P), ("rows", 4), ("eps", 1),
                    ("seg0", NT * E0), ("seg1", NT * E1)])
    half = layout([("sel0", (E0 + 1) * P), ("sel1", (E1 // 2) * P), ("pick", 16 * P), ("lower", P), ("ones", P),
                   ("identb", P)])
    groups = [
        layout([("wq", P), ("wk", P), ("wv", P), ("wo", P)]),
        layout([("gate", E0), ("gate_b", E0), ("b1g", 9), ("b1l", 9), ("b3g", 9), ("b3l", 9), ("b2", P)]
               + [(f"w2{e}", P) for e in range(E0 + 1)]),
        layout([("wqkv", 3 * H * DB), ("wout", H * DB)]),
        layout([("wq", P), ("wqf", P), ("wk", P), ("wkf", P), ("wv", P), ("wo", P)]),
        layout([("gate", E1), ("sg", 64), ("su", 64), ("sd", P)]
               + [(f"d{p}", P) for p in range(E1 // 2)]),
        layout([("left", P), ("right", P), ("delta", P), ("wb", P), ("wc", P), ("down", P), ("b_left", 1),
                ("b_right", 1), ("conv_w", 3), ("conv_b", 1), ("b_delta", 1), ("b_b", 1), ("b_c", 1),
                ("skip", 1), ("b_down", 1), ("a_log", 64)]),
    ]
    return const, half, groups


def up_tables():
    return [layout([(f"{w}{e}", P) for e in range(E0 + 1) for w in ("w1g", "w3g", "w1l", "w3l")]),
            layout([(f"{w}{p}", P) for p in range(E1 // 2) for w in ("g", "u")])]


class Core:

    def __init__(self, nc, ctx):
        self.nc, self.ctx = nc, ctx
        self.const_at, self.half_at, self.group_at = tables()
        sb = self.sb
        self.const = sb("const", [P, self.const_at[1]])
        self.half = sb("half", [P, self.half_at[1]], BF16)
        self.weights = [sb(f"weights{g}", [P, width]) for g, (_, width) in enumerate(self.group_at)]
        self.up_at = up_tables()
        self.up_high = [sb(f"up_high{n}", [P, width], F32R) for n, (_, width) in enumerate(self.up_at)]
        self.up_low = [sb(f"up_low{n}", [P, width], F32R) for n, (_, width) in enumerate(self.up_at)]
        self.x = sb("x_resid", [P, T])
        self.xn = sb("x_norm", [P, T])
        self.sq = sb("x_square", [P, T])
        self.a_neg = sb("a_neg", [P, 64])
        self.base = sb("base", [P, 2, E1])
        self.banks = ctx.enter_context(nc.psum_tensor("banks", [P, 8, 512], F32))
        self.bank = [self.banks[:, i, :] for i in range(8)]
        self.tok_in, self.tok_out = sb("tok_in", [P, NT, P]), sb("tok_out", [P, NT, P])
        self.tokens = ctx.enter_context(nc.semaphore("tokens"))
        self.half_loaded = ctx.enter_context(nc.semaphore("half_loaded"))
        self.loaded = ctx.enter_context(nc.semaphore("loaded"))
        self.w_loaded = [ctx.enter_context(nc.semaphore(f"w_loaded{g}")) for g in range(6)]
        self.up_loaded = [ctx.enter_context(nc.semaphore(f"up_loaded{n}")) for n in range(2)]
        self.up_cut = ctx.enter_context(nc.semaphore("up_cut"))
        self.sets = {}
        self.stale = None

    def sb(self, name, shape, dt=F32):
        return self.ctx.enter_context(self.nc.sbuf_tensor(name, shape, dt))

    def c(self, name):
        at, width = self.const_at[0][name]
        return self.const[:, at:at + width]

    def h(self, name):
        at, width = self.half_at[0][name]
        return self.half[:, at:at + width]

    def w(self, g, name):
        at, width = self.group_at[g][0][name]
        return self.weights[g][:, at:at + width]

    def up_parts(self, n, name):
        at, width = self.up_at[n][0][name]
        return self.up_high[n][:, at:at + width], self.up_low[n][:, at:at + width]

    def semaphores(self, layer, names, kind=None, shared=()):
        for group, members in ((kind, shared), (layer, names)):
            if group is not None and group not in self.sets:
                self.sets[group] = {n: self.ctx.enter_context(self.nc.semaphore(f"{group}_{n}")) for n in members}
        return {**self.sets.get(kind, {}), **self.sets[layer]}

    def zero_stale(self, engine, mine):
        if self.stale is not None and self.stale != mine:
            for nums in runs(sorted(s.num for s in self.stale.values())):
                engine.sem_clear(nums)
        self.stale = mine


def runs(nums):
    found = []
    for n in nums:
        if found and found[-1].stop == n:
            found[-1] = range(found[-1].start, n + 1)
        else:
            found.append(range(n, n + 1))
    return found


def chained(engine, sem):
    count = [0]

    def link(ins):
        count[0] += 1
        ins.then_inc(sem, 1)
        engine.wait_ge(sem, count[0])
    return link


def spread(ap, shape, axis):
    return ap.unsqueeze(axis).broadcast_to(shape)


CUT = ["x_high", "x_low"]


def cut_scalar(k, act, s, x_high):
    for n, cols in enumerate(halves()):
        act.wait_ge(s["n_out"], n + 1)
        act.activation(x_high[:, cols], k.xn[:, cols], ACT.Copy).then_inc(s["x_high"], 1)


def cut_vector(k, dve, s, x_high, x_low):
    for n, cols in enumerate(halves()):
        dve.wait_ge(s["x_high"], n + 1)
        dve.tensor_tensor(x_low[:, cols], k.xn[:, cols], x_high[:, cols].bitcast(F32), ALU.subtract) \
            .then_inc(s["x_low"], 1)


def cut_product(pe, out, weights, tokens):
    (w_high, w_low), (x_high, x_low) = weights, tokens
    pe.matmul(out, w_high, x_high, start=True, stop=False)
    pe.matmul(out, w_high, x_low, start=False, stop=False)
    return pe.matmul(out, w_low, x_high, start=False, stop=True)


TURN = ["turned", "turned_in", "copied", "copied_in", "stored"]
NORM = ["n_cent", "n_sq", "n_var", "n_ln", "n_rstd", "n_out"]


def halves():
    return [slice(b * L, (b + 1) * L) for b in range(NB)]


def keep_clock(k, pe, n, bank=5):
    for _ in range(n):
        pe.matmul(k.bank[bank][:], k.h("identb"), k.half[:, 0:512], start=True, stop=True)


def norm_tensor(k, pe, s):
    for n, cols in enumerate(halves()):
        pe.matmul(k.bank[6 + n][:, 0:L], k.c("centre"), k.x[:, cols], start=True, stop=True).then_inc(s["n_cent"], 1)
    keep_clock(k, pe, WARM["squares"])
    for n, cols in enumerate(halves()):
        pe.wait_ge(s["n_sq"], n + 1)
        pe.matmul(k.bank[6 + n][:, L:2 * L], k.c("mean"), k.sq[:, cols], start=True, stop=True).then_inc(s["n_var"], 1)
    keep_clock(k, pe, WARM["norm"])
    pe.wait_ge(s["n_out"], NB)


def norm_scalar(k, act, s, then):
    for n, cols in enumerate(halves()):
        act.wait_ge(s["n_cent"], n + 1)
        act.activation(k.sq[:, cols], k.bank[6 + n][:, 0:L], ACT.Square).then_inc(s["n_sq"], 1)
    for n, cols in enumerate(halves()):
        act.wait_ge(s["n_var"], n + 1)
        act.activation(k.sq[:, cols], k.bank[6 + n][:, L:2 * L], ACT.Ln, bias=k.c("eps")).then_inc(s["n_ln"], 1)
        act.wait_ge(s["n_ln"], n + 1)
        act.activation(k.sq[:, cols], k.sq[:, cols], ACT.Exp, scale=-0.5).then_inc(s["n_rstd"], 1)
    if then is not None:
        act.preload_act_table_set(then)


def norm_vector(k, dve, s):
    for n, cols in enumerate(halves()):
        dve.wait_ge(s["n_rstd"], n + 1)
        dve.tensor_tensor(k.xn[:, cols], k.bank[6 + n][:, 0:L], k.sq[:, cols], ALU.mult).then_inc(s["n_out"], 1)
    dve.wait_ge(s["n_out"], NB)


def turn_tokens(k, x_out, it, tag):
    nc = k.nc
    s = k.semaphores("turn", TURN)
    with nc.Block(no_gpsimd_drain=True) as block:
        @block.sync
        def _(sp):
            k.zero_stale(sp, s)
            if it is not None:
                sp.wait_ge(s["copied"], 1)
                sp.dma_start(x_out[bass.ds(it, 1)].rearrange("o (j p) d -> p (o j) d", p=P), k.tok_out[:]) \
                    .then_inc(s["stored"], 16)
            else:
                sp.sem_inc(s["stored"], 16)

        @block.tensor
        def _(pe):
            pe.wait_ge(k.loaded, 16)
            if it is not None:
                for j in range(NT):
                    ins = pe.transpose(k.bank[0][:, j * P:(j + 1) * P], k.x[:, j * P:(j + 1) * P], k.c("ident"))
                ins.then_inc(s["turned"], 1)
            pe.wait_ge(k.tokens, 16)
            for j in range(NT):
                ins = pe.transpose(k.bank[1][:, j * P:(j + 1) * P], k.tok_in[:, j, :], k.c("ident"))
            ins.then_inc(s["turned_in"], 1)

        @block.vector
        def _(dve):
            if it is not None:
                dve.wait_ge(s["turned"], 1)
                dve.tensor_copy(k.tok_out[:].rearrange("p j d -> p (j d)"), k.bank[0][:]).then_inc(s["copied"], 1)
            dve.wait_ge(s["turned_in"], 1)
            dve.tensor_copy(k.x[:], k.bank[1][:]).then_inc(s["copied_in"], 1)


def narrow_attention(k, tag, linear, x_in=None, it=None):
    nc = k.nc
    G = 0 if linear else 3
    layer = "lin" if linear else "rot"
    passes = x_in.shape[0] if linear else None
    s = k.semaphores("narrow", ["proj", "low", "high", "qk", "vcopy", "dve", "scores", "probs_in", "probs",
                                "turned", "pt", "pv", "sums", "prod", "cleared", "k_turned", "k_tokens", "state",
                                "states", "wide", "wide_t", "ot", "y", "done"], "mixer", NORM)
    w = lambda name: k.w(G, name)
    stages = [(b, c, jj) for b in range(NB) for c in range(4) for jj in range(2)]
    NS = len(stages)
    with ExitStack() as ctx:
        def sb(name, shape, dt=F32):
            return ctx.enter_context(nc.sbuf_tensor(f"{layer}_{name}{tag}", shape, dt))
        vm = sb("v_by_head", [P, NT, H * (P + DA)])
        by_head = vm[:, :, 0:H * (P + DA)].rearrange("p t (h x) -> p t h x", x=P + DA)[:, :, :, 0:DA]
        q, kk = sb("q", [P, T]), sb("k", [P, T])
        km = sb("km", [P, 4, T])
        t1, t2 = sb("t1", [P, T]), sb("t2", [P, T])
        if not linear:
            pin = sb("pin", [P, 2, 2, 3 * P])
        pt = sb("pt", [P, 2, 2, 3 * P])
        low = sb("low", [P, 2, 4])
        den = sb("den", [P, NT, H])
        wide = sb("wide", [P, NT, H, DA])
        if linear:
            vt, kt = sb("vt", [P, NB, P]), sb("kt", [P, NB, P])
            states = sb("states", [P, NB, P])
        ot = sb("ot", [P, T])
        block = ctx.enter_context(nc.Block(no_gpsimd_drain=True))

        @block.sync
        def _(sp):
            if linear:
                if it is not None:
                    sp.wait_ge(k.stale["stored"], 16)
                k.zero_stale(sp, s)
                sp.sem_clear(k.tokens)
                ahead = x_in[bass.ds((it + 1) % passes, 1)]
                sp.dma_start(k.tok_in[:], ahead.rearrange("o (j p) d -> p (o j) d", p=P)).then_inc(k.tokens, 16)
            else:
                k.zero_stale(sp, s)

        @block.tensor
        def _(pe):
            pe.wait_ge(k.loaded, 16)
            pe.wait_ge(k.half_loaded, 16)
            pe.wait_ge(k.w_loaded[G], 16)
            norm_tensor(k, pe, s)
            names = ["wq", "wk"] if linear else ["wq", "wqf", "wk", "wkf"]
            for n, name in enumerate(names):
                pe.matmul(k.bank[n][:], w(name), k.xn[:], start=True, stop=True).then_inc(s["proj"], 1)
            for j in range(NT):
                ins = pe.matmul(k.bank[4][:, j * P:(j + 1) * P], k.xn[:, j * P:(j + 1) * P], w("wv"),
                                start=True, stop=True)
            ins.then_inc(s["proj"], 1)
            keep_clock(k, pe, WARM["features"] if linear else WARM["rotary"])

            def scores(i):
                b, c, jj = stages[i]
                pe.wait_ge(s["qk"], c + 1)
                if i >= 2:
                    pe.wait_ge(s["probs" if linear else "probs_in"], i - 1)
                for m in range(2):
                    j = 2 * jj + m
                    r = slice(32 * j, 32 * j + 32)
                    t0, o = b * L, k.bank[2 * (i % 2) + m]
                    if linear:
                        for t in range(2):
                            cols = slice(t0 + t * P, t0 + (t + 1) * P)
                            ins = pe.matmul(o[:, t * P:(t + 1) * P], km[r, c, cols], q[r, cols],
                                            start=True, stop=True)
                    else:
                        pe.matmul(o[:, 0:P], q[r, t0:t0 + P], km[r, c, t0:t0 + P], start=True, stop=True)
                        ins = pe.matmul(o[:, P:P + L], q[r, t0 + P:t0 + L], km[r, c, t0:t0 + L],
                                        start=True, stop=True)
                ins.then_inc(s["scores"], 1)

            def turn(i):
                pe.wait_ge(s["probs"], i + 1)
                if i >= 1:
                    pe.wait_ge(s["pt"], i)
                for m in range(2):
                    for n in range(3):
                        ins = pe.transpose(k.bank[4 + m][:, n * P:(n + 1) * P],
                                           pin[:, i % 2, m, n * P:(n + 1) * P], k.c("ident"))
                ins.then_inc(s["turned"], 1)

            def turn_shares():
                pe.wait_ge(s["wide"], 1)
                for j in range(NT):
                    ins = pe.transpose(k.bank[7][:, j * P:(j + 1) * P],
                                       wide[:, j].rearrange("p h e -> p (h e)"), k.c("ident"))
                ins.then_inc(s["wide_t"], 1)

            def weigh(i):
                b, c, jj = stages[i]
                pe.wait_ge(s["probs" if linear else "pt"], i + 1)
                for m in range(2):
                    head = 4 * (2 * jj + m) + c
                    p, first, last = pt[:, i % 2, m, :], c == jj == m == 0, head == 4 * 3 + 3
                    v = lambda tile: vm[:, tile, head * P:(head + 1) * P]
                    if linear:
                        for t in range(2):
                            ins = pe.matmul(k.bank[6][:, b * L + t * P:b * L + (t + 1) * P], v(2 * b + t),
                                            p[:, t * P:(t + 1) * P], start=first and t == 0, stop=last,
                                            skip_group_check=True)
                        continue
                    pe.matmul(k.bank[6][:, b * L:(b + 1) * L], v(2 * b), p[:, 0:L], start=first, stop=False,
                              skip_group_check=True)
                    ins = pe.matmul(k.bank[6][:, b * L + P:(b + 1) * L], v(2 * b + 1), p[:, L:L + P],
                                    start=False, stop=last, skip_group_check=True)
                ins.then_inc(s["pv"], 1)

            scores(0)
            scores(1)
            pe.wait_ge(s["vcopy"], 1)
            if linear:
                for b in range(NB):
                    ins = pe.transpose(k.bank[7][:, b * P:(b + 1) * P], kk[:, b * L:b * L + P], k.c("ident"))
                ins.then_inc(s["k_turned"], 1)
                for i in range(NS):
                    weigh(i)
                    if i + 2 < NS:
                        scores(i + 2)
                    if i == 0:
                        pe.wait_ge(s["k_tokens"], 1)
                        for b in range(NB):
                            ins = pe.matmul(k.bank[7][:, (2 + b) * P:(3 + b) * P], kt[:, b, :], vt[:, b, :],
                                            start=True, stop=True)
                        ins.then_inc(s["state"], 1)
                    if i == 7:
                        turn_shares()
                    if i in (3, NS // 2 + 1):
                        pe.wait_ge(s["states"], 1)
                        b = 2 * i // NS
                        pe.matmul(k.bank[6][:, b * L + P:(b + 1) * L], states[:, b, :], q[:, b * L + P:(b + 1) * L],
                                  start=False, stop=False, skip_group_check=True)
                    if i == 1:
                        pe.wait_ge(s["prod"], 1)
                        for j in range(NT):
                            ins = pe.matmul(k.bank[5][:, j * H:(j + 1) * H], t1[:, j * P:(j + 1) * P],
                                            k.c("heads"), start=True, stop=True)
                        ins.then_inc(s["sums"], 1)
            else:
                turn(0)
                for i in range(NS):
                    if i + 2 < NS:
                        scores(i + 2)
                    if i + 1 < NS:
                        turn(i + 1)
                    weigh(i)
            if not linear:
                turn_shares()
            pe.wait_ge(s["ot"], 1)
            pe.matmul(k.bank[0][:], w("wo"), ot[:], start=True, stop=True).then_inc(s["y"], 1)
            keep_clock(k, pe, WARM["residual"], bank=3)

        @block.gpsimd
        def _(pool):
            pool.memset(vm[:], 0.0).then_inc(s["cleared"], 1)

        @block.scalar
        def _(act):
            act.wait_ge(k.loaded, 16)
            norm_scalar(k, act, s, None)
            if linear:
                for n, t in enumerate((t1, t2)):
                    act.wait_ge(s["low"], n + 1)
                    act.activation(t[:], t[:], ACT.Exp).then_inc(s["high"], 1)
            act.wait_ge(s["cleared"], 1)
            act.wait_ge(s["proj"], 3 if linear else 5)
            act.activation(by_head, k.bank[4][:].rearrange("p (t h e) -> p t h e", t=NT, h=H),
                           ACT.Copy).then_inc(s["vcopy"], 1)
            if linear:
                act.activation(vt[:], k.bank[4][:].rearrange("p (b t e) -> p b t e", b=NB, t=2)[:, :, 0, :], ACT.Copy)
                act.wait_ge(s["k_turned"], 1)
                act.activation(kt[:].rearrange("p b e -> p (b e)"), k.bank[7][:, 0:NB * P], ACT.Copy) \
                    .then_inc(s["k_tokens"], 1)
            if not linear:
                for i in range(NS):
                    b, c, jj = stages[i]
                    act.wait_ge(s["probs_in"], i + 1)
                    for m in range(2):
                        for t, cols in enumerate((slice(0, P), slice(P, 3 * P))):
                            head = 4 * (2 * jj + m) + c
                            ins = act.activation(pin[:, i % 2, m, cols], pin[:, i % 2, m, cols], ACT.Exp,
                                                 bias=low[:, i % 2, 2 * m + t:2 * m + t + 1], scale=-1.0,
                                                 accum_out=den[:, 2 * b + t, head:head + 1])
                    ins.then_inc(s["probs"], 1)
            act.wait_ge(s["wide_t"], 1)
            act.activation(t2[:], k.bank[7][:], ACT.Copy).then_inc(s["wide_t"], 1)

        @block.vector
        def _(dve):
            link = chained(dve, s["dve"])
            dve.wait_ge(k.loaded, 16)
            norm_vector(k, dve, s)
            if linear:
                for n, t in enumerate((t1, t2)):
                    dve.wait_ge(s["proj"], n + 1)
                    dve.tensor_scalar(t[:], k.bank[n][:], 0.0, None, ALU.min).then_inc(s["low"], 1)
                for n, (t, o) in enumerate(((t1, q), (t2, kk))):
                    dve.wait_ge(s["high"], n + 1)
                    link(dve.scalar_tensor_tensor(o[:], k.bank[n][:], 0.0, t[:], ALU.max, ALU.add))
            else:
                rope = [(q, 0, 1, "cosq", "sinq"), (kk, 2, 3, "cosk", "sink")]
                for o, a, f, cos, sin in rope:
                    dve.wait_ge(s["proj"], f + 1)
                    table = lambda name: spread(k.c(name), [P, NB, L], 1)
                    two = lambda ap: ap.rearrange("p (b t) -> p b t", b=NB)
                    link(dve.tensor_tensor(two(t1[:]), two(k.bank[a][:]), table(cos), ALU.mult))
                    link(dve.tensor_tensor(two(t2[:]), two(k.bank[f][:]), table(sin), ALU.mult))
                    link(dve.tensor_tensor(o[:], t1[:], t2[:], ALU.add))
            for c in range(4):
                dve.tensor_scalar(km[:, c, :], kk[:], k.c("rows")[:, c:c + 1], None, ALU.mult).then_inc(s["qk"], 1)

            def shares():
                link(dve.reciprocal(den[:], den[:]))
                dve.tensor_copy(wide[:], spread(den[:], [P, NT, H, DA], 3)).then_inc(s["wide"], 1)

            for i in range(NS + 1):
                if i < NS:
                    dve.wait_ge(s["scores"], i + 1)
                    if linear:
                        if i >= 2:
                            dve.wait_ge(s["pv"], i - 1)
                        dve.tensor_tensor(
                            pt[:, i % 2, :, 0:L].rearrange("p m (t q) -> p m t q", t=2),
                            k.banks[:, 2 * (i % 2):2 * (i % 2) + 2, 0:L].rearrange("p m (t q) -> p m t q", t=2),
                            k.c("tri")[:, 0:P].unsqueeze(1).unsqueeze(1).broadcast_to([P, 2, 2, P]),
                            ALU.mult).then_inc(s["probs"], 1)
                    else:
                        if i >= 2:
                            dve.wait_ge(s["turned"], i - 1)
                        for m in range(2):
                            for t, cols in enumerate((slice(0, P), slice(P, 3 * P))):
                                ins = dve.tensor_tensor_reduce(
                                    pin[:, i % 2, m, cols], k.bank[2 * (i % 2) + m][:, cols],
                                    k.c("trib")[:, cols], 1.0, 3e38, ALU.add, ALU.min,
                                    low[:, i % 2, 2 * m + t:2 * m + t + 1])
                        ins.then_inc(s["probs_in"], 1)
                if linear and i == 1:
                    dve.wait_ge(s["state"], 1)
                    own = k.c("heads").unsqueeze(1).unsqueeze(3).broadcast_to([P, NB, H, DA])
                    dve.tensor_tensor(states[:].rearrange("p b (h e) -> p b h e", h=H),
                                      k.bank[7][:, 2 * P:4 * P].rearrange("p (b h e) -> p b h e", b=NB, h=H),
                                      own, ALU.mult).then_inc(s["states"], 1)
                if linear and i == 5:
                    dve.wait_ge(s["sums"], 1)
                    link(dve.tensor_scalar(den[:].rearrange("p t h -> p (t h)"), k.bank[5][:, 0:NT * H], 1e-6, None,
                                           ALU.max))
                    shares()
                if linear and i == 0:
                    for b in range(NB):
                        cols = slice(b * L, (b + 1) * L)
                        link(dve.tensor_tensor_scan(t2[:, cols], k.c("ones"), kk[:, cols], 0.0, ALU.mult, ALU.add))
                    dve.tensor_tensor(t1[:], t2[:], q[:], ALU.mult).then_inc(s["prod"], 1)
                if i >= 1 and not linear:
                    dve.wait_ge(s["turned"], i)
                    if i >= 3:
                        dve.wait_ge(s["pv"], i - 2)
                    for m in range(2):
                        ins = dve.tensor_copy(pt[:, (i - 1) % 2, m, :], k.bank[4 + m][:, 0:3 * P])
                    ins.then_inc(s["pt"], 1)
            if not linear:
                dve.wait_ge(s["probs"], NS)
                shares()
            dve.wait_ge(s["pv"], NS)
            dve.wait_ge(s["wide_t"], 2)
            dve.tensor_tensor(ot[:], k.bank[6][:], t2[:], ALU.mult).then_inc(s["ot"], 1)
            dve.wait_ge(s["y"], 1)
            dve.tensor_tensor(k.x[:], k.x[:], k.bank[0][:], ALU.add).then_inc(s["done"], 1)


ROUTE = ["logits", "r_diff", "r_exp", "r_split", "r_turned", "r_rows", "r_count"]


def route_logits(k, pe, s, g, experts):
    for j in range(NT):
        ins = pe.matmul(k.bank[6][:, j * experts:(j + 1) * experts], k.xn[:, j * P:(j + 1) * P], k.w(g, "gate"),
                        start=True, stop=True)
    ins.then_inc(s["logits"], 1)


def route_counts(k, pe, s, experts, mask):
    pe.wait_ge(s["r_count"], 1)
    pe.wait_ge(s["r_diff"], 1)
    for j in range(NT + 1):
        out = k.bank[6][:, j * experts:(j + 1) * experts]
        for i in range(min(j, NT)):
            ins = pe.matmul(out, k.h("ones"), mask[:, i, :], start=(i == 0), stop=(i == j - 1 and j == NT))
        if j < NT:
            ins = pe.matmul(out, k.h("lower"), mask[:, j, :], start=(j == 0), stop=True)
    ins.then_inc(s["r_count"], 1)


def route_turn(k, pe, s, split):
    pe.wait_ge(s["r_split"], 1)
    rows = split.shape[2]
    turned = k.bank[7][:].bitcast(BF16)
    for j in range(NT):
        ins = pe.transpose(turned[0:rows, j * P:(j + 1) * P], split[:, j, :], k.h("identb"))
    ins.then_inc(s["r_turned"], 1)


def route_vector(k, dve, s, link, buf, experts, choices, bias, seg, cap, meanwhile):
    E = experts
    logits = k.bank[6][:, 0:NT * E].rearrange("p (j e) -> p j e", e=E)
    full = [P, NT, E]
    dve.wait_ge(s["logits"], 1)
    link(dve.tensor_reduce(buf["top"][:], logits, AX_X, ALU.max))
    dve.tensor_tensor(buf["diff"][:], logits, spread(buf["top"][:], full, 2), ALU.subtract).then_inc(s["r_diff"], 1)
    meanwhile(0)
    dve.wait_ge(s["r_exp"], 1)
    link(dve.tensor_reduce(buf["sum"][:], buf["exp"][:], AX_X, ALU.add))
    link(dve.reciprocal(buf["sum"][:], buf["sum"][:]))
    link(dve.tensor_tensor(buf["score"][:], buf["exp"][:], spread(buf["sum"][:], full, 2), ALU.mult))
    ranked = buf["score"]
    if bias is not None:
        ranked = buf["diff"]
        link(dve.tensor_tensor(ranked[:], buf["score"][:], spread(bias, full, 1), ALU.add))
    for j in range(NT):
        ins = dve.max(buf["best"][:, j, :], ranked[:, j, :])
    link(ins)
    last = spread(buf["best"][:, :, choices - 1], full, 2)
    link(dve.tensor_tensor(buf["over"][:], ranked[:], last, ALU.is_gt))
    link(dve.tensor_reduce(buf["top"][:], buf["over"][:], AX_X, ALU.add))
    link(dve.tensor_scalar(buf["top"][:], buf["top"][:], -1.0, float(choices), ALU.mult, ALU.add))
    link(dve.tensor_tensor(buf["equal"][:], ranked[:], last, ALU.is_equal))
    flat = lambda b: b[:].rearrange("p j e -> p (j e)")
    link(dve.tensor_tensor_scan(flat(buf["rank"]), k.c(seg), flat(buf["equal"]), 0.0, ALU.mult, ALU.add))
    link(dve.tensor_tensor(buf["rank"][:], buf["rank"][:], spread(buf["top"][:], full, 2), ALU.is_le))
    link(dve.tensor_tensor(buf["equal"][:], buf["equal"][:], buf["rank"][:], ALU.mult))
    link(dve.tensor_tensor(buf["over"][:], buf["over"][:], buf["equal"][:], ALU.add))
    cw = buf["cw"][:, :, 0:E]
    link(dve.tensor_tensor(cw, buf["score"][:], buf["over"][:], ALU.mult))
    if cap:
        dve.tensor_copy(buf["mask"][:], buf["over"][:]).then_inc(s["r_count"], 1)
        link(dve.tensor_reduce(buf["sum"][:], cw, AX_X, ALU.add))
        link(dve.reciprocal(buf["sum"][:], buf["sum"][:]))
        link(dve.tensor_tensor(cw, cw, spread(buf["sum"][:], full, 2), ALU.mult))
        meanwhile(1)
        dve.wait_ge(s["r_count"], 2)
        link(dve.tensor_tensor(buf["rank"][:], logits, spread(buf["base"], full, 1), ALU.add))
        link(dve.tensor_scalar(buf["rank"][:], buf["rank"][:], float(CAP), None, ALU.is_le))
        dve.tensor_tensor(buf["base"], buf["base"], k.bank[6][:, NT * E:(NT + 1) * E], ALU.add)
        link(dve.tensor_tensor(cw, cw, buf["rank"][:], ALU.mult))
    else:
        meanwhile(1)
    W = buf["cw"].shape[2]
    part = lambda n: buf["split"][:, :, n * W:(n + 1) * W]
    link(dve.tensor_copy(part(0), buf["cw"][:]))
    link(dve.tensor_tensor(buf["rest"][:], buf["cw"][:], part(0), ALU.subtract))
    link(dve.tensor_copy(part(1), buf["rest"][:]))
    link(dve.tensor_tensor(buf["rest"][:], buf["rest"][:], part(1), ALU.subtract))
    dve.tensor_copy(part(2), buf["rest"][:]).then_inc(s["r_split"], 1)
    meanwhile(2)
    dve.wait_ge(s["r_turned"], 1)
    rows = 3 * W
    dve.tensor_copy(buf["rows"][0:rows, :], k.bank[7][:].bitcast(BF16)[0:rows, 0:T]).then_inc(s["r_rows"], 1)


def route_buffers(sb, experts, width, base):
    full = [P, NT, experts]
    buf = {n: sb("r_" + n, full) for n in ("diff", "exp", "score", "over", "equal", "rank")}
    buf["best"] = sb("r_best", [P, NT, 8])
    buf["top"], buf["sum"] = sb("r_top", [P, NT]), sb("r_sum", [P, NT])
    buf["cw"], buf["rest"] = sb("r_cw", [P, NT, width]), sb("r_rest", [P, NT, width])
    buf["split"] = sb("r_split", [P, NT, 3 * width], BF16)
    buf["rows"] = sb("r_rows", [P, T], BF16)
    buf["mask"] = sb("r_mask", full, BF16)
    buf["base"] = base
    return buf


def biased_ffn(k, tag):
    nc = k.nc
    G, N, W = 1, E0 + 1, E0 + 1
    CW = (4, 6)
    s = k.semaphores("ffn0", ["dve", "h", "cw", "h1", "h3", "gate", "linear", "tanh", "act", "down",
                                            "b2", "done"], "ffn", NORM + CUT + ROUTE)
    w = lambda name: k.w(G, name)
    with ExitStack() as ctx:
        def sb(name, shape, dt=F32):
            return ctx.enter_context(nc.sbuf_tensor(f"ffn0_{name}{tag}", shape, dt))
        buf = route_buffers(sb, E0, W, None)
        s1 = [sb(f"s1{c}", [P, 2, T]) for c in "gl"]
        hg, hl = sb("hg", [P, 2, T]), sb("hl", [P, 2, T])
        th = sb("th", [P, 2, T])
        p1 = sb("p1", [P, T])
        a = sb("a", [P, 2, T])
        cwr = sb("cwr", [P, T])
        x_high, x_low = sb("x_high", [P, T], F32R), sb("x_low", [P, T], F32R)
        block = ctx.enter_context(nc.Block(no_gpsimd_drain=True))

        @block.sync
        def _(sp):
            k.zero_stale(sp, s)

        @block.tensor
        def _(pe):
            pe.wait_ge(k.loaded, 16)
            pe.wait_ge(k.half_loaded, 16)
            pe.wait_ge(k.w_loaded[G], 16)
            norm_tensor(k, pe, s)

            def up(e):
                for n, (name, freed) in enumerate((("w1g", "h1"), ("w3g", "h3"), ("w1l", "h1"), ("w3l", "h3"))):
                    if e >= 1:
                        pe.wait_ge(s[freed], 2 * (e - 1) + n // 2 + 1)
                    cut_product(pe, k.bank[n][:], k.up_parts(0, f"{name}{e}"), (x_high[:], x_low[:])) \
                        .then_inc(s["h"], 1)

            def spread_weights(e):
                if e >= 2:
                    pe.wait_ge(s["act"], e - 1)
                pe.matmul(k.bank[CW[e % 2]][:], k.h("sel0")[0:3 * W, e * P:(e + 1) * P], buf["rows"][0:3 * W, :],
                          start=True, stop=True).then_inc(s["cw"], 1)

            def down(e):
                pe.wait_ge(s["act"], e + 1)
                pe.matmul(k.bank[5][:], w(f"w2{e}"), a[:, e % 2, :], start=(e == 0), stop=False) \
                    .then_inc(s["down"], 1)

            route_logits(k, pe, s, G, E0)
            pe.wait_ge(s["x_low"], NB)
            for e in range(3):
                up(e)
            route_turn(k, pe, s, buf["split"])
            pe.wait_ge(s["r_rows"], 1)
            spread_weights(0)
            for e in range(1, N):
                if e + 2 < N:
                    up(e + 2)
                spread_weights(e)
                down(e - 1)
            for j in range(NT):
                ins = pe.transpose(k.bank[7][0:W, j * P:(j + 1) * P], buf["cw"][:, j, :], k.c("ident"))
            ins.then_inc(s["b2"], 1)
            down(N - 1)
            pe.wait_ge(s["b2"], 2)
            pe.matmul(k.bank[5][:], w("b2")[0:W, :], cwr[0:W, :], start=False, stop=True).then_inc(s["down"], 1)
            keep_clock(k, pe, WARM["residual"], bank=3)

        @block.scalar
        def _(act):
            act.wait_ge(k.loaded, 16)
            act.wait_ge(k.w_loaded[G], 16)
            norm_scalar(k, act, s, None)
            cut_scalar(k, act, s, x_high)
            act.preload_act_table_set("exp_and_others")

            def first(e, c):
                act.wait_ge(s["h"], 4 * e + 2 * c + 1)
                if e >= 2:
                    act.wait_ge(s["h3"], 2 * (e - 2) + c + 1)
                act.activation(s1[c][:, e % 2, :], k.bank[2 * c][:], ACT.Identity,
                               bias=w("b1" + "gl"[c])[:, e:e + 1]).then_inc(s["h1"], 1)

            first(0, 0)
            act.wait_ge(s["r_diff"], 1)
            act.activation(buf["exp"][:], buf["diff"][:], ACT.Exp).then_inc(s["r_exp"], 1)
            first(0, 1)
            for e in range(N):
                if e + 1 < N:
                    first(e + 1, 0)
                    first(e + 1, 1)
                act.wait_ge(s["gate"], e + 1)
                if e >= 2:
                    act.wait_ge(s["act"], e - 1)
                act.activation(th[:, e % 2, :], hg[:, e % 2, :], ACT.Tanh, scale=ALPHA / 2).then_inc(s["tanh"], 1)
            act.preload_act_table_set("natural_log_exp_and_others")
            act.wait_ge(s["b2"], 1)
            act.activation(cwr[0:W, :], k.bank[7][0:W, :], ACT.Copy).then_inc(s["b2"], 1)

        @block.gpsimd
        def _(pool):
            for e in range(N):
                pool.wait_ge(s["h3"], 2 * e + 1)
                pool.tensor_scalar(hg[:, e % 2, :], hg[:, e % 2, :], LIMIT, None, ALU.min).then_inc(s["gate"], 1)
                pool.wait_ge(s["h3"], 2 * e + 2)
                pool.tensor_scalar(hl[:, e % 2, :], hl[:, e % 2, :], 1.0, LIMIT + 1.0, ALU.add, ALU.min) \
                    .then_inc(s["linear"], 1)

        @block.vector
        def _(dve):
            link = chained(dve, s["dve"])
            dve.wait_ge(k.loaded, 16)
            dve.wait_ge(k.w_loaded[G], 16)
            norm_vector(k, dve, s)
            cut_vector(k, dve, s, x_high, x_low)
            link(dve.memset(buf["cw"][:, :, E0:W], 1.0))

            def hidden(e):
                for c, h in enumerate((hg, hl)):
                    dve.wait_ge(s["h1"], 2 * e + c + 1)
                    dve.wait_ge(s["h"], 4 * e + 2 * c + 2)
                    dve.scalar_tensor_tensor(h[:, e % 2, :], k.bank[2 * c + 1][:], w("b3" + "gl"[c])[:, e:e + 1],
                                             s1[c][:, e % 2, :], ALU.add, ALU.mult).then_inc(s["h3"], 1)

            def meanwhile(n):
                if n < 2:
                    hidden(n)

            route_vector(k, dve, s, link, buf, E0, K0, w("gate_b"), "seg0", False, meanwhile)
            for e in range(N):
                dve.wait_ge(s["tanh"], e + 1)
                link(dve.scalar_tensor_tensor(p1[:], th[:, e % 2, :], 1.0, hg[:, e % 2, :], ALU.add, ALU.mult))
                dve.wait_ge(s["linear"], e + 1)
                link(dve.scalar_tensor_tensor(p1[:], hl[:, e % 2, :], 1.0 - LIMIT, p1[:], ALU.max, ALU.mult))
                if e + 2 < N:
                    hidden(e + 2)
                dve.wait_ge(s["cw"], e + 1)
                if e >= 2:
                    dve.wait_ge(s["down"], e - 1)
                dve.tensor_tensor(a[:, e % 2, :], p1[:], k.bank[CW[e % 2]][:], ALU.mult).then_inc(s["act"], 1)
                dve.wait_ge(s["act"], e + 1)
            dve.wait_ge(s["down"], N + 1)
            dve.tensor_tensor(k.x[:], k.x[:], k.bank[5][:], ALU.add).then_inc(s["done"], 1)


def wide_attention(k, tag):
    nc = k.nc
    G, HP = 2, H // 2
    s = k.semaphores("wide", ["v", "v_act", "v_dve", "q", "qc", "q_low", "k", "kc", "k_low", "scores", "max", "probs",
                              "turned", "pt_act", "pt_dve", "pv", "outn", "ot", "ot_act", "ot_dve", "y", "dve", "done"],
                     "mixer", NORM)
    at, _ = k.group_at[G][0]["wqkv"]
    wcol = lambda n: k.weights[G][:, at + n * P:at + (n + 1) * P]
    stages = [(g, b) for g in range(HP) for b in range(NB)]
    NS = len(stages)
    with ExitStack() as ctx:
        def sb(name, shape, dt=F32):
            return ctx.enter_context(nc.sbuf_tensor(f"wide_{name}{tag}", shape, dt))
        q, kk = ([sb(f"{name}_{part}", [P, 2, T], F32R) for part in ("high", "low")] for name in "qk")
        va = sb("va", [P, NT, H, DB + 1])
        pin = sb("pin", [P, 2, 2, T])
        pt = sb("pt", [P, 2, 2, T])
        low = sb("low", [P, 2, 4])
        rden = sb("rden", [P, 2, 2])
        on = sb("on", [P, NT, H, DB])
        ot = sb("ot", [P, 2, T])
        block = ctx.enter_context(nc.Block(no_gpsimd_drain=True))
        out = k.bank[6][:, 0:4 * (DB + 1)].rearrange("p (t m e) -> p t m e", t=2, m=2)

        @block.sync
        def _(sp):
            k.zero_stale(sp, s)

        @block.tensor
        def _(pe):
            pe.wait_ge(k.loaded, 16)
            pe.wait_ge(k.half_loaded, 16)
            pe.wait_ge(k.w_loaded[G], 16)
            norm_tensor(k, pe, s)
            def project(g, which):
                if which == 0:
                    if g >= 1:
                        pe.wait_ge(s["k_low"], g)
                    pe.matmul(k.bank[7][:], wcol(g), k.xn[:], start=True, stop=True).then_inc(s["q"], 1)
                else:
                    pe.wait_ge(s["q_low"], g + 1)
                    pe.matmul(k.bank[7][:], wcol(HP + g), k.xn[:], start=True, stop=True).then_inc(s["k"], 1)

            for n in range(2 * NT):
                j, half = n // 2, n % 2
                if n in (0, 2, 4):
                    project(n // 4, n // 2 % 2)
                if n >= 6:
                    pe.wait_ge(s["v_act" if n % 2 == 0 else "v_dve"], (n - 6) // 2 + 1)
                first = at + (2 * H * DB) + half * 512
                pe.matmul(k.bank[n % 6][:], k.xn[:, j * P:(j + 1) * P], k.weights[G][:, first:first + 512],
                          start=True, stop=True).then_inc(s["v"], 1)

            def scores(i):
                g, b = stages[i]
                pe.wait_ge(s["k_low"], g + 1)
                if i >= 2:
                    pe.wait_ge(s["probs"], i - 1)
                else:
                    pe.wait_ge(s["v_act"], NT)
                    pe.wait_ge(s["v_dve"], NT)
                for m in range(2):
                    r = slice(64 * m, 64 * m + 64)
                    for t in range(2):
                        ins = cut_product(pe, k.bank[2 * (i % 2) + m][:, t * L:(t + 1) * L],
                                          [part[r, g % 2, b * L + t * P:b * L + (t + 1) * P] for part in q],
                                          [part[r, g % 2, b * L:(b + 1) * L] for part in kk])
                ins.then_inc(s["scores"], 1)

            def turn(i):
                pe.wait_ge(s["probs"], i + 1)
                if i >= 1:
                    pe.wait_ge(s["pt_act"], i)
                    pe.wait_ge(s["pt_dve"], i)
                for m in range(2):
                    for key in range(2):
                        for t in range(2):
                            ins = pe.transpose(k.bank[4 + m][:, key * L + t * P:key * L + (t + 1) * P],
                                               pin[:, i % 2, m, t * L + key * P:t * L + (key + 1) * P], k.c("ident"))
                ins.then_inc(s["turned"], 1)

            def weigh(i):
                g, b = stages[i]
                pe.wait_ge(s["pt_act"], i + 1)
                pe.wait_ge(s["pt_dve"], i + 1)
                if i >= 1:
                    pe.wait_ge(s["outn"], i)
                for m in range(2):
                    for t in range(2):
                        for key in range(2):
                            ins = pe.matmul(out[:, t, m, :], pt[:, i % 2, m, key * L + t * P:key * L + (t + 1) * P],
                                            va[:, 2 * b + key, 2 * g + m, :], start=(key == 0), stop=(key == 1))
                ins.then_inc(s["pv"], 1)

            for i in range(NS + 2):
                if i < NS:
                    scores(i)
                    if i + 3 < NS:
                        project((i + 3) // 2, (i + 3) % 2)
                if 1 <= i <= NS:
                    turn(i - 1)
                if i >= 2:
                    weigh(i - 2)
            pe.wait_ge(s["outn"], NS)
            for g in range(HP):
                if g >= 2:
                    pe.wait_ge(s["ot_act" if g % 2 == 0 else "ot_dve"], g // 2)
                for j in range(NT):
                    ins = pe.transpose(k.bank[g % 2][:, j * P:(j + 1) * P],
                                       on[:, j, 2 * g:2 * g + 2, :].rearrange("p h e -> p (h e)"), k.c("ident"))
                ins.then_inc(s["ot"], 1)
                if g >= 1:
                    last = g - 1
                    pe.wait_ge(s["ot_act" if last % 2 == 0 else "ot_dve"], last // 2 + 1)
                    pe.matmul(k.bank[7][:], k.w(G, "wout")[:, last * P:(last + 1) * P], ot[:, last % 2, :],
                              start=(last == 0), stop=False).then_inc(s["y"], 1)
            pe.wait_ge(s["ot_dve"], HP // 2)
            pe.matmul(k.bank[7][:], k.w(G, "wout")[:, (HP - 1) * P:], ot[:, 1, :],
                      start=False, stop=True).then_inc(s["y"], 1)
            keep_clock(k, pe, WARM["residual"], bank=3)

        @block.scalar
        def _(act):
            act.wait_ge(k.loaded, 16)
            norm_scalar(k, act, s, None)
            def copy_q(g):
                act.wait_ge(s["q"], g + 1)
                if g >= 2:
                    act.wait_ge(s["scores"], 2 * g - 2)
                act.activation(q[0][:, g % 2, :], k.bank[7][:], ACT.Copy, scale=float(DB) ** -0.5).then_inc(s["qc"], 1)

            def copy_k(g):
                act.wait_ge(s["k"], g + 1)
                if g >= 2:
                    act.wait_ge(s["scores"], 2 * g - 2)
                act.activation(kk[0][:, g % 2, :], k.bank[7][:], ACT.Copy).then_inc(s["kc"], 1)

            for n in range(0, 2 * NT, 2):
                if n in (0, 2, 4):
                    (copy_q, copy_k)[n // 2 % 2](n // 4)
                act.wait_ge(s["v"], n + 1)
                act.activation(va[:, n // 2, 0:8, 0:DB], k.bank[n % 6].rearrange("p (h e) -> p h e", e=DB),
                               ACT.Copy).then_inc(s["v_act"], 1)

            for i in range(NS + 1):
                if i < NS:
                    act.wait_ge(s["max"], i + 1)
                    if i >= 2:
                        act.wait_ge(s["turned"], i - 1)
                    for m in range(2):
                        for t in range(2):
                            cols = slice(t * L, (t + 1) * L)
                            ins = act.activation(pin[:, i % 2, m, cols], k.bank[2 * (i % 2) + m][:, cols], ACT.Exp,
                                                 bias=low[:, i % 2, 2 * m + t:2 * m + t + 1])
                    ins.then_inc(s["probs"], 1)
                    if i + 3 < NS:
                        (copy_q if (i + 3) % 2 == 0 else copy_k)((i + 3) // 2)
                if i >= 1:
                    act.wait_ge(s["turned"], i)
                    if i >= 3:
                        act.wait_ge(s["pv"], i - 2)
                    act.activation(pt[:, (i - 1) % 2, 0, :], k.bank[4][:], ACT.Copy).then_inc(s["pt_act"], 1)
            for g in range(0, HP, 2):
                act.wait_ge(s["ot"], g + 1)
                if g >= 2:
                    act.wait_ge(s["y"], g - 1)
                act.activation(ot[:, 0, :], k.bank[0][:], ACT.Copy).then_inc(s["ot_act"], 1)

        @block.vector
        def _(dve):
            link = chained(dve, s["dve"])
            dve.wait_ge(k.loaded, 16)
            norm_vector(k, dve, s)
            link(dve.memset(va[:, :, :, DB:DB + 1], 1.0))
            def low_part(g, which):
                (high, low), scale = ((q, float(DB) ** -0.5), (kk, 1.0))[which]
                dve.wait_ge(s["qc" if which == 0 else "kc"], g + 1)
                dve.scalar_tensor_tensor(low[:, g % 2, :], k.bank[7][:], scale, high[:, g % 2, :].bitcast(F32),
                                         ALU.mult, ALU.subtract).then_inc(s["q_low" if which == 0 else "k_low"], 1)

            for n in range(1, 2 * NT, 2):
                if n in (1, 3, 5):
                    low_part(n // 4, n // 2 % 2)
                dve.wait_ge(s["v"], n + 1)
                dve.tensor_copy(va[:, n // 2, 8:16, 0:DB], k.bank[n % 6].rearrange("p (h e) -> p h e", e=DB)) \
                    .then_inc(s["v_dve"], 1)
            for i in range(NS + 2):
                if i < NS:
                    dve.wait_ge(s["scores"], i + 1)
                    if i >= 2:
                        dve.wait_ge(s["probs"], i - 1)
                    dve.tensor_reduce(low[:, i % 2, :],
                                      k.banks[:, 2 * (i % 2):2 * (i % 2) + 2, :].rearrange("p m (t c) -> p (m t) c", c=L),
                                      AX_X, ALU.max, negate=True).then_inc(s["max"], 1)
                if 1 <= i <= NS:
                    dve.wait_ge(s["turned"], i)
                    if i >= 3:
                        dve.wait_ge(s["pv"], i - 2)
                    dve.tensor_copy(pt[:, (i - 1) % 2, 1, :], k.bank[5][:]).then_inc(s["pt_dve"], 1)
                if i + 3 < NS:
                    low_part((i + 3) // 2, (i + 3) % 2)
                if i >= 2:
                    g, b = stages[i - 2]
                    dve.wait_ge(s["pv"], i - 1)
                    link(dve.reciprocal(rden[:], out[:, :, :, DB]))
                    dve.tensor_tensor(on[:, 2 * b:2 * b + 2, 2 * g:2 * g + 2, :], out[:, :, :, 0:DB],
                                      spread(rden[:], [P, 2, 2, DB], 3), ALU.mult).then_inc(s["outn"], 1)
                    dve.wait_ge(s["outn"], i - 1)
            for g in range(1, HP, 2):
                dve.wait_ge(s["ot"], g + 1)
                if g >= 2:
                    dve.wait_ge(s["y"], g - 1)
                dve.tensor_copy(ot[:, 1, :], k.bank[1][:]).then_inc(s["ot_dve"], 1)
            dve.wait_ge(s["y"], HP)
            dve.tensor_tensor(k.x[:], k.x[:], k.bank[7][:], ALU.add).then_inc(s["done"], 1)


def capped_ffn(k, tag):
    nc = k.nc
    G, N = 4, E1 // 2 + 1
    CW = (4, 6)
    AHEAD = 4
    which = int(tag) // 7
    s = k.semaphores("ffn1", ["dve", "g", "u", "cw", "tanh", "g_read", "u_read", "act", "down", "done"],
                     "ffn", NORM + CUT + ROUTE)
    w = lambda name: k.w(G, name)
    with ExitStack() as ctx:
        def sb(name, shape, dt=F32):
            return ctx.enter_context(nc.sbuf_tensor(f"ffn1_{name}{tag}", shape, dt))
        buf = route_buffers(sb, E1, E1, k.base[:, which, :])
        th, p1, a = sb("th", [P, 2, T]), sb("p1", [P, AHEAD + 1, T]), sb("a", [P, 2, T])
        x_high, x_low = sb("x_high", [P, T], F32R), sb("x_low", [P, T], F32R)
        block = ctx.enter_context(nc.Block(no_gpsimd_drain=True))

        @block.sync
        def _(sp):
            k.zero_stale(sp, s)

        @block.tensor
        def _(pe):
            pe.wait_ge(k.loaded, 16)
            pe.wait_ge(k.half_loaded, 16)
            pe.wait_ge(k.w_loaded[G], 16)
            norm_tensor(k, pe, s)

            def up(n):
                for m, sem in enumerate("gu"):
                    if n >= 2:
                        pe.wait_ge(s[sem + "_read"], n - 1)
                    out = k.bank[2 * m + n % 2]
                    if n == 0:
                        ins = pe.matmul(out[0:64, :], w("s" + sem), k.xn[:], start=True, stop=True)
                    else:
                        ins = cut_product(pe, out, k.up_parts(1, f"{sem}{n - 1}"), (x_high[:], x_low[:]))
                    ins.then_inc(s[sem], 1)

            def spread_weights(n):
                if n >= 3:
                    pe.wait_ge(s["act"], n - 1)
                pe.matmul(k.bank[CW[n % 2]][:], k.h("sel1")[0:3 * E1, (n - 1) * P:n * P], buf["rows"][0:3 * E1, :],
                          start=True, stop=True).then_inc(s["cw"], 1)

            def down(n):
                pe.wait_ge(s["act"], n + 1)
                rows = 64 if n == 0 else P
                pe.matmul(k.bank[5][:], w("sd" if n == 0 else f"d{n - 1}")[0:rows, :], a[0:rows, n % 2, :],
                          start=(n == 0), stop=(n == N - 1)).then_inc(s["down"], 1)

            route_logits(k, pe, s, G, E1)
            up(0)
            pe.wait_ge(s["x_low"], NB)
            up(1)
            up(2)
            route_counts(k, pe, s, E1, buf["mask"])
            up(3)
            down(0)
            route_turn(k, pe, s, buf["split"])
            up(4)
            pe.wait_ge(s["r_rows"], 1)
            spread_weights(1)
            for n in range(2, N):
                if n + 3 < N:
                    up(n + 3)
                spread_weights(n)
                down(n - 1)
            down(N - 1)
            keep_clock(k, pe, WARM["residual"], bank=3)

        @block.scalar
        def _(act):
            act.wait_ge(k.loaded, 16)
            norm_scalar(k, act, s, None)
            cut_scalar(k, act, s, x_high)
            act.preload_act_table_set("exp_and_others")
            for n in range(N):
                rows = 64 if n == 0 else P
                act.wait_ge(s["g"], n + 1)
                if n >= 2:
                    act.wait_ge(s["g_read"], n - 1)
                act.activation(th[0:rows, n % 2, :], k.bank[n % 2][0:rows, :], ACT.Tanh, scale=0.5) \
                    .then_inc(s["tanh"], 1)
                if n == 0:
                    act.wait_ge(s["r_diff"], 1)
                    act.activation(buf["exp"][:], buf["diff"][:], ACT.Exp).then_inc(s["r_exp"], 1)
            act.preload_act_table_set("natural_log_exp_and_others")

        @block.vector
        def _(dve):
            link = chained(dve, s["dve"])
            dve.wait_ge(k.loaded, 16)
            norm_vector(k, dve, s)
            cut_vector(k, dve, s, x_high, x_low)

            def hidden(n):
                rows = slice(0, 64 if n == 0 else P)
                i, o = n % 2, p1[:, n % (AHEAD + 1), :]
                dve.wait_ge(s["tanh"], n + 1)
                dve.scalar_tensor_tensor(o[rows], th[rows, i, :], 1.0, k.bank[i][rows, :], ALU.add, ALU.mult) \
                    .then_inc(s["g_read"], 1)
                dve.wait_ge(s["g_read"], n + 1)
                dve.wait_ge(s["u"], n + 1)
                dve.tensor_tensor(o[rows], o[rows], k.bank[2 + i][rows, :], ALU.mult).then_inc(s["u_read"], 1)

            def weigh(n):
                o = p1[:, n % (AHEAD + 1), :]
                dve.wait_ge(s["u_read"], n + 1)
                if n >= 2:
                    dve.wait_ge(s["down"], n - 1)
                if n == 0:
                    dve.tensor_scalar(a[0:64, 0, :], o[0:64], 0.5, None, ALU.mult).then_inc(s["act"], 1)
                else:
                    dve.wait_ge(s["cw"], n)
                    dve.tensor_tensor(a[:, n % 2, :], o, k.bank[CW[n % 2]][:], ALU.mult).then_inc(s["act"], 1)

            def meanwhile(n):
                hidden(n)
                if n == 1:
                    weigh(0)
                if n == 2:
                    hidden(3)

            route_vector(k, dve, s, link, buf, E1, K1, None, "seg1", True, meanwhile)
            for n in range(1, N):
                if n + 3 < N:
                    hidden(n + 3)
                weigh(n)
            dve.wait_ge(s["down"], N)
            dve.tensor_tensor(k.x[:], k.x[:], k.bank[5][:], ALU.add).then_inc(s["done"], 1)


def state_space(k, tag):
    nc = k.nc
    G, NP = 5, 64
    AHEAD, HOLD = 3, 4
    DELTA, DELTA_X = (0, 1, 4), (2, 3, 6)
    s = k.semaphores("ssm", ["up", "left", "right", "tanh_r", "conv", "tanh_c", "x", "proj", "z", "e", "ln",
                                    "split", "packed0", "packed1", "packed2", "packed3", "bc", "cc", "a", "da",
                                    "dbx", "h", "hc", "red", "gated", "down", "dve", "acts", "done"], "mixer", NORM)
    w = lambda name: k.w(G, name)
    with ExitStack() as ctx:
        def sb(name, shape, dt=F32):
            return ctx.enter_context(nc.sbuf_tensor(f"ssm_{name}{tag}", shape, dt))
        left = sb("left", [P, NB, L + 2])
        right, gate = sb("right", [P, T]), sb("gate", [P, T])
        conv, tc, xs = sb("conv", [P, T]), sb("tc", [P, T]), sb("xs", [P, T])
        z, u, fix, delta = sb("z", [P, T]), sb("u", [P, T]), sb("fix", [P, T]), sb("delta", [P, T])
        e, ln, dx = tc, right, z
        parts = sb("parts", [P, 2, 3, T], BF16)
        packed = sb("packed", [P, 2, 4, T], BF16)
        bm, cm = sb("bm", [P, T]), sb("cm", [P, T])
        da, dbx = sb("da", [P, AHEAD, T]), sb("dbx", [P, AHEAD, T])
        h, hc = sb("h", [P, HOLD, T]), sb("hc", [P, HOLD, T])
        block = ctx.enter_context(nc.Block(no_gpsimd_drain=True))
        two = lambda ap: ap.rearrange("p (b t) -> p b t", b=NB)

        def spot(p):
            return p // 16, p % 16

        @block.sync
        def _(sp):
            k.zero_stale(sp, s)
            sp.wait_ge(s["split"], 6)
            for g in range(4):
                for part in range(3):
                    sp.dma_start(packed[32 * part:32 * part + 32, :, g, :], parts[32 * g:32 * g + 32, :, part, :]) \
                        .then_inc(s[f"packed{g}"], 16)

        @block.tensor
        def _(pe):
            pe.wait_ge(k.loaded, 16)
            pe.wait_ge(k.half_loaded, 16)
            pe.wait_ge(k.w_loaded[G], 16)
            norm_tensor(k, pe, s)
            pe.matmul(k.bank[0][:], w("left"), k.xn[:], start=True, stop=True).then_inc(s["up"], 1)
            pe.matmul(k.bank[1][:], w("right"), k.xn[:], start=True, stop=True).then_inc(s["up"], 1)
            keep_clock(k, pe, WARM["conv"])
            pe.wait_ge(s["x"], 1)
            for n, name in enumerate(("delta", "wb", "wc")):
                pe.matmul(k.bank[2 + n][:], w(name), xs[:], start=True, stop=True).then_inc(s["proj"], 1)
            keep_clock(k, pe, WARM["parts"])
            pe.wait_ge(s["cc"], 2)

            def spread_rows(p):
                g, c = spot(p)
                if c == 0:
                    pe.wait_ge(s[f"packed{g}"], 16 * 3)
                if p >= AHEAD:
                    pe.wait_ge(s["da"], p - AHEAD + 1)
                    pe.wait_ge(s["dbx"], p - AHEAD + 1)
                pick = k.h("pick")[0:96, c * P:(c + 1) * P]
                pe.matmul(k.bank[DELTA[p % AHEAD]][:], pick, packed[0:96, 0, g, :], start=True, stop=True) \
                    .then_inc(s["bc"], 1)
                pe.matmul(k.bank[DELTA_X[p % AHEAD]][:], pick, packed[0:96, 1, g, :], start=True, stop=True) \
                    .then_inc(s["bc"], 1)

            def reduce(p):
                g, c = spot(p)
                pe.wait_ge(s["hc"], p + 1)
                row = 32 * g + c
                pe.matmul(k.bank[5][:], k.c("hot")[:, P - row:2 * P - row], hc[:, p % HOLD, :],
                          start=(p == 0), stop=(p == NP - 1)).then_inc(s["red"], 1)

            for p in range(NP + HOLD):
                if p < NP:
                    spread_rows(p)
                if p >= HOLD:
                    reduce(p - HOLD)
            pe.wait_ge(s["gated"], 1)
            pe.matmul(k.bank[6][:], w("down"), conv[:], start=True, stop=True).then_inc(s["down"], 1)
            keep_clock(k, pe, WARM["residual"], bank=3)

        @block.scalar
        def _(act):
            link = chained(act, s["acts"])
            act.wait_ge(k.loaded, 16)
            act.wait_ge(k.w_loaded[G], 16)
            act.activation(k.a_neg[:], w("a_log"), ACT.Exp).then_inc(s["a"], 1)
            norm_scalar(k, act, s, "exp_and_others")
            act.wait_ge(s["up"], 1)
            act.activation(left[:, :, 2:L + 2], two(k.bank[0]), ACT.Identity, bias=w("b_left")).then_inc(s["left"], 1)
            act.wait_ge(s["up"], 2)
            act.activation(right[:], k.bank[1][:], ACT.Identity, bias=w("b_right")).then_inc(s["right"], 1)
            act.wait_ge(s["right"], 1)
            act.activation(gate[:], right[:], ACT.Tanh, scale=0.5).then_inc(s["tanh_r"], 1)
            act.wait_ge(s["conv"], 1)
            act.activation(tc[:], conv[:], ACT.Tanh, scale=0.5).then_inc(s["tanh_c"], 1)
            act.wait_ge(s["proj"], 1)
            act.activation(z[:], k.bank[2][:], ACT.Identity, bias=w("b_delta")).then_inc(s["z"], 1)
            act.preload_act_table_set("natural_log_exp_and_others")
            act.wait_ge(s["z"], 1)
            link(act.activation(e[:], z[:], ACT.Abs))
            act.activation(e[:], e[:], ACT.Exp, scale=-1.0).then_inc(s["e"], 1)
            act.wait_ge(s["proj"], 2)
            act.activation(bm[:], k.bank[3][:], ACT.Identity, bias=w("b_b")).then_inc(s["cc"], 1)
            act.wait_ge(s["proj"], 3)
            act.activation(cm[:], k.bank[4][:], ACT.Identity, bias=w("b_c")).then_inc(s["cc"], 1)
            act.wait_ge(s["e"], 2)
            act.activation(ln[:], u[:], ACT.Ln).then_inc(s["ln"], 1)
            act.wait_ge(s["a"], 2)
            for p in range(NP):
                act.wait_ge(s["bc"], 2 * p + 1)
                if p >= AHEAD:
                    act.wait_ge(s["h"], p - AHEAD + 1)
                act.activation(da[:, p % AHEAD, :], k.bank[DELTA[p % AHEAD]][:], ACT.Exp, scale=k.a_neg[:, p:p + 1]) \
                    .then_inc(s["da"], 1)

        @block.gpsimd
        def _(pool):
            pool.wait_ge(s["cc"], 2)
            for p in range(NP):
                pool.wait_ge(s["h"], p + 1)
                if p >= HOLD:
                    pool.wait_ge(s["red"], p - HOLD + 1)
                pool.tensor_tensor(hc[:, p % HOLD, :], h[:, p % HOLD, :], cm[:], ALU.mult).then_inc(s["hc"], 1)

        @block.vector
        def _(dve):
            link = chained(dve, s["dve"])
            dve.wait_ge(k.loaded, 16)
            dve.wait_ge(k.w_loaded[G], 16)
            norm_vector(k, dve, s)
            dve.wait_ge(s["a"], 1)
            dve.tensor_scalar(k.a_neg[:], k.a_neg[:], -1.0, None, ALU.mult).then_inc(s["a"], 1)
            link(dve.memset(left[:, :, 0:2], 0.0))
            dve.wait_ge(s["left"], 1)
            taps = w("conv_w")
            link(dve.tensor_scalar(two(conv[:]), left[:, :, 0:L], taps[:, 0:1], w("conv_b"), ALU.mult, ALU.add))
            link(dve.scalar_tensor_tensor(two(conv[:]), left[:, :, 1:L + 1], taps[:, 1:2], two(conv[:]),
                                          ALU.mult, ALU.add))
            dve.scalar_tensor_tensor(two(conv[:]), left[:, :, 2:L + 2], taps[:, 2:3], two(conv[:]),
                                     ALU.mult, ALU.add).then_inc(s["conv"], 1)
            dve.wait_ge(s["tanh_c"], 1)
            link(dve.scalar_tensor_tensor(xs[:], tc[:], 1.0, conv[:], ALU.add, ALU.mult))
            dve.tensor_scalar(xs[:], xs[:], 0.5, None, ALU.mult).then_inc(s["x"], 1)
            dve.wait_ge(s["x"], 1)
            dve.wait_ge(s["tanh_r"], 1)
            link(dve.scalar_tensor_tensor(gate[:], gate[:], 1.0, right[:], ALU.add, ALU.mult))
            dve.wait_ge(s["e"], 1)
            dve.tensor_scalar(u[:], e[:], 1.0, None, ALU.add).then_inc(s["e"], 1)
            dve.wait_ge(s["e"], 2)
            link(dve.scalar_tensor_tensor(fix[:], u[:], 1.0, e[:], ALU.subtract, ALU.subtract))
            dve.wait_ge(s["ln"], 1)
            link(dve.tensor_tensor(ln[:], ln[:], fix[:], ALU.subtract))
            link(dve.scalar_tensor_tensor(delta[:], z[:], 0.0, ln[:], ALU.max, ALU.add))
            link(dve.tensor_tensor(dx[:], delta[:], xs[:], ALU.mult))
            for which, v in enumerate((delta, dx)):
                dve.tensor_copy(parts[:, which, 0, :], v[:]).then_inc(s["split"], 1)
                dve.wait_ge(s["split"], 3 * which + 1)
                link(dve.tensor_tensor(fix[:], v[:], parts[:, which, 0, :], ALU.subtract))
                dve.tensor_copy(parts[:, which, 1, :], fix[:]).then_inc(s["split"], 1)
                dve.wait_ge(s["split"], 3 * which + 2)
                link(dve.tensor_tensor(fix[:], fix[:], parts[:, which, 1, :], ALU.subtract))
                dve.tensor_copy(parts[:, which, 2, :], fix[:]).then_inc(s["split"], 1)
                dve.wait_ge(s["split"], 3 * which + 3)
            dve.wait_ge(s["cc"], 1)
            for p in range(NP + 1):
                if p < NP:
                    dve.wait_ge(s["bc"], 2 * p + 2)
                    if p >= AHEAD:
                        dve.wait_ge(s["h"], p - AHEAD + 1)
                    dve.tensor_tensor(dbx[:, p % AHEAD, :], k.bank[DELTA_X[p % AHEAD]][:], bm[:], ALU.mult) \
                        .then_inc(s["dbx"], 1)
                if p >= 1:
                    n = p - 1
                    dve.wait_ge(s["dbx"], n + 1)
                    dve.wait_ge(s["da"], n + 1)
                    if n >= HOLD:
                        dve.wait_ge(s["hc"], n - HOLD + 1)
                    for b in range(NB):
                        cols = slice(b * L, (b + 1) * L)
                        ins = dve.tensor_tensor_scan(h[:, n % HOLD, cols], da[:, n % AHEAD, cols], dbx[:, n % AHEAD, cols], 0.0,
                                                     ALU.mult, ALU.add)
                    ins.then_inc(s["h"], 1)
            dve.wait_ge(s["red"], NP)
            link(dve.scalar_tensor_tensor(fix[:], xs[:], w("skip"), k.bank[5][:], ALU.mult, ALU.add))
            dve.scalar_tensor_tensor(conv[:], fix[:], 0.5, gate[:], ALU.mult, ALU.mult).then_inc(s["gated"], 1)
            dve.wait_ge(s["down"], 1)
            dve.scalar_tensor_tensor(k.x[:], k.bank[6][:], w("b_down"), k.x[:], ALU.add, ALU.add) \
                .then_inc(s["done"], 1)
def hybrid_kernel(nc, x_in, const_in, half_in, weights_in, up_in, x_out):
    with ExitStack() as ctx:
        k = Core(nc, ctx)
        a_log_at = k.group_at[5][0]["a_log"][0]
        step = 4 * P
        cuts = [(n, slice(at, at + step)) for n, (_, width) in enumerate(k.up_at) for at in range(0, width, step)]
        with ExitStack() as early:
            whole = [early.enter_context(nc.sbuf_tensor(f"up_whole{n}", [P, width], F32))
                     for n, (_, width) in enumerate(k.up_at)]
            block = early.enter_context(nc.Block(no_gpsimd_drain=True))

            @block.sync
            def _(sp):
                sp.dma_start(k.tok_in[:], x_in[0].rearrange("(j p) d -> p j d", p=P)).then_inc(k.tokens, 16)
                sp.dma_start(k.const[:], const_in).then_inc(k.loaded, 16)
                sp.dma_start(k.half[:], half_in).then_inc(k.half_loaded, 16)
                sp.dma_start(whole[0][:], up_in[0]).then_inc(k.up_loaded[0], 16)
                sp.dma_start(whole[1][:], up_in[1]).then_inc(k.up_loaded[1], 16)
                sp.dma_start(k.weights[0][:], weights_in[0]).then_inc(k.w_loaded[0], 16)
                sp.dma_start(k.weights[1][:], weights_in[1]).then_inc(k.w_loaded[1], 16)
                for g in range(2, 6):
                    sp.dma_start(k.weights[g][:], weights_in[g]).then_inc(k.w_loaded[g], 16)

            @block.scalar
            def _(act):
                act.preload_act_table_set("natural_log_exp_and_others")
                for n, cols in cuts:
                    act.wait_ge(k.up_loaded[n], 16)
                    act.activation(k.up_high[n][:, cols], whole[n][:, cols], ACT.Copy) \
                        .then_inc(k.up_cut, 1)

            @block.vector
            def _(dve):
                dve.memset(k.base[:], 0.0)
                for i, (n, cols) in enumerate(cuts):
                    dve.wait_ge(k.up_cut, i + 1)
                    dve.tensor_tensor(k.up_low[n][:, cols], whole[n][:, cols], k.up_high[n][:, cols].bitcast(F32),
                                      ALU.subtract)
        turn_tokens(k, x_out, None, "first")
        with nc.Fori(0, x_in.shape[0]) as it:
            for n, layer in enumerate(PLAN[:LAYERS]):
                layer(k, n, x_in, it)
            turn_tokens(k, x_out, it, "")
        with nc.Block(no_gpsimd_drain=True) as block:
            @block.sync
            def _(sp):
                sp.wait_ge(k.semaphores("turn", TURN)["stored"], 16)
                sp.wait_ge(k.tokens, 16)


PLAN = [lambda k, n, x_in, it: narrow_attention(k, n, True, x_in, it), lambda k, n, *_: biased_ffn(k, n),
        lambda k, n, *_: wide_attention(k, n), lambda k, n, *_: biased_ffn(k, n),
        lambda k, n, *_: narrow_attention(k, n, False), lambda k, n, *_: capped_ffn(k, n),
        lambda k, n, *_: state_space(k, n), lambda k, n, *_: capped_ffn(k, n)]


def kernel(**inputs):
    import numpy as np
    import concourse.bacc as bacc
    from concourse.bass_utils import run_bass_kernel_spmd

    const_at, half_at, group_at = tables()
    v = {name: np.ascontiguousarray(a) for name, a in inputs.items()}
    f32 = np.dtype("float32")

    const = np.zeros((P, const_at[1]), f32)
    half = np.zeros((P, half_at[1]), f32)

    def put(packed, where, name, a, rows=slice(0, P)):
        at, width = where[name]
        packed[rows, at:at + width] = a

    idx = np.arange(P)
    tri = (idx[:, None] <= idx[None, :])
    ones = np.ones((P, P), f32)
    put(const, const_at[0], "mean", ones / P)
    put(const, const_at[0], "centre", np.eye(P) - 1.0 / P)
    put(const, const_at[0], "ident", np.eye(P))
    put(const, const_at[0], "tri", np.concatenate([tri, ones, tri], 1))
    hide = np.where(tri.T, 0.0, BIG)
    put(const, const_at[0], "trib", np.concatenate([hide, hide * 0, hide], 1))
    pair = (idx % DA) % (DA // 2)
    theta = (1.0 / np.float32(10000.0) ** (np.arange(0, DA, 2, dtype=f32) / np.float32(DA))).astype(f32)
    angle = (np.arange(L, dtype=f32)[None, :] * theta[pair][:, None]).astype(f32)
    sign = np.where(idx % DA < DA // 2, -1.0, 1.0)[:, None]
    scale = -1.0 / np.sqrt(np.float64(DA))
    cos, sin = np.cos(angle.astype(np.float64)), np.sin(angle.astype(np.float64)) * sign
    put(const, const_at[0], "cosq", cos * scale)
    put(const, const_at[0], "sinq", sin * scale)
    put(const, const_at[0], "cosk", cos)
    put(const, const_at[0], "sink", sin)
    hot = np.zeros((P, 2 * P), f32)
    hot[:64, P] = 1.0
    hot[64:, P + 16] = 1.0
    put(const, const_at[0], "hot", hot)
    put(const, const_at[0], "rows", (idx[:, None] // DA % 4 == np.arange(4)[None, :]))
    put(const, const_at[0], "eps", 1e-5)
    put(const, const_at[0], "ones", 1.0)
    put(const, const_at[0], "heads", (idx[:, None] // DA == np.arange(H)[None, :]))
    put(const, const_at[0], "seg0", np.tile(np.arange(E0) != 0, NT)[None, :])
    put(const, const_at[0], "seg1", np.tile(np.arange(E1) != 0, NT)[None, :])
    for e in range(E0 + 1):
        sel = np.zeros((P, P), f32)
        sel[[e, E0 + 1 + e, 2 * (E0 + 1) + e], :] = 0.5
        at = half_at[0]["sel0"][0] + e * P
        half[:, at:at + P] = sel
    for p in range(E1 // 2):
        sel = np.zeros((P, P), f32)
        for part in range(3):
            sel[part * E1 + 2 * p, :64] = 0.5
            sel[part * E1 + 2 * p + 1, 64:] = 0.5
        at = half_at[0]["sel1"][0] + p * P
        half[:, at:at + P] = sel
    for c in range(16):
        sel = np.zeros((P, P), f32)
        for part in range(3):
            sel[part * 32 + c, :64] = 1.0
            sel[part * 32 + 16 + c, 64:] = 1.0
        at = half_at[0]["pick"][0] + c * P
        half[:, at:at + P] = sel
    put(half, half_at[0], "lower", tri)
    put(half, half_at[0], "ones", 1.0)
    put(half, half_at[0], "identb", np.eye(P))
    half = half.astype(np.dtype("bfloat16"))

    packs = [np.zeros((P, width), f32) for _, width in group_at]

    ups = [np.zeros((P, width), f32) for _, width in up_tables()]

    def lay_up(n, name, a):
        at, width = up_tables()[n][0][name]
        ups[n][:, at:at + width] = a

    def lay(g, name, a):
        at, width = group_at[g][0][name]
        packs[g][:a.shape[0], at:at + width] = a

    for name, key in (("wq", "Wq"), ("wk", "Wk"), ("wv", "Wv"), ("wo", "Wo")):
        lay(0, name, v[f"L0_attn_a_{key}"].T)
    lay(1, "gate", v["L0_ffn_gate_w"].T)
    lay(1, "gate_b", np.broadcast_to(v["L0_ffn_gate_b"], (P, E0)))
    lay(1, "b2", np.concatenate([v["L0_ffn_b2"], v["L0_ffn_sb2"][None]], 0))
    w1 = np.concatenate([v["L0_ffn_w1"], v["L0_ffn_sw1"][None]], 0)
    w3 = np.concatenate([v["L0_ffn_w3"], v["L0_ffn_sw3"][None]], 0)
    w2 = np.concatenate([v["L0_ffn_w2"], v["L0_ffn_sw2"][None]], 0)
    b1 = np.concatenate([v["L0_ffn_b1"], v["L0_ffn_sb1"][None]], 0)
    b3 = np.concatenate([v["L0_ffn_b3"], v["L0_ffn_sb3"][None]], 0)
    for name, b in (("b1", b1), ("b3", b3)):
        lay(1, name + "g", b[:, 0::2].T)
        lay(1, name + "l", b[:, 1::2].T)
    for e in range(E0 + 1):
        for name, a in (("w1", w1), ("w3", w3)):
            lay_up(0, f"{name}g{e}", a[e, 0::2].T)
            lay_up(0, f"{name}l{e}", a[e, 1::2].T)
        lay(1, f"w2{e}", w2[e].T)
    lay(2, "wqkv", v["L0_attn_b_w_qkv"])
    lay(2, "wout", v["L0_attn_b_w_out"].reshape(8, P, P).transpose(1, 0, 2).reshape(P, 8 * P))
    flip = (idx // DA) * DA + (idx % DA + DA // 2) % DA
    for name, key in (("wq", "W_Q"), ("wk", "W_K"), ("wv", "W_V"), ("wo", "W_O")):
        lay(3, name, v[f"L1_attn_a_{key}"].T)
    lay(3, "wqf", v["L1_attn_a_W_Q"][flip].T)
    lay(3, "wkf", v["L1_attn_a_W_K"][flip].T)
    gu, dn = v["L1_ffn_w_gate_up"], v["L1_ffn_w_down"]
    lay(4, "gate", v["L1_ffn_gate_w"].T)
    lay(4, "sg", v["L1_ffn_shared_w_gate_up"][:, :64])
    lay(4, "su", v["L1_ffn_shared_w_gate_up"][:, 64:])
    lay(4, "sd", v["L1_ffn_shared_w_down"])
    for p in range(E1 // 2):
        lay_up(1, f"g{p}", np.concatenate([gu[2 * p][:, :64], gu[2 * p + 1][:, :64]], 1))
        lay_up(1, f"u{p}", np.concatenate([gu[2 * p][:, 64:], gu[2 * p + 1][:, 64:]], 1))
        lay(4, f"d{p}", np.concatenate([dn[2 * p], dn[2 * p + 1]], 0))
    m = {key[len("L1_attn_b_"):]: a for key, a in v.items() if key.startswith("L1_attn_b_")}
    lay(5, "left", m["W_up"][:, :P])
    lay(5, "right", m["W_up"][:, P:])
    lay(5, "delta", m["W_delta"])
    lay(5, "wb", np.concatenate([m["W_B"], m["W_B"]], 1))
    lay(5, "wc", np.concatenate([m["W_C"], m["W_C"]], 1))
    lay(5, "down", m["W_down"])
    lay(5, "b_left", m["b_up"][:P, None])
    lay(5, "b_right", m["b_up"][P:, None])
    lay(5, "conv_w", m["conv_w"])
    lay(5, "conv_b", m["conv_b"][:, None])
    lay(5, "b_delta", m["b_delta"][:, None])
    lay(5, "b_b", np.concatenate([m["b_B"], m["b_B"]], 0)[:, None])
    lay(5, "b_c", np.concatenate([m["b_C"], m["b_C"]], 0)[:, None])
    lay(5, "skip", m["D_skip"][:, None])
    lay(5, "b_down", m["b_down"][:, None])
    lay(5, "a_log", m["A_log"].reshape(4, 2, 16, 64).transpose(1, 3, 0, 2).reshape(P, 64))

    x = v["L0_attn_a_x"]
    passes = x.shape[0] // NB
    arrays = {"x": x.reshape(passes, T, P), "const": const, "half": half}
    arrays.update({f"weights_{g}": a for g, a in enumerate(packs)})
    arrays.update({f"up_{n}": a for n, a in enumerate(ups)})
    nc = bacc.Bacc("TRN2", target_bir_lowering=False, num_devices=1)
    ap = {name: nc.dram_tensor(f"in_{name}", a.shape, mybir.dt.from_np(a.dtype), kind="ExternalInput").ap()
          for name, a in arrays.items()}
    out = nc.dram_tensor("out", (passes, T, P), F32, kind="ExternalOutput").ap()
    hybrid_kernel(nc, ap["x"], ap["const"], ap["half"], [ap[f"weights_{g}"] for g in range(6)],
                  [ap[f"up_{n}"] for n in range(2)], out)
    got = run_bass_kernel_spmd(nc, [{f"in_{name}": a for name, a in arrays.items()}], core_ids=[0])
    return got.results[0]["out"].reshape(x.shape)
```
